# Optimizing a Trainium2 kernel written in Bass

```python
import numpy as np
import jax
import jax.numpy as jnp

def _softmax(x, axis=-1):
    return jax.nn.softmax(x, axis=axis)
def _gelu(x):
    return jax.nn.gelu(x, approximate=True)
def _silu(x):
    return jax.nn.silu(x)
def _sigmoid(x):
    return jax.nn.sigmoid(x)
def _layernorm(x, axis=-1, eps=1e-5):
    m = jnp.mean(x, axis=axis, keepdims=True)
    v = jnp.var(x, axis=axis, keepdims=True)
    return (x - m) / jnp.sqrt(v + eps)
def _scatter_add(tgt, idx, src, axis=0):
    return tgt.at[idx].add(src)
def _segment_sum(src, seg, n):
    return jax.ops.segment_sum(src, seg, n)

kernel_name = 'mk_metaformer_d2_conv_nhwc128_8344a6'

def setup_inputs(seed: int = 0):
    np.random.seed(seed)
    _w = jnp.asarray
    def _rec_inputs():
        import jax
        import jax.numpy as jnp
        _gk = jax.random.key(seed)
        x = 7.22e-05 + 1 * jax.random.normal(jax.random.fold_in(_gk, 1), (1, 256, 256, 128), jnp.float32)
        return x
    x = _rec_inputs()
    def _L0_conv_setup():
        import jax, jax.numpy as jnp
        import numpy as np
        PAIR_DIM = 128
        N_HEADS = 4
        HIDDEN = 32
        L = 256
        B = 1
        EPS = 1e-05
        key = jax.random.key(seed)
        ks = jax.random.split(key, 10)
        s = 0.02
        return {'pair': jax.random.normal(ks[0], (B, L, L, PAIR_DIM), dtype=jnp.float32), 'ln_g': jnp.ones((PAIR_DIM,), jnp.float32), 'ln_b': jnp.zeros((PAIR_DIM,), jnp.float32), 'Wq': jax.random.normal(ks[1], (PAIR_DIM, N_HEADS * HIDDEN), jnp.float32) * s, 'Wk': jax.random.normal(ks[2], (PAIR_DIM, N_HEADS * HIDDEN), jnp.float32) * s, 'Wv': jax.random.normal(ks[3], (PAIR_DIM, N_HEADS * HIDDEN), jnp.float32) * s, 'Wb': jax.random.normal(ks[4], (PAIR_DIM, N_HEADS), jnp.float32) * s, 'Wg': jax.random.normal(ks[5], (PAIR_DIM, N_HEADS * HIDDEN), jnp.float32) * s, 'bg': jnp.zeros((N_HEADS * HIDDEN,), jnp.float32), 'Wo': jax.random.normal(ks[6], (N_HEADS * HIDDEN, PAIR_DIM), jnp.float32) * s, 'bo': jnp.zeros((PAIR_DIM,), jnp.float32)}
    _L0_conv_all = _L0_conv_setup()
    _L0_conv_in = {k: v for k, v in _L0_conv_all.items() if k in ('ln_g', 'ln_b', 'Wq', 'Wk', 'Wv', 'Wb', 'Wg', 'bg', 'Wo', 'bo', )}
    del _L0_conv_all

    def _L0_ffn_setup():
        import jax, jax.numpy as jnp
        import numpy as np
        BN_EPS = 1e-05
        key = jax.random.key(seed)
        k1, k2, k3 = jax.random.split(key, 3)
        B, T, I, H = (64, 2048, 128, 128)
        x = jax.random.normal(k1, (B, T, I), dtype=jnp.float32)
        W = jax.random.normal(k2, (H, I), dtype=jnp.float32) * (1.0 / np.sqrt(I))
        V = jnp.linalg.qr(jax.random.normal(k3, (H, H), dtype=jnp.float32))[0]
        gamma = jnp.ones((H,), dtype=jnp.float32)
        beta = jnp.zeros((H,), dtype=jnp.float32)
        return {'x': x, 'W': W, 'V': V, 'gamma': gamma, 'beta': beta}
    _L0_ffn_all = _L0_ffn_setup()
    _L0_ffn_in = {k: v for k, v in _L0_ffn_all.items() if k in ('W', 'V', 'gamma', 'beta', )}
    del _L0_ffn_all

    def _L1_conv_setup():
        import jax, jax.numpy as jnp
        import numpy as np
        D_STATE = 8
        DT_RANK = 8

        def _grouped_1x1(x, w):
            B, H, W, _ = x.shape
            g, o, i = w.shape
            xg = x.reshape(B, H, W, g, i)
            return jnp.einsum('bhwgi,goi->bhwgo', xg, w).reshape(B, H, W, g * o)

        def _mamba(x_seq, in_proj_w, conv1d_w, conv1d_b, x_proj_w, dt_proj_w, dt_proj_b, A_log, D_param, out_proj_w):
            B, L, D = x_seq.shape
            N, R = (D_STATE, DT_RANK)
            xz = jnp.einsum('bld,ed->ble', x_seq, in_proj_w)
            u, z = (xz[..., :D], xz[..., D:])
            up = jnp.pad(u, ((0, 0), (2, 0), (0, 0)))
            u = up[:, 0:L] * conv1d_w[:, 0] + up[:, 1:L + 1] * conv1d_w[:, 1] + up[:, 2:L + 2] * conv1d_w[:, 2] + conv1d_b
            u = jax.nn.silu(u)
            x_dbl = jnp.einsum('bld,ed->ble', u, x_proj_w)
            dt = x_dbl[..., :R]
            Bm = x_dbl[..., R:R + N]
            Cm = x_dbl[..., R + N:]
            delta = jax.nn.softplus(jnp.einsum('blr,dr->bld', dt, dt_proj_w) + dt_proj_b)
            A = -jnp.exp(A_log)

            def step(h, inp):
                d_t, u_t, b_t, c_t = inp
                dA = jnp.exp(d_t[..., None] * A)
                h = dA * h + (d_t * u_t)[..., None] * b_t[:, None, :]
                y_t = jnp.einsum('bdn,bn->bd', h, c_t)
                return (h, y_t)
            h0 = jnp.zeros((B, D, N), dtype=x_seq.dtype)
            xs = (jnp.swapaxes(delta, 0, 1), jnp.swapaxes(u, 0, 1), jnp.swapaxes(Bm, 0, 1), jnp.swapaxes(Cm, 0, 1))
            _, ys = jax.lax.scan(step, h0, xs)
            y = jnp.swapaxes(ys, 0, 1) + u * D_param
            y = y * jax.nn.silu(z)
            return jnp.einsum('bld,ed->ble', y, out_proj_w)
        key = jax.random.key(seed)
        ks = jax.random.split(key, 16)
        B, H, W, C = (8, 64, 64, 128)
        g = 4
        D = 128
        N = D_STATE
        R = DT_RANK
        inp = {}
        inp['x'] = jax.random.normal(ks[0], (B, H, W, C), dtype=jnp.float32)
        inp['w1'] = jax.random.normal(ks[1], (g, D // g, C // g), dtype=jnp.float32) * 0.1
        inp['dw'] = jax.random.normal(ks[2], (3, 3, 1, D), dtype=jnp.float32) * 0.1
        inp['in_proj_w'] = jax.random.normal(ks[3], (2 * D, D), dtype=jnp.float32) * 0.05
        inp['conv1d_w'] = jax.random.normal(ks[4], (D, 3), dtype=jnp.float32) * 0.1
        inp['conv1d_b'] = jax.random.normal(ks[5], (D,), dtype=jnp.float32) * 0.05
        inp['x_proj_w'] = jax.random.normal(ks[6], (R + 2 * N, D), dtype=jnp.float32) * 0.05
        inp['dt_proj_w'] = jax.random.normal(ks[7], (D, R), dtype=jnp.float32) * 0.05
        inp['dt_proj_b'] = jax.random.normal(ks[8], (D,), dtype=jnp.float32) * 0.05
        inp['A_log'] = jnp.log(jnp.tile(jnp.arange(1, N + 1, dtype=jnp.float32)[None, :], (D, 1)))
        inp['D_param'] = jnp.ones((D,), dtype=jnp.float32)
        inp['out_proj_w'] = jax.random.normal(ks[9], (D, D), dtype=jnp.float32) * 0.05
        inp['gamma'] = jnp.ones((D,), dtype=jnp.float32)
        inp['beta'] = jnp.zeros((D,), dtype=jnp.float32)
        inp['w2'] = jax.random.normal(ks[10], (g, D // g, C // g), dtype=jnp.float32) * 0.1
        inp['wout'] = jax.random.normal(ks[11], (g, C // g, D // g), dtype=jnp.float32) * 0.1
        return inp
    _L1_conv_all = _L1_conv_setup()
    _L1_conv_in = {k: v for k, v in _L1_conv_all.items() if k in ('w1', 'dw', 'in_proj_w', 'conv1d_w', 'conv1d_b', 'x_proj_w', 'dt_proj_w', 'dt_proj_b', 'A_log', 'D_param', 'out_proj_w', 'gamma', 'beta', 'w2', 'wout', )}
    del _L1_conv_all

    def _L1_ffn_setup():
        import jax, jax.numpy as jnp
        import numpy as np
        B, N, D, C, E, K = (8, 8192, 128, 128, 8, 2)
        key = jax.random.key(seed)
        k0, k1, k2 = jax.random.split(key, 3)
        x = jax.random.normal(k0, (B, N, D), dtype=jnp.float32)
        router_w = jax.random.normal(k1, (D, E), dtype=jnp.float32) * 0.05
        router_b = jnp.zeros((E,), dtype=jnp.float32)
        expert_w = jax.random.normal(k2, (E, D, C), dtype=jnp.float32) * (1.0 / np.sqrt(D))
        expert_b = jnp.zeros((E, C), dtype=jnp.float32)
        return {'x': x, 'router_w': router_w, 'router_b': router_b, 'expert_w': expert_w, 'expert_b': expert_b}
    _L1_ffn_all = _L1_ffn_setup()
    _L1_ffn_in = {k: v for k, v in _L1_ffn_all.items() if k in ('router_w', 'router_b', 'expert_w', 'expert_b', )}
    del _L1_ffn_all

    return {
        "x": x,
        "L0_conv_ln_g": _L0_conv_in["ln_g"],
        "L0_conv_ln_b": _L0_conv_in["ln_b"],
        "L0_conv_Wq": _L0_conv_in["Wq"],
        "L0_conv_Wk": _L0_conv_in["Wk"],
        "L0_conv_Wv": _L0_conv_in["Wv"],
        "L0_conv_Wb": _L0_conv_in["Wb"],
        "L0_conv_Wg": _L0_conv_in["Wg"],
        "L0_conv_bg": _L0_conv_in["bg"],
        "L0_conv_Wo": _L0_conv_in["Wo"],
        "L0_conv_bo": _L0_conv_in["bo"],
        "L0_ffn_W": _L0_ffn_in["W"],
        "L0_ffn_V": _L0_ffn_in["V"],
        "L0_ffn_gamma": _L0_ffn_in["gamma"],
        "L0_ffn_beta": _L0_ffn_in["beta"],
        "L1_conv_w1": _L1_conv_in["w1"],
        "L1_conv_dw": _L1_conv_in["dw"],
        "L1_conv_in_proj_w": _L1_conv_in["in_proj_w"],
        "L1_conv_conv1d_w": _L1_conv_in["conv1d_w"],
        "L1_conv_conv1d_b": _L1_conv_in["conv1d_b"],
        "L1_conv_x_proj_w": _L1_conv_in["x_proj_w"],
        "L1_conv_dt_proj_w": _L1_conv_in["dt_proj_w"],
        "L1_conv_dt_proj_b": _L1_conv_in["dt_proj_b"],
        "L1_conv_A_log": _L1_conv_in["A_log"],
        "L1_conv_D_param": _L1_conv_in["D_param"],
        "L1_conv_out_proj_w": _L1_conv_in["out_proj_w"],
        "L1_conv_gamma": _L1_conv_in["gamma"],
        "L1_conv_beta": _L1_conv_in["beta"],
        "L1_conv_w2": _L1_conv_in["w2"],
        "L1_conv_wout": _L1_conv_in["wout"],
        "L1_ffn_router_w": _L1_ffn_in["router_w"],
        "L1_ffn_router_b": _L1_ffn_in["router_b"],
        "L1_ffn_expert_w": _L1_ffn_in["expert_w"],
        "L1_ffn_expert_b": _L1_ffn_in["expert_b"],
    }

def reference(x, L0_conv_ln_g, L0_conv_ln_b, L0_conv_Wq, L0_conv_Wk, L0_conv_Wv, L0_conv_Wb, L0_conv_Wg, L0_conv_bg, L0_conv_Wo, L0_conv_bo, L0_ffn_W, L0_ffn_V, L0_ffn_gamma, L0_ffn_beta, L1_conv_w1, L1_conv_dw, L1_conv_in_proj_w, L1_conv_conv1d_w, L1_conv_conv1d_b, L1_conv_x_proj_w, L1_conv_dt_proj_w, L1_conv_dt_proj_b, L1_conv_A_log, L1_conv_D_param, L1_conv_out_proj_w, L1_conv_gamma, L1_conv_beta, L1_conv_w2, L1_conv_wout, L1_ffn_router_w, L1_ffn_router_b, L1_ffn_expert_w, L1_ffn_expert_b):
    import jax
    import jax.numpy as jnp
    def _L0_conv_ref(pair, ln_g, ln_b, Wq, Wk, Wv, Wb, Wg, bg, Wo, bo):
        import jax, jax.numpy as jnp
        import numpy as np
        PAIR_DIM = 128
        N_HEADS = 4
        HIDDEN = 32
        L = 256
        B = 1
        EPS = 1e-05
        b, l, _, d = pair.shape
        factor = 1.0 / jnp.sqrt(jnp.asarray(HIDDEN, pair.dtype))
        mu = jnp.mean(pair, axis=-1, keepdims=True)
        var = jnp.mean(jnp.square(pair - mu), axis=-1, keepdims=True)
        x = (pair - mu) * jax.lax.rsqrt(var + EPS) * ln_g + ln_b
        Q = (x @ Wq).reshape(b, l, l, N_HEADS, HIDDEN)
        K = (x @ Wk).reshape(b, l, l, N_HEADS, HIDDEN)
        V = (x @ Wv).reshape(b, l, l, N_HEADS, HIDDEN)
        bias = jnp.transpose(x @ Wb, (0, 3, 2, 1))[:, :, None, :, :]
        attn = jnp.einsum('bijnh,biknh->bnijk', Q, K) * factor + bias
        attn = jax.nn.softmax(attn, axis=-1)
        gate = jax.nn.sigmoid(x @ Wg + bg).reshape(b, l, l, N_HEADS, HIDDEN)
        out = jnp.einsum('bnijk,biknh->bijnh', attn, V) * gate
        out = out.reshape(b, l, l, N_HEADS * HIDDEN) @ Wo + bo
        return out

    def _L0_ffn_ref(x, W, V, gamma, beta):
        import jax, jax.numpy as jnp
        import numpy as np
        BN_EPS = 1e-05
        B, T, H = (x.shape[0], x.shape[1], W.shape[0])
        Wx = jnp.einsum('bti,hi->bth', x, W)
        flat = Wx.reshape(B * T, H)
        mean = jnp.mean(flat, axis=0)
        var = jnp.var(flat, axis=0)
        Wx = ((flat - mean) * jax.lax.rsqrt(var + BN_EPS) * gamma + beta).reshape(B, T, H)
        Vt = V.T

        def step(yt, wx_t):
            yt = jax.nn.sigmoid(wx_t + yt @ Vt)
            return (yt, yt)
        y0 = jnp.zeros((B, H), dtype=Wx.dtype)
        _, ys = jax.lax.scan(step, y0, jnp.swapaxes(Wx, 0, 1))
        return jnp.swapaxes(ys, 0, 1)

    def _L1_conv_ref(x, w1, dw, in_proj_w, conv1d_w, conv1d_b, x_proj_w, dt_proj_w, dt_proj_b, A_log, D_param, out_proj_w, gamma, beta, w2, wout):
        import jax, jax.numpy as jnp
        import numpy as np
        D_STATE = 8
        DT_RANK = 8

        def _grouped_1x1(x, w):
            B, H, W, _ = x.shape
            g, o, i = w.shape
            xg = x.reshape(B, H, W, g, i)
            return jnp.einsum('bhwgi,goi->bhwgo', xg, w).reshape(B, H, W, g * o)

        def _mamba(x_seq, in_proj_w, conv1d_w, conv1d_b, x_proj_w, dt_proj_w, dt_proj_b, A_log, D_param, out_proj_w):
            B, L, D = x_seq.shape
            N, R = (D_STATE, DT_RANK)
            xz = jnp.einsum('bld,ed->ble', x_seq, in_proj_w)
            u, z = (xz[..., :D], xz[..., D:])
            up = jnp.pad(u, ((0, 0), (2, 0), (0, 0)))
            u = up[:, 0:L] * conv1d_w[:, 0] + up[:, 1:L + 1] * conv1d_w[:, 1] + up[:, 2:L + 2] * conv1d_w[:, 2] + conv1d_b
            u = jax.nn.silu(u)
            x_dbl = jnp.einsum('bld,ed->ble', u, x_proj_w)
            dt = x_dbl[..., :R]
            Bm = x_dbl[..., R:R + N]
            Cm = x_dbl[..., R + N:]
            delta = jax.nn.softplus(jnp.einsum('blr,dr->bld', dt, dt_proj_w) + dt_proj_b)
            A = -jnp.exp(A_log)

            def step(h, inp):
                d_t, u_t, b_t, c_t = inp
                dA = jnp.exp(d_t[..., None] * A)
                h = dA * h + (d_t * u_t)[..., None] * b_t[:, None, :]
                y_t = jnp.einsum('bdn,bn->bd', h, c_t)
                return (h, y_t)
            h0 = jnp.zeros((B, D, N), dtype=x_seq.dtype)
            xs = (jnp.swapaxes(delta, 0, 1), jnp.swapaxes(u, 0, 1), jnp.swapaxes(Bm, 0, 1), jnp.swapaxes(Cm, 0, 1))
            _, ys = jax.lax.scan(step, h0, xs)
            y = jnp.swapaxes(ys, 0, 1) + u * D_param
            y = y * jax.nn.silu(z)
            return jnp.einsum('bld,ed->ble', y, out_proj_w)
        B, H, W, C = x.shape
        D = dw.shape[-1]
        x1 = _grouped_1x1(x, w1)
        x1 = jax.lax.conv_general_dilated(x1, dw, window_strides=(1, 1), padding='SAME', feature_group_count=D, dimension_numbers=('NHWC', 'HWIO', 'NHWC'))
        x1 = jax.nn.silu(x1)
        x1_seq = x1.reshape(B, H * W, D)
        x1_seq = _mamba(x1_seq, in_proj_w, conv1d_w, conv1d_b, x_proj_w, dt_proj_w, dt_proj_b, A_log, D_param, out_proj_w)
        x1 = x1_seq.reshape(B, H, W, D)
        mu = jnp.mean(x1, axis=-1, keepdims=True)
        var = jnp.mean(jnp.square(x1 - mu), axis=-1, keepdims=True)
        x1 = (x1 - mu) * jax.lax.rsqrt(var + 1e-05) * gamma + beta
        x2 = jax.nn.silu(_grouped_1x1(x, w2))
        x_fuse = x1 * x2
        return _grouped_1x1(x_fuse, wout)

    def _L1_ffn_ref(x, router_w, router_b, expert_w, expert_b):
        import jax, jax.numpy as jnp
        import numpy as np
        B, N, D, C, E, K = (8, 8192, 128, 128, 8, 2)
        router_probs = jax.nn.softmax(x @ router_w + router_b, axis=-1)
        top_p, top_i = jax.lax.top_k(router_probs, K)
        top_p = top_p / jnp.sum(top_p, axis=-1, keepdims=True)
        expert_out = jnp.einsum('bnd,edc->bnec', x, expert_w) + expert_b
        gathered = jnp.take_along_axis(expert_out, top_i[..., None], axis=2)
        return jnp.einsum('bnk,bnkc->bnc', top_p, gathered)

    def _gn(v, G=32, eps=1e-5):
        B_, H_, W_, C_ = v.shape
        g = v.reshape(B_, H_, W_, G, C_ // G)
        m = jnp.mean(g, axis=(1, 2, 4), keepdims=True)
        s = jnp.var(g, axis=(1, 2, 4), keepdims=True)
        return ((g - m) / jnp.sqrt(s + eps)).reshape(v.shape)

    def _ln_c(v, eps=1e-6):
        m = jnp.mean(v, axis=-1, keepdims=True)
        s = jnp.var(v, axis=-1, keepdims=True)
        return (v - m) / jnp.sqrt(s + eps)

    def _ln_t(v, eps=1e-5):
        m = jnp.mean(v, axis=-1, keepdims=True)
        s = jnp.var(v, axis=-1, keepdims=True)
        return (v - m) / jnp.sqrt(s + eps)

    def _to_tokens(v):
        B_, H_, W_, C_ = v.shape
        return v.reshape(B_, H_ * W_, C_)
    def _from_tokens(t, like):
        return t.reshape(like.shape)

    x = x + _L0_conv_ref(_ln_c(x), L0_conv_ln_g, L0_conv_ln_b, L0_conv_Wq, L0_conv_Wk, L0_conv_Wv, L0_conv_Wb, L0_conv_Wg, L0_conv_bg, L0_conv_Wo, L0_conv_bo)
    t = _to_tokens(x)
    t = t + _L0_ffn_ref(_ln_t(t), L0_ffn_W, L0_ffn_V, L0_ffn_gamma, L0_ffn_beta)
    x = _from_tokens(t, x)
    x = x + _L1_conv_ref(_ln_c(x), L1_conv_w1, L1_conv_dw, L1_conv_in_proj_w, L1_conv_conv1d_w, L1_conv_conv1d_b, L1_conv_x_proj_w, L1_conv_dt_proj_w, L1_conv_dt_proj_b, L1_conv_A_log, L1_conv_D_param, L1_conv_out_proj_w, L1_conv_gamma, L1_conv_beta, L1_conv_w2, L1_conv_wout)
    t = _to_tokens(x)
    t = t + _L1_ffn_ref(_ln_t(t), L1_ffn_router_w, L1_ffn_router_b, L1_ffn_expert_w, L1_ffn_expert_b)
    x = _from_tokens(t, x)
    return x


_drawn_inputs = setup_inputs


def setup_inputs(seed=0):
    import zlib

    import numpy as np

    out = dict(_drawn_inputs(seed))
    spreads = {'L0_conv_ln_g': (1.0, 0.6),
     'L0_conv_ln_b': (0.0, 0.403),
     'L0_conv_bg': (0.0, 0.8),
     'L0_conv_bo': (0.0, 0.1),
     'L0_ffn_gamma': (1.0, 0.2),
     'L0_ffn_beta': (0.0, 0.1),
     'L1_conv_D_param': (1.0, 0.6),
     'L1_conv_gamma': (1.0, 0.2),
     'L1_conv_beta': (0.0, 0.1),
     'L1_ffn_router_b': (0.0, 0.1),
     'L1_ffn_expert_b': (0.0, 0.1)}
    factors = {'L0_conv_Wq': 8.0,
     'L0_conv_Wk': 8.0,
     'L0_conv_Wv': 2.803,
     'L0_conv_Wb': 7.843,
     'L0_conv_Wg': 8.0,
     'L0_conv_Wo': 2.977,
     'L1_conv_x_proj_w': 64.0,
     'L1_conv_dt_proj_w': 64.0,
     'L1_conv_dt_proj_b': 64.0,
     'L1_conv_A_log': 64.0}
    for name, (base, spread) in spreads.items():
        noise = np.random.default_rng([zlib.crc32(name.encode()), seed]).standard_normal(out[name].shape)
        drawn = base * np.exp(spread * noise) if base else spread * noise
        out[name] = jnp.asarray(drawn.astype(out[name].dtype))
    for name, factor in factors.items():
        out[name] = (out[name] * factor).astype(out[name].dtype)
    return out
```

```python
from contextlib import ExitStack

import concourse.bass as bass
from concourse import mybir

F32 = mybir.dt.float32
BF16 = mybir.dt.bfloat16
I32 = mybir.dt.int32
U32 = mybir.dt.uint32
ALU = mybir.AluOpType
ACT = mybir.ActivationFunctionType
AX = mybir.AxisListType

P = 128
C = 128
SIDE = 256
TOKENS = SIDE * SIDE
BANK = 512
HEADS = 4
HID = C // HEADS
AHEAD = 2
RB = SIDE // P


class Space:

    def __init__(self, nc, ctx, name):
        self.nc, self.ctx, self.name = nc, ctx, name
        self.sems = []

    def sb(self, name, shape, dt=F32):
        return self.ctx.enter_context(self.nc.sbuf_tensor(f"{self.name}_{name}", shape, dt))

    def bank(self, name, n=1):
        return self.ctx.enter_context(self.nc.psum_tensor(f"{self.name}_{name}_bank", [P, n * BANK], F32))

    def sem(self, name):
        self.sems.append(self.nc.alloc_semaphore(name=f"{self.name}_{name}"))
        return self.sems[-1]

    def clear(self):
        self.nc.clear_and_free_semaphores(self.sems)
        self.nc.all_engine_barrier()


def column(v):
    return v.rearrange("(p a) -> p a", a=1)


def hold(eng, sem, value, passed):
    eng.wait_ge(sem, value)
    eng.sem_inc(passed, 1)


def make_identity(pool, ident, zeroed, done):
    pool.memset(ident[:, :], 0.0).then_inc(zeroed, 1)
    pool.wait_ge(zeroed, 1)
    pool.affine_select(out=ident[:, :], in_=ident[:, :], compare_op=ALU.not_equal, fill=1.0,
                       base=0, pattern=[[-1, P]], channel_multiplier=1).then_inc(done, 1)


def phase_bias(nc, io, keep):
    ROWS = 4
    NB = ROWS * RB
    TILES = SIDE // ROWS
    x_v = io["x"].rearrange("a (t r) (b p) c -> (a t) p (r b) c", r=ROWS, p=P)
    with ExitStack() as ctx:
        s = Space(nc, ctx, "bias")
        x = [s.sb(f"x{u}", [P, NB, C]) for u in range(2)]
        h = [s.sb(f"h{u}", [P, NB, C]) for u in range(2)]
        stats = [s.sb(f"stats{u}", [P, NB, 6]) for u in range(2)]
        mv = [s.sb(f"mv{u}", [P, NB, 2]) for u in range(2)]
        vv = [s.sb(f"vv{u}", [P, NB]) for u in range(2)]
        scale = [s.sb(f"scale{u}", [P, NB]) for u in range(2)]
        shift = [s.sb(f"shift{u}", [P, NB]) for u in range(2)]
        xT = [s.sb(f"xT{u}", [P, NB * P]) for u in range(2)]
        half = s.sb("half", [P, NB])
        wb = s.sb("wb", [P, HEADS])
        g, b = s.sb("g", [P, 1]), s.sb("b", [P, 1])
        t_ps = [s.bank(f"t{u}", 2) for u in range(2)]
        b_ps = [s.bank(f"b{u}") for u in range(2)]

        params = s.sem("params")
        zeroed, ident_ready = s.sem("zeroed"), s.sem("ident_ready")
        x_loaded = [s.sem(f"x_loaded{u}") for u in range(2)]
        stats_step, vv_ready, shift_ready = s.sem("stats_step"), s.sem("vv_ready"), s.sem("shift_ready")
        scale_ready, h_ready, passed = s.sem("scale_ready"), s.sem("h_ready"), s.sem("passed")
        kept = s.sem("kept")
        t_ready, xT_ready = s.sem("t_ready"), s.sem("xT_ready")
        b_ready, b_kept = s.sem("b_ready"), s.sem("b_kept")

        with nc.Block() as block:
            @block.sync
            def _(sp):
                sp.dma_start(wb[:, :], io["L0_conv_Wb"]).then_inc(params, 16)
                sp.dma_start(g[:, :], column(io["L0_conv_ln_g"])).then_inc(params, 16)
                sp.dma_start(b[:, :], column(io["L0_conv_ln_b"])).then_inc(params, 16)
                with sp.Fori(0, TILES // 2) as i:
                    for u in range(2):
                        sp.wait_ge(h_ready, 2 * i + u + 1)
                        sp.dma_start(x[u][:, :, :], x_v[2 * i + u]).then_inc(x_loaded[u], 16)

            @block.vector
            def _(dve):
                dve.sem_inc(h_ready, AHEAD)
                with dve.Fori(0, TILES // 2) as i:
                    for u in range(2):
                        t = 2 * i + u
                        dve.wait_ge(x_loaded[u], 16 * i + 16)
                        for k in range(NB):
                            last = nc.vector.bn_stats(stats[u][:, k, :], x[u][:, k, :])
                        last.then_inc(stats_step, 1)
                        hold(dve, stats_step, t * 2 + 1, passed)
                        for k in range(NB):
                            last = nc.vector.bn_aggr(mv[u][:, k, :], stats[u][:, k, :])
                        last.then_inc(stats_step, 1)
                        dve.wait_ge(stats_step, t * 2 + 2)
                        nc.vector.tensor_scalar(vv[u][:, :], mv[u][:, :, 1], 1.0 + 1e-5, 1e-11,
                                                ALU.mult, ALU.add).then_inc(vv_ready, 1)
                    for u in range(2):
                        t = 2 * i + u
                        dve.wait_ge(scale_ready, t + 1)
                        nc.vector.scalar_tensor_tensor(shift[u][:, :], mv[u][:, :, 0], -1.0,
                                                       scale[u][:, :], ALU.mult,
                                                       ALU.mult).then_inc(shift_ready, 1)
                        dve.wait_ge(shift_ready, t + 1)
                        hold(dve, t_ready, t + 1, passed)
                        for k in range(NB):
                            last = nc.vector.tensor_scalar(h[u][:, k, :], x[u][:, k, :],
                                                           scale[u][:, k:k + 1], shift[u][:, k:k + 1],
                                                           ALU.mult, ALU.add)
                        last.then_inc(h_ready, 1)

            @block.gpsimd
            def _(pool):
                make_identity(pool, keep["ident"], zeroed, ident_ready)
                pool.memset(half[:, :], -0.5).then_inc(zeroed, 1)
                pool.sem_inc(kept, AHEAD)
                pool.wait_ge(zeroed, 2)
                with pool.Fori(0, TILES // 2) as i:
                    for u in range(2):
                        t = 2 * i + u
                        hold(pool, kept, t + 1, passed)
                        pool.wait_ge(vv_ready, t + 1)
                        nc.gpsimd.tensor_tensor(scale[u][:, :], vv[u][:, :], half[:, :],
                                                ALU.pow).then_inc(scale_ready, 1)
                    for u in range(2):
                        t = 2 * i + u
                        hold(pool, shift_ready, t + 1, passed)
                        nc.gpsimd.tensor_copy(keep["scale"][:, bass.ds(t * NB, NB)], scale[u][:, :])
                        nc.gpsimd.tensor_copy(keep["shift"][:, bass.ds(t * NB, NB)],
                                              shift[u][:, :]).then_inc(kept, 1)

            @block.tensor
            def _(pe):
                pe.sem_inc(t_ready, AHEAD)
                pe.wait_ge(ident_ready, 1)
                pe.wait_ge(params, 48)
                with pe.Fori(0, TILES // 2) as i:
                    for u in range(2):
                        t = 2 * i + u
                        pe.wait_ge(h_ready, t + 1 + AHEAD)
                        for k in range(NB):
                            last = nc.tensor.transpose(t_ps[u][:, k * P:(k + 1) * P], h[u][:, k, :],
                                                       keep["ident"][:, :])
                        last.then_inc(t_ready, 1)
                        pe.wait_ge(xT_ready, 2 * t + 2)
                        pe.wait_ge(b_kept, t + 1)
                        for k in range(NB):
                            last = nc.tensor.matmul(b_ps[u][:, k * HEADS:(k + 1) * HEADS],
                                                    xT[u][:, k * P:(k + 1) * P], wb[:, :],
                                                    start=True, stop=True)
                        last.then_inc(b_ready, 1)

            @block.scalar
            def _(act):
                act.preload_act_table_set("exp_and_others")
                act.sem_inc(b_kept, AHEAD)
                act.wait_ge(params, 48)
                with act.Fori(0, TILES // 2) as i:
                    for u in range(2):
                        t = 2 * i + u
                        act.wait_ge(t_ready, t + 1 + AHEAD)
                        for k in range(2):
                            nc.scalar.activation(xT[u][:, k * BANK:(k + 1) * BANK],
                                                 t_ps[u][:, k * BANK:(k + 1) * BANK], ACT.Identity,
                                                 bias=b[:, :], scale=g[:, :]).then_inc(xT_ready, 1)
                        act.wait_ge(b_ready, t + 1)
                        nc.scalar.activation(
                            keep["bias"][:, :, :, bass.ds(t * ROWS, ROWS)].rearrange("p n b r -> p r b n"),
                            b_ps[u][:, 0:NB * HEADS].rearrange("p (r b n) -> p r b n", r=ROWS, b=RB),
                            ACT.Copy).then_inc(b_kept, 1)
        s.clear()


def phase_attention(nc, io, keep):
    PAIRS = SIDE // 2
    UNITS = 2 * HEADS
    x_v = io["x"].rearrange("a r (b p) c -> (a r) p b c", p=P)
    x1_v = io["x1"].rearrange("(r b p) c -> r p b c", r=SIDE, p=P)
    with ExitStack() as ctx:
        s = Space(nc, ctx, "attn")

        def two(name, shape):
            return [s.sb(f"{name}{u}", shape) for u in range(2)]

        wq, wk, wv, wg, wo = (s.sb(n, [P, C]) for n in ("wq", "wk", "wv", "wg", "wo"))
        g, b, bg, hbg = (s.sb(n, [P, 1]) for n in ("g", "b", "bg", "hbg"))
        bo = s.sb("bo", [P, RB, C])
        x, h, xb, x1 = (two(n, [P, RB, C]) for n in ("x", "h", "xb", "x1"))
        ln = two("ln", [P, 2 * RB])
        xT, qT, kT, gate, oT = (two(n, [P, SIDE]) for n in ("xT", "qT", "kT", "gate", "oT"))
        v = two("v", [P, RB, HEADS, HID + 1])
        biased, less_max, probs = (two(n, [P, RB, SIDE]) for n in ("biased", "less_max", "probs"))
        top = two("top", [P, RB])
        half_inv = two("half_inv", [P, RB * HEADS])
        o = two("o", [P, RB, HEADS, HID])

        s_ps = [s.bank(f"s{k}") for k in range(2)]
        p_ps = [s.bank(f"p{k}") for k in range(2)]
        m_ps = [s.bank(f"m{k}") for k in range(4)]
        x_ps, qk_ps, vg_ps = [m_ps[0], m_ps[3]], [m_ps[1], m_ps[0]], [m_ps[2], m_ps[3]]
        o_ps, oT_ps, y_ps = [m_ps[1], m_ps[2]], [m_ps[0], m_ps[3]], [m_ps[1], m_ps[2]]

        def o_view(u):
            return o_ps[u][:, 0:RB * HEADS * (HID + 1)].rearrange("p (b n d) -> p b n d", b=RB, n=HEADS)

        params, hbg_ready, ones_ready = s.sem("params"), s.sem("hbg_ready"), s.sem("ones_ready")
        passed = s.sem("passed")
        x_loaded = [s.sem(f"x_loaded{u}") for u in range(2)]
        stored = [s.sem(f"stored{u}") for u in range(2)]
        ln_copied, h_ready, xb_ready = s.sem("ln_copied"), s.sem("h_ready"), s.sem("xb_ready")
        x_turned, xT_ready = s.sem("x_turned"), s.sem("xT_ready")
        qk_done, qk_ready, vg_done, vg_ready = (s.sem(n) for n in ("qk_done", "qk_ready", "vg_done", "vg_ready"))
        scored, maxed, lessened, turned = (s.sem(n) for n in ("scored", "maxed", "lessened", "turned"))
        exped, valued = s.sem("exped"), s.sem("valued")
        inv_ready, o_ready, o_turned, oT_ready = (s.sem(n) for n in ("inv_ready", "o_ready", "o_turned", "oT_ready"))
        y_done, x1_ready = s.sem("y_done"), s.sem("x1_ready")

        with nc.Block() as block:
            @block.sync
            def _(sp):
                for w, name in ((wq, "Wq"), (wk, "Wk"), (wv, "Wv"), (wg, "Wg"), (wo, "Wo")):
                    sp.dma_start(w[:, :], io[f"L0_conv_{name}"]).then_inc(params, 16)
                for w, name in ((g, "ln_g"), (b, "ln_b"), (bg, "bg")):
                    sp.dma_start(w[:, :], column(io[f"L0_conv_{name}"])).then_inc(params, 16)
                for k in range(RB):
                    sp.dma_start(bo[:, k, :], io["L0_conv_bo"].partition_broadcast(P)).then_inc(params, 16)

                def load(i):
                    for u in range(2):
                        sp.wait_ge(xb_ready, 2 * i + u + 1)
                        sp.dma_start(x[u][:, :, :], x_v[2 * i + u]).then_inc(x_loaded[u], 16)

                def store(i):
                    for u in range(2):
                        sp.wait_ge(x1_ready, 2 * i + u + 1 + AHEAD)
                        sp.dma_start(x1_v[2 * i + u], x1[u][:, :, :]).then_inc(stored[u], 16)

                load(0)
                with sp.Fori(0, PAIRS - 1) as i:
                    load(i + 1)
                    store(i)
                store(PAIRS - 1)
                for u in range(2):
                    sp.wait_ge(stored[u], 16 * PAIRS)

            @block.gpsimd
            def _(pool):
                pool.sem_inc(xb_ready, AHEAD)
                pool.sem_inc(lessened, AHEAD)
                for u in range(2):
                    pool.memset(v[u][:, :, :, HID:HID + 1], 2.0).then_inc(ones_ready, 1)
                pool.wait_ge(params, 160)

                def norm(i):
                    for u in range(2):
                        t = 2 * i + u
                        nc.gpsimd.tensor_copy(ln[u][:, 0:RB], keep["scale"][:, bass.ds(t * RB, RB)])
                        nc.gpsimd.tensor_copy(ln[u][:, RB:2 * RB],
                                              keep["shift"][:, bass.ds(t * RB, RB)]).then_inc(ln_copied, 1)
                        hold(pool, ln_copied, t + 1, passed)
                        hold(pool, x_loaded[u], 16 * i + 16, passed)
                        hold(pool, x_turned, t + 1, passed)
                        for k in range(RB):
                            last = nc.gpsimd.tensor_scalar(h[u][:, k, :], x[u][:, k, :], ln[u][:, k:k + 1],
                                                           ln[u][:, RB + k:RB + k + 1], ALU.mult, ALU.add)
                        last.then_inc(h_ready, 1)

                def add_bo(i):
                    for u in range(2):
                        t = 2 * i + u
                        pool.wait_ge(x1_ready, t + 1)
                        nc.gpsimd.tensor_tensor(xb[u][:, :, :], x[u][:, :, :], bo[:, :, :],
                                                ALU.add).then_inc(xb_ready, 1)

                def less(i, units):
                    for k in units:
                        q = UNITS * i + k
                        hold(pool, turned, q + 1, passed)
                        pool.wait_ge(maxed, q + 1 + AHEAD)
                        nc.gpsimd.tensor_tensor(
                            less_max[k % 2][:, :, :], biased[k % 2][:, :, :],
                            top[k % 2][:, :].unsqueeze(2).broadcast_to([P, RB, SIDE]),
                            ALU.subtract).then_inc(lessened, 1)

                norm(0)
                with pool.Fori(0, PAIRS - 1) as i:
                    add_bo(i)
                    less(i, range(0, HEADS))
                    norm(i + 1)
                    less(i, range(HEADS, UNITS))
                add_bo(PAIRS - 1)
                less(PAIRS - 1, range(UNITS))

            @block.tensor
            def _(pe):
                pe.sem_inc(x_turned, AHEAD)
                pe.sem_inc(turned, AHEAD)
                pe.sem_inc(valued, AHEAD)
                pe.wait_ge(params, 160)
                ident = keep["ident"][:, :]

                def turn_x(t, u):
                    pe.wait_ge(h_ready, t + 1)
                    for k in range(RB):
                        last = nc.tensor.transpose(x_ps[u][:, k * P:(k + 1) * P], h[u][:, k, :], ident)
                    last.then_inc(x_turned, 1)

                def project(t, u):
                    pe.wait_ge(xT_ready, t + 1)
                    if u == 0:
                        pe.wait_ge(x1_ready, t + 1)
                    nc.tensor.matmul(qk_ps[u][:, 0:SIDE], wq[:, :], xT[u][:, :], start=True, stop=True)
                    nc.tensor.matmul(qk_ps[u][:, SIDE:2 * SIDE], wk[:, :], xT[u][:, :],
                                     start=True, stop=True).then_inc(qk_done, 1)
                    if u == 0:
                        pe.wait_ge(x1_ready, t + 2)
                    for k in range(RB):
                        nc.tensor.matmul(vg_ps[u][:, k * C:(k + 1) * C], xT[u][:, k * P:(k + 1) * P],
                                         wv[:, :], start=True, stop=True)
                    nc.tensor.matmul(vg_ps[u][:, SIDE:2 * SIDE], wg[:, :], xT[u][:, :],
                                     start=True, stop=True).then_inc(vg_done, 1)

                def score(i, k):
                    u, n = divmod(k, HEADS)
                    rows = slice(n * HID, (n + 1) * HID)
                    if n == 0:
                        pe.wait_ge(qk_ready, 2 * i + u + 1)
                    pe.wait_ge(maxed, UNITS * i + k + 1)
                    for j in range(RB):
                        last = nc.tensor.matmul(s_ps[k % 2][:, j * SIDE:(j + 1) * SIDE],
                                                qT[u][rows, j * P:(j + 1) * P], kT[u][rows, :],
                                                start=True, stop=True)
                    last.then_inc(scored, 1)

                def turn(i, k):
                    pe.wait_ge(lessened, UNITS * i + k + 1 + AHEAD)
                    for j in range(RB):
                        for kb in range(RB):
                            last = nc.tensor.transpose(
                                p_ps[k % 2][:, kb * SIDE + j * P:kb * SIDE + (j + 1) * P],
                                less_max[k % 2][:, j, kb * P:(kb + 1) * P], ident)
                    last.then_inc(turned, 1)

                def value(i, k):
                    u, n = divmod(k, HEADS)
                    if n == 0:
                        pe.wait_ge(vg_ready, 2 * i + u + 1)
                    pe.wait_ge(exped, UNITS * i + k + 1)
                    for j in range(RB):
                        for kb in range(RB):
                            last = nc.tensor.matmul(o_view(u)[:, j, n, :],
                                                    probs[k % 2][:, kb, j * P:(j + 1) * P],
                                                    v[u][:, kb, n, :], start=kb == 0, stop=kb == RB - 1)
                    last.then_inc(valued, 1)

                def turn_o(t, u):
                    pe.wait_ge(o_ready, t + 1)
                    for k in range(RB):
                        last = nc.tensor.transpose(oT_ps[u][:, k * P:(k + 1) * P],
                                                   o[u][:, k, :, :].rearrange("p n d -> p (n d)"), ident)
                    last.then_inc(o_turned, 1)

                def output(t, u):
                    pe.wait_ge(oT_ready, t + 1)
                    for k in range(RB):
                        last = nc.tensor.matmul(y_ps[u][:, k * C:(k + 1) * C], oT[u][:, k * P:(k + 1) * P],
                                                wo[:, :], start=True, stop=True)
                    last.then_inc(y_done, 1)

                with pe.Fori(0, PAIRS) as i:
                    for u in range(2):
                        turn_x(2 * i + u, u)
                    for u in range(2):
                        project(2 * i + u, u)
                    for k in range(UNITS + 3):
                        if k < UNITS:
                            score(i, k)
                        if 2 <= k < UNITS + 2:
                            turn(i, k - 2)
                        if 3 <= k:
                            value(i, k - 3)
                        if k == UNITS:
                            turn_o(2 * i, 0)
                        if k == UNITS + 1:
                            output(2 * i, 0)
                    turn_o(2 * i + 1, 1)
                    output(2 * i + 1, 1)

            @block.scalar
            def _(act):
                act.preload_act_table_set("exp_and_others")
                act.wait_ge(params, 160)
                nc.scalar.activation(hbg[:, :], bg[:, :], ACT.Copy, scale=0.5).then_inc(hbg_ready, 1)
                act.wait_ge(hbg_ready, 1)
                act.wait_ge(ones_ready, 2)

                def evacuate_x(t, u):
                    act.wait_ge(x_turned, t + 1 + AHEAD)
                    nc.scalar.activation(xT[u][:, :], x_ps[u][:, 0:SIDE], ACT.Identity, bias=b[:, :],
                                         scale=g[:, :]).then_inc(xT_ready, 1)

                def evacuate(t, u):
                    act.wait_ge(qk_done, t + 1)
                    nc.scalar.activation(qT[u][:, :], qk_ps[u][:, 0:SIDE], ACT.Copy, scale=HID ** -0.5)
                    nc.scalar.activation(kT[u][:, :], qk_ps[u][:, SIDE:2 * SIDE],
                                         ACT.Copy).then_inc(qk_ready, 1)
                    act.wait_ge(vg_done, t + 1)
                    nc.scalar.activation(
                        v[u][:, :, :, 0:HID],
                        vg_ps[u][:, 0:SIDE].rearrange("p (b n d) -> p b n d", b=RB, n=HEADS), ACT.Copy)
                    nc.scalar.activation(gate[u][:, :], vg_ps[u][:, SIDE:2 * SIDE], ACT.Tanh,
                                         bias=hbg[:, :], scale=0.5).then_inc(vg_ready, 1)

                with act.Fori(0, PAIRS) as i:
                    for u in range(2):
                        evacuate_x(2 * i + u, u)
                    for u in range(2):
                        evacuate(2 * i + u, u)
                    for k in range(UNITS):
                        q = UNITS * i + k
                        act.wait_ge(valued, q + 1)
                        act.wait_ge(turned, q + 1 + AHEAD)
                        nc.scalar.activation(probs[k % 2][:, :, :].rearrange("p b j -> p (b j)"),
                                             p_ps[k % 2][:, :], ACT.Exp).then_inc(exped, 1)

            @block.vector
            def _(dve):
                dve.sem_inc(maxed, AHEAD)
                dve.sem_inc(x1_ready, AHEAD)

                def finish(i, u):
                    t = 2 * i + u
                    dve.wait_ge(valued, UNITS * i + HEADS * (u + 1) + AHEAD)
                    nc.vector.reciprocal(half_inv[u][:, :].rearrange("p (b n) -> p b n", b=RB),
                                         o_view(u)[:, :, :, HID]).then_inc(inv_ready, 1)
                    dve.wait_ge(inv_ready, t + 1)
                    nc.vector.tensor_tensor(
                        o[u][:, :, :, :], o_view(u)[:, :, :, 0:HID],
                        half_inv[u][:, :].rearrange("p (b n) -> p b n", b=RB).unsqueeze(3)
                        .broadcast_to([P, RB, HEADS, HID]), ALU.mult).then_inc(o_ready, 1)
                    dve.wait_ge(o_turned, t + 1)
                    nc.vector.scalar_tensor_tensor(oT[u][:, :], gate[u][:, :], 1.0, oT_ps[u][:, 0:SIDE],
                                                   ALU.add, ALU.mult).then_inc(oT_ready, 1)
                    hold(dve, stored[u], 16 * i, passed)
                    hold(dve, xb_ready, t + 1 + AHEAD, passed)
                    dve.wait_ge(y_done, t + 1)
                    nc.vector.tensor_tensor(x1[u][:, :, :], xb[u][:, :, :],
                                            y_ps[u][:, 0:RB * C].rearrange("p (b c) -> p b c", b=RB),
                                            ALU.add).then_inc(x1_ready, 1)

                with dve.Fori(0, PAIRS) as i:
                    for k in range(UNITS):
                        q = UNITS * i + k
                        hold(dve, lessened, q + 1, passed)
                        hold(dve, scored, q + 1, passed)
                        for j in range(RB):
                            last = nc.vector.tensor_tensor_reduce(
                                out=biased[k % 2][:, j, :], in0=s_ps[k % 2][:, j * SIDE:(j + 1) * SIDE],
                                in1=keep["bias"][:, k % HEADS, j, :], scale=1.0, scalar=-3.4e38,
                                op0=ALU.add, op1=ALU.max, accum_out=top[k % 2][:, j:j + 1])
                        last.then_inc(maxed, 1)
                    finish(i, 0)
                    finish(i, 1)
        s.clear()


TB = 4
TILE = TB * P
TILES = TOKENS // TILE


def phase_batchnorm(nc, io, keep):
    x1_v = io["x1"].rearrange("(t b p) c -> t p b c", b=TB, p=P)
    with ExitStack() as ctx:
        s = Space(nc, ctx, "bn")

        def two(name, shape):
            return [s.sb(f"{name}{u}", shape) for u in range(2)]

        w, wT = s.sb("w", [P, C]), s.sb("wT", [P, C])
        gamma, beta = s.sb("gamma", [P, 1]), s.sb("beta", [P, 1])
        x, h = two("x", [P, TB, C]), two("h", [P, TB, C])
        stats, mv = two("stats", [P, TB, 6]), two("mv", [P, TB, 2])
        vv, root, scale, shift = (two(n, [P, TB]) for n in ("vv", "root", "scale", "shift"))
        hT, wx = two("hT", [P, TILE]), two("wx", [P, TILE])
        all_stats, all_mv = s.sb("all_stats", [P, TILES, 6]), s.sb("all_mv", [P, 2])
        all_vv, all_root, all_inv, down = (s.sb(n, [P, 1]) for n in ("all_vv", "all_root", "all_inv", "down"))
        h_ps = [s.bank(f"h{u}") for u in range(2)]
        w_ps = [s.bank(f"w{u}") for u in range(2)]

        params, w_turned, wT_ready, passed = (s.sem(n) for n in ("params", "w_turned", "wT_ready", "passed"))
        x_loaded = [s.sem(f"x_loaded{u}") for u in range(2)]
        stored = [s.sem(f"stored{u}") for u in range(2)]
        step, vv_ready, root_ready, scaled, h_ready = (
            s.sem(n) for n in ("step", "vv_ready", "root_ready", "scaled", "h_ready"))
        h_turned, hT_ready, wx_done, wx_ready, counted = (
            s.sem(n) for n in ("h_turned", "hT_ready", "wx_done", "wx_ready", "counted"))
        final, final_vv, final_root = s.sem("final"), s.sem("final_vv"), s.sem("final_root")

        with nc.Block() as block:
            @block.sync
            def _(sp):
                sp.dma_start(w[:, :], io["L0_ffn_W"]).then_inc(params, 16)
                sp.dma_start(gamma[:, :], column(io["L0_ffn_gamma"])).then_inc(params, 16)
                sp.dma_start(beta[:, :], column(io["L0_ffn_beta"])).then_inc(params, 16)

                def load(i):
                    for u in range(2):
                        sp.wait_ge(h_ready, 2 * i + u + 1)
                        sp.dma_start(x[u][:, :, :], x1_v[2 * i + u]).then_inc(x_loaded[u], 16)

                def store(i):
                    for u in range(2):
                        t = 2 * i + u
                        sp.wait_ge(wx_ready, t + 1 + AHEAD)
                        sp.dma_start(io["wx"][:, bass.ds(t * TILE, TILE)], wx[u][:, :]).then_inc(stored[u], 16)

                load(0)
                with sp.Fori(0, TILES // 2 - 1) as i:
                    load(i + 1)
                    store(i)
                store(TILES // 2 - 1)
                for u in range(2):
                    sp.wait_ge(stored[u], 16 * (TILES // 2))

            @block.vector
            def _(dve):
                def count(t, u):
                    dve.wait_ge(wx_ready, t + 1 + AHEAD)
                    nc.vector.bn_stats(all_stats[:, bass.ds(t, 1), :].rearrange("p a s -> p (a s)"),
                                       wx[u][:, :]).then_inc(counted, 1)

                dve.sem_inc(counted, AHEAD)
                with dve.Fori(0, TILES // 2) as i:
                    for u in range(2):
                        t = 2 * i + u
                        dve.wait_ge(x_loaded[u], 16 * i + 16)
                        for k in range(TB):
                            last = nc.vector.bn_stats(stats[u][:, k, :], x[u][:, k, :])
                        last.then_inc(step, 1)
                        hold(dve, step, t * 2 + 1, passed)
                        for k in range(TB):
                            last = nc.vector.bn_aggr(mv[u][:, k, :], stats[u][:, k, :])
                        last.then_inc(step, 1)
                        dve.wait_ge(step, t * 2 + 2)
                        nc.vector.tensor_scalar(vv[u][:, :], mv[u][:, :, 1], 1.0, 1e-5,
                                                ALU.mult, ALU.add).then_inc(vv_ready, 1)
                    for u in range(2):
                        t = 2 * i + u
                        dve.wait_ge(root_ready, t + 1)
                        nc.vector.reciprocal(scale[u][:, :], root[u][:, :]).then_inc(scaled, 1)
                        dve.wait_ge(scaled, 2 * t + 1)
                        nc.vector.scalar_tensor_tensor(shift[u][:, :], mv[u][:, :, 0], -1.0, scale[u][:, :],
                                                       ALU.mult, ALU.mult).then_inc(scaled, 1)
                    for u in range(2):
                        count(2 * i + u, u)
                hold(dve, counted, TILES + AHEAD, passed)
                nc.vector.bn_aggr(all_mv[:, :], all_stats[:, :, :].rearrange("p t s -> p (t s)")).then_inc(final, 1)
                dve.wait_ge(final, 1)
                nc.vector.tensor_scalar(all_vv[:, :], all_mv[:, 1:2], 1.0, 1e-5, ALU.mult,
                                        ALU.add).then_inc(final_vv, 1)
                dve.wait_ge(final_root, 1)
                nc.vector.reciprocal(all_inv[:, :], all_root[:, :]).then_inc(final, 1)
                dve.wait_ge(final, 2)
                nc.vector.tensor_tensor(keep["bn_scale"][:, :], all_inv[:, :], gamma[:, :],
                                        ALU.mult).then_inc(final, 1)
                dve.wait_ge(final, 3)
                nc.vector.tensor_tensor(down[:, :], all_mv[:, 0:1], keep["bn_scale"][:, :],
                                        ALU.mult).then_inc(final, 1)
                dve.wait_ge(final, 4)
                nc.vector.tensor_tensor(keep["bn_shift"][:, :], beta[:, :], down[:, :], ALU.subtract)

            @block.gpsimd
            def _(pool):
                pool.sem_inc(h_ready, AHEAD)
                with pool.Fori(0, TILES // 2) as i:
                    for u in range(2):
                        t = 2 * i + u
                        hold(pool, scaled, 2 * t + 2, passed)
                        hold(pool, h_turned, t + 1, passed)
                        for k in range(TB):
                            last = nc.gpsimd.tensor_scalar(h[u][:, k, :], x[u][:, k, :],
                                                           scale[u][:, k:k + 1], shift[u][:, k:k + 1],
                                                           ALU.mult, ALU.add)
                        last.then_inc(h_ready, 1)

            @block.tensor
            def _(pe):
                pe.sem_inc(h_turned, AHEAD)
                pe.wait_ge(params, 48)
                nc.tensor.transpose(w_ps[0][:, 0:C], w[:, :], keep["ident"][:, :]).then_inc(w_turned, 1)
                pe.wait_ge(wT_ready, 1)
                with pe.Fori(0, TILES // 2) as i:
                    for u in range(2):
                        t = 2 * i + u
                        pe.wait_ge(h_ready, t + 1 + AHEAD)
                        for k in range(TB):
                            last = nc.tensor.transpose(h_ps[u][:, k * P:(k + 1) * P], h[u][:, k, :],
                                                       keep["ident"][:, :])
                        last.then_inc(h_turned, 1)
                    for u in range(2):
                        t = 2 * i + u
                        pe.wait_ge(wx_ready, t + 1)
                        pe.wait_ge(hT_ready, t + 1)
                        nc.tensor.matmul(w_ps[u][:, :], wT[:, :], hT[u][:, :], start=True,
                                         stop=True).then_inc(wx_done, 1)

            @block.scalar
            def _(act):
                act.preload_act_table_set("sqrt_and_others")
                act.sem_inc(wx_ready, AHEAD)
                act.wait_ge(w_turned, 1)
                nc.scalar.activation(wT[:, :], w_ps[0][:, 0:C], ACT.Copy).then_inc(wT_ready, 1)
                with act.Fori(0, TILES // 2) as i:
                    for u in range(2):
                        t = 2 * i + u
                        act.wait_ge(vv_ready, t + 1)
                        nc.scalar.activation(root[u][:, :], vv[u][:, :], ACT.Sqrt).then_inc(root_ready, 1)
                    for u in range(2):
                        t = 2 * i + u
                        act.wait_ge(h_turned, t + 1 + AHEAD)
                        nc.scalar.activation(hT[u][:, :], h_ps[u][:, :], ACT.Copy).then_inc(hT_ready, 1)
                    for u in range(2):
                        t = 2 * i + u
                        act.wait_ge(stored[u], 16 * i)
                        act.wait_ge(counted, t + 1)
                        act.wait_ge(wx_done, t + 1)
                        nc.scalar.activation(wx[u][:, :], w_ps[u][:, :], ACT.Copy).then_inc(wx_ready, 1)
                act.wait_ge(final_vv, 1)
                nc.scalar.activation(all_root[:, :], all_vv[:, :], ACT.Sqrt).then_inc(final_root, 1)
        s.clear()


HALVES = 2
CHUNKS = 256
RUN = TOKENS // HALVES // CHUNKS
WARM = 32
GROUPS = 2
LANES = CHUNKS // GROUPS
TOLERANCE = 1e-6


def phase_recurrence(nc, io, keep):
    PART = 2048
    PARTS = TOKENS // HALVES // PART
    N = CHUNKS * RUN
    DONE = 2 * GROUPS
    with ExitStack() as ctx:
        s = Space(nc, ctx, "rnn")
        v, vT = s.sb("v", [P, C]), s.sb("vT", [P, C])
        seq = s.sb("seq", [P, N])
        y = [[s.sb(f"y{g}{k}", [P, LANES]) for k in range(2)] for g in range(GROUPS)]
        z = [s.sb(f"z{g}", [P, LANES]) for g in range(GROUPS)]
        starts = s.sb("starts", [P, CHUNKS + 1])
        gap, zero = s.sb("gap", [P, CHUNKS]), s.sb("zero", [P, LANES])
        worst, worst_all, z1 = s.sb("worst", [P, 1]), s.sb("worst_all", [P, 1]), s.sb("z_one", [P, 1])
        flag = [s.sb(f"flag{f}", [P, 1], I32) for f in range(HALVES)]
        v_ps = [s.bank(f"v{g}") for g in range(GROUPS)]
        one_ps = s.bank("one")

        params, v_turned, vT_ready, first, zeroed, passed = (
            s.sem(n) for n in ("params", "v_turned", "vT_ready", "first", "zeroed", "passed"))
        names = ("loaded", "normed", "multiplied", "added", "squashed", "written", "started", "gapped",
                 "reduced", "all_reduced", "flagged", "reloaded", "renormed", "one_product", "one_sum",
                 "one_state", "settled", "stored")
        hs = [{n: s.sem(f"{n}{f}") for n in names} for f in range(HALVES)]

        def lanes(g, t):
            return seq[:, :].rearrange("p (g l r) -> p g l r", g=GROUPS, l=LANES)[:, g, :, bass.ds(t, 1)] \
                .rearrange("p l a -> p (l a)")

        with nc.Block() as block:
            @block.sync
            def _(sp):
                def load(f, sem):
                    for k in range(PARTS):
                        sp.dma_start(seq[:, k * PART:(k + 1) * PART],
                                     io["wx"][:, (f * PARTS + k) * PART:(f * PARTS + k + 1) * PART]
                                     ).then_inc(sem, 16)

                sp.dma_start(v[:, :], io["L0_ffn_V"]).then_inc(params, 16)
                for f in range(HALVES):
                    m = hs[f]
                    if f:
                        sp.wait_ge(hs[f - 1]["stored"], 16 * PARTS)
                    load(f, m["loaded"])
                    sp.wait_ge(m["flagged"], 1)
                    with sp.If(sp.value_load(flag[f][0:1, 0:1])):
                        load(f, m["reloaded"])
                    sp.wait_ge(m["settled"], 1)
                    for k in range(PARTS):
                        sp.dma_start(io["yT"][:, (f * PARTS + k) * PART:(f * PARTS + k + 1) * PART],
                                     seq[:, k * PART:(k + 1) * PART]).then_inc(m["stored"], 16)
                sp.wait_ge(hs[HALVES - 1]["stored"], 16 * PARTS)

            @block.tensor
            def _(pe):
                pe.wait_ge(params, 16)
                nc.tensor.transpose(v_ps[0][:, 0:C], v[:, :], keep["ident"][:, :]).then_inc(v_turned, 1)
                pe.wait_ge(vT_ready, 1)
                for f in range(HALVES):
                    m = hs[f]
                    with pe.Fori(0, (WARM + RUN) // 2) as i:
                        for k in range(2):
                            for g in range(GROUPS):
                                pe.wait_ge(m["squashed"], (2 * i + k) * GROUPS + g + 1)
                                nc.tensor.matmul(v_ps[g][:, 0:LANES], vT[:, :], y[g][k][:, :], start=True,
                                                 stop=True).then_inc(m["multiplied"], 1)
                    pe.wait_ge(m["flagged"], 1)
                    with pe.If(pe.value_load(flag[f][0:1, 0:1])):
                        nc.tensor.matmul(one_ps[:, 0:1], vT[:, :], starts[:, 0:1], start=True,
                                         stop=True).then_inc(m["one_product"], 1)
                        with pe.Fori(1, N) as i:
                            pe.wait_ge(m["one_state"], i)
                            nc.tensor.matmul(one_ps[:, 0:1], vT[:, :], seq[:, bass.ds(i - 1, 1)], start=True,
                                             stop=True).then_inc(m["one_product"], 1)

            @block.vector
            def _(dve):
                nc.vector.memset(starts[:, 0:1], 0.0).then_inc(first, 1)
                for f in range(HALVES):
                    m = hs[f]

                    def norm(before, after):
                        dve.wait_ge(before, 16 * PARTS)
                        for k in range(PARTS):
                            piece = seq[:, k * PART:(k + 1) * PART]
                            nc.vector.tensor_scalar(piece, piece, keep["bn_scale"][:, :], keep["bn_shift"][:, :],
                                                    ALU.mult, ALU.add).then_inc(after, 1)
                        dve.wait_ge(after, PARTS)

                    def add(count, g, t):
                        dve.wait_ge(m["multiplied"], count + 1)
                        nc.vector.tensor_tensor(z[g][:, :], v_ps[g][:, 0:LANES], lanes(g, t),
                                                ALU.add).then_inc(m["added"], 1)

                    norm(m["loaded"], m["normed"])
                    with dve.Fori(0, WARM // 2) as i:
                        for k in range(2):
                            for g in range(GROUPS):
                                add((2 * i + k) * GROUPS + g, g, RUN - WARM + 2 * i + k)
                    with dve.Fori(0, RUN // 2) as i:
                        for k in range(2):
                            for g in range(GROUPS):
                                add((WARM + 2 * i + k) * GROUPS + g, g, 2 * i + k)
                    dve.wait_ge(m["written"], GROUPS * RUN + DONE)
                    ends = seq[:, :].rearrange("p (c r) -> p c r", r=RUN)[:, :, RUN - 1]
                    nc.vector.tensor_tensor(gap[:, 0:CHUNKS - 1], ends[:, 0:CHUNKS - 1], starts[:, 1:CHUNKS],
                                            ALU.subtract).then_inc(m["gapped"], 1)
                    dve.wait_ge(m["gapped"], 1)
                    nc.vector.tensor_reduce(worst[:, :], gap[:, 0:CHUNKS - 1], AX.X, ALU.max,
                                            apply_absolute_value=True).then_inc(m["reduced"], 1)
                    dve.wait_ge(m["all_reduced"], 1)
                    nc.vector.tensor_scalar(flag[f][:, :], worst_all[:, :], TOLERANCE, None,
                                            ALU.is_gt).then_inc(m["flagged"], 1)
                    dve.wait_ge(m["flagged"], 1)
                    with dve.If(dve.value_load(flag[f][0:1, 0:1])):
                        norm(m["reloaded"], m["renormed"])
                        with dve.Fori(0, N) as i:
                            dve.wait_ge(m["one_product"], i + 1)
                            nc.vector.tensor_tensor(z1[:, :], one_ps[:, 0:1], seq[:, bass.ds(i, 1)],
                                                    ALU.add).then_inc(m["one_sum"], 1)
                        dve.wait_ge(m["one_state"], N)
                    nc.vector.tensor_copy(starts[:, 0:1], seq[:, N - 1:N]).then_inc(m["settled"], 1)

            @block.scalar
            def _(act):
                act.preload_act_table_set("sigmoid_and_others")
                act.wait_ge(v_turned, 1)
                nc.scalar.activation(vT[:, :], v_ps[0][:, 0:C], ACT.Copy).then_inc(vT_ready, 1)
                act.wait_ge(first, 1)
                act.wait_ge(zeroed, 1)
                for f in range(HALVES):
                    m = hs[f]
                    if f:
                        act.wait_ge(hs[f - 1]["settled"], 1)

                    for g in range(GROUPS):
                        nc.scalar.activation(y[g][0][:, :], zero[:, :], ACT.Copy).then_inc(m["squashed"], 1)

                    def squash(step, g, k):
                        act.wait_ge(m["added"], step * GROUPS + g + 1)
                        nc.scalar.activation(y[g][1 - k][:, :], z[g][:, :], ACT.Sigmoid
                                             ).then_inc(m["squashed"], 1)

                    with act.Fori(0, WARM // 2 - 1) as i:
                        for k in range(2):
                            for g in range(GROUPS):
                                squash(2 * i + k, g, k)
                    for g in range(GROUPS):
                        squash(WARM - 2, g, 0)
                    for g in range(GROUPS):
                        act.wait_ge(m["added"], (WARM - 1) * GROUPS + g + 1)
                        nc.scalar.activation(starts[:, g * LANES + 1:(g + 1) * LANES + 1], z[g][:, :],
                                             ACT.Sigmoid).then_inc(m["started"], 1)
                    act.wait_ge(m["started"], GROUPS)
                    for g in range(GROUPS):
                        nc.scalar.activation(y[g][0][:, :], starts[:, g * LANES:(g + 1) * LANES], ACT.Copy
                                             ).then_inc(m["squashed"], 1)
                    with act.Fori(0, RUN // 2) as i:
                        for k in range(2):
                            for g in range(GROUPS):
                                act.wait_ge(m["written"], (2 * i + k) * GROUPS + g + 1)
                                squash(WARM + 2 * i + k, g, k)
                    act.wait_ge(m["flagged"], 1)
                    with act.If(act.value_load(flag[f][0:1, 0:1])):
                        with act.Fori(0, N) as i:
                            act.wait_ge(m["one_sum"], i + 1)
                            nc.scalar.activation(seq[:, bass.ds(i, 1)], z1[:, :], ACT.Sigmoid
                                                 ).then_inc(m["one_state"], 1)

            @block.gpsimd
            def _(pool):
                pool.memset(zero[:, :], 0.0).then_inc(zeroed, 1)
                for f in range(HALVES):
                    m = hs[f]
                    pool.sem_inc(m["written"], DONE)
                    with pool.Fori(0, RUN // 2) as i:
                        for k in range(2):
                            for g in range(GROUPS):
                                hold(pool, m["squashed"], (WARM + 2 * i + k + 1) * GROUPS + g + 1, passed)
                                nc.gpsimd.tensor_copy(lanes(g, 2 * i + k), y[g][1 - k][:, :]
                                                      ).then_inc(m["written"], 1)
                    pool.wait_ge(m["reduced"], 1)
                    nc.gpsimd.partition_all_reduce(worst_all[:, :], worst[:, :], P,
                                                   bass.bass_isa.ReduceOp.max).then_inc(m["all_reduced"], 1)
        s.clear()


def phase_join(nc, io, keep):
    U = 4
    x1_v = io["x1"].rearrange("(t b p) c -> t p b c", b=TB, p=P)
    x2_v = io["x2"].rearrange("(t b p) c -> t p b c", b=TB, p=P)
    hT_v = io["hT"].rearrange("p r w -> p (r w)")
    with ExitStack() as ctx:
        s = Space(nc, ctx, "join")

        def ring(name, shape):
            return [s.sb(f"{name}{u}", shape) for u in range(U)]

        x1, x2, h = (ring(n, [P, TB, C]) for n in ("x1", "x2", "h"))
        y, hT = ring("y", [P, TILE]), ring("hT", [P, TILE])
        stats, mv = ring("stats", [P, TB, 6]), ring("mv", [P, TB, 2])
        vv, root, scale, shift = (ring(n, [P, TB]) for n in ("vv", "root", "scale", "shift"))
        zeros = s.sb("zeros", [P, SIDE])
        y_ps = [s.bank(f"y{u}") for u in range(U)]
        h_ps = [s.bank(f"h{u}") for u in range(U)]

        zeros_ready, edges, passed = s.sem("zeros_ready"), s.sem("edges"), s.sem("passed")
        x1_loaded = [s.sem(f"x1_loaded{u}") for u in range(U)]
        y_loaded = [s.sem(f"y_loaded{u}") for u in range(U)]
        x2_stored = [s.sem(f"x2_stored{u}") for u in range(U)]
        hT_stored = [s.sem(f"hT_stored{u}") for u in range(U)]
        y_turned, x2_ready, step, vv_ready, root_ready, scaled, h_ready, h_turned, hT_ready = (
            s.sem(n) for n in ("y_turned", "x2_ready", "step", "vv_ready", "root_ready", "scaled",
                               "h_ready", "h_turned", "hT_ready"))

        with nc.Block() as block:
            @block.sync
            def _(sp):
                sp.wait_ge(zeros_ready, 1)
                for r in (0, SIDE + 1):
                    sp.dma_start(io["hT"][:, r, :], zeros[:, :]).then_inc(edges, 16)

                def load(i):
                    for u in range(U):
                        t = U * i + u
                        sp.wait_ge(x2_ready, t + 1)
                        sp.dma_start(x1[u][:, :, :], x1_v[t]).then_inc(x1_loaded[u], 16)
                        sp.wait_ge(y_turned, t + 1)
                        sp.dma_start(y[u][:, :], io["yT"][:, bass.ds(t * TILE, TILE)]).then_inc(y_loaded[u], 16)

                def store(i):
                    for u in range(U):
                        t = U * i + u
                        sp.wait_ge(x2_ready, t + 1 + U)
                        sp.dma_start(x2_v[t], x2[u][:, :, :]).then_inc(x2_stored[u], 16)
                        sp.wait_ge(hT_ready, t + 1)
                        sp.dma_start(hT_v[:, bass.ds(t * TILE + SIDE, TILE)], hT[u][:, :]).then_inc(hT_stored[u], 16)

                load(0)
                with sp.Fori(0, TILES // U - 1) as i:
                    load(i + 1)
                    store(i)
                store(TILES // U - 1)
                sp.wait_ge(edges, 32)
                for u in range(U):
                    sp.wait_ge(x2_stored[u], 16 * (TILES // U))
                    sp.wait_ge(hT_stored[u], 16 * (TILES // U))

            @block.tensor
            def _(pe):
                pe.sem_inc(y_turned, U)
                pe.sem_inc(h_turned, U)
                with pe.Fori(0, TILES // U) as i:
                    for u in range(U):
                        t = U * i + u
                        pe.wait_ge(y_loaded[u], 16 * i + 16)
                        pe.wait_ge(x2_ready, t + 1)
                        for k in range(TB):
                            last = nc.tensor.transpose(y_ps[u][:, k * P:(k + 1) * P],
                                                       y[u][:, k * P:(k + 1) * P], keep["ident"][:, :])
                        last.then_inc(y_turned, 1)
                    for u in range(U):
                        t = U * i + u
                        pe.wait_ge(h_ready, t + 1 + U)
                        pe.wait_ge(hT_ready, t)
                        for k in range(TB):
                            last = nc.tensor.transpose(h_ps[u][:, k * P:(k + 1) * P], h[u][:, k, :],
                                                       keep["ident"][:, :])
                        last.then_inc(h_turned, 1)

            @block.vector
            def _(dve):
                nc.vector.memset(zeros[:, :], 0.0).then_inc(zeros_ready, 1)
                dve.sem_inc(x2_ready, U)
                with dve.Fori(0, TILES // U) as i:
                    for u in range(U):
                        t = U * i + u
                        hold(dve, x2_stored[u], 16 * i, passed)
                        hold(dve, h_ready, t + 1, passed)
                        hold(dve, x1_loaded[u], 16 * i + 16, passed)
                        dve.wait_ge(y_turned, t + 1 + U)
                        nc.vector.tensor_tensor(x2[u][:, :, :], x1[u][:, :, :],
                                                y_ps[u][:, :].rearrange("p (b c) -> p b c", b=TB),
                                                ALU.add).then_inc(x2_ready, 1)
                        dve.wait_ge(x2_ready, t + 1 + U)
                        for k in range(TB):
                            last = nc.vector.bn_stats(stats[u][:, k, :], x2[u][:, k, :])
                        last.then_inc(step, 1)
                        hold(dve, step, t * 2 + 1, passed)
                        for k in range(TB):
                            last = nc.vector.bn_aggr(mv[u][:, k, :], stats[u][:, k, :])
                        last.then_inc(step, 1)
                        dve.wait_ge(step, t * 2 + 2)
                        nc.vector.tensor_scalar(vv[u][:, :], mv[u][:, :, 1], 1.0, 1e-6,
                                                ALU.mult, ALU.add).then_inc(vv_ready, 1)
                    for u in range(U):
                        t = U * i + u
                        dve.wait_ge(root_ready, t + 1)
                        nc.vector.reciprocal(scale[u][:, :], root[u][:, :]).then_inc(scaled, 1)
                        dve.wait_ge(scaled, 2 * t + 1)
                        nc.vector.scalar_tensor_tensor(shift[u][:, :], mv[u][:, :, 0], -1.0, scale[u][:, :],
                                                       ALU.mult, ALU.mult).then_inc(scaled, 1)

            @block.gpsimd
            def _(pool):
                pool.sem_inc(h_ready, U)
                with pool.Fori(0, TILES // U) as i:
                    for u in range(U):
                        t = U * i + u
                        hold(pool, scaled, 2 * t + 2, passed)
                        hold(pool, h_turned, t + 1, passed)
                        for k in range(TB):
                            last = nc.gpsimd.tensor_scalar(h[u][:, k, :], x2[u][:, k, :],
                                                           scale[u][:, k:k + 1], shift[u][:, k:k + 1],
                                                           ALU.mult, ALU.add)
                        last.then_inc(h_ready, 1)

            @block.scalar
            def _(act):
                act.preload_act_table_set("sqrt_and_others")
                with act.Fori(0, TILES // U) as i:
                    for u in range(U):
                        t = U * i + u
                        act.wait_ge(vv_ready, t + 1)
                        nc.scalar.activation(root[u][:, :], vv[u][:, :], ACT.Sqrt).then_inc(root_ready, 1)
                    for u in range(U):
                        t = U * i + u
                        act.wait_ge(hT_stored[u], 16 * i)
                        act.wait_ge(h_turned, t + 1 + U)
                        nc.scalar.activation(hT[u][:, :], h_ps[u][:, :], ACT.Copy).then_inc(hT_ready, 1)
        s.clear()


STATES = 8
RANK = 8
TAPS = 3
PAD = SIDE + 2
OVERFLOW = 88.72283936
BELOW = 88.72283172607
SLOT = 32


def phase_mamba(nc, io, keep):
    ROWS = TILE // SIDE
    x2_v = io["x2"].rearrange("(t b p) c -> t p b c", b=TB, p=P)
    x3_v = io["x3"].rearrange("(t b p) c -> t p b c", b=TB, p=P)
    par = {k[8:]: v for k, v in io.items() if k.startswith("L1_conv_")}
    groups = par["w1"].shape[0]
    G = C // groups
    with ExitStack() as ctx:
        s = Space(nc, ctx, "mamba")

        def two(name, shape, dt=F32):
            return [s.sb(f"{name}{u}", shape, dt) for u in range(2)]

        w1n, w2n, won, inn_u, inn_z, outn = (s.sb(n, [P, C]) for n in ("w1n", "w2n", "won", "inn_u", "inn_z", "outn"))
        tapn = s.sb("tapn", [P, TAPS * TAPS, C])
        xpn = s.sb("xpn", [3 * SLOT, C])
        xp_dt, dt_t = s.sb("xp_dt", [RANK, C]), s.sb("dt_t", [RANK, C])
        tap_t = s.sb("tap_t", [P, TAPS * TAPS, C])
        w2_t, wo_t, in_u_t, in_z_t, out_t, d_t = (s.sb(n, [P, C]) for n in ("w2_t", "wo_t", "in_u_t", "in_z_t", "out_t", "d_t"))
        xp_t = s.sb("xp_t", [P, 3 * SLOT])
        dw, cw, a_log, a_neg = s.sb("dw", [P, TAPS * TAPS]), s.sb("cw", [P, 3]), s.sb("a_log", [P, STATES]), s.sb("a_neg", [P, STATES])
        a_exp, a_low, a_gone, a_mil, limit = (
            s.sb(n, [P, STATES]) for n in ("a_exp", "a_low", "a_gone", "a_mil", "limit"))
        cb, dtb, dpar, gamma, beta = (s.sb(n, [P, 1]) for n in ("cb", "dtb", "dpar", "gamma", "beta"))
        select = s.sb("select", [3 * SLOT, 2 * STATES, P], BF16)
        half, one = s.sb("half", [P, TB]), s.sb("one", [P, 1])
        win = two("win", [P, ROWS + 2, PAD])
        conv, bent, size, ex, logs, rest, over = (s.sb(n, [P, TILE]) for n in
                                                  ("conv", "bent", "size", "ex", "logs", "rest", "over"))
        raw = two("raw", [P, TILE + 2])
        u_act, z_act, delta, du = (two(n, [P, TILE]) for n in ("u_act", "z_act", "delta", "du"))
        parts = two("parts", [3 * SLOT, TILE], BF16)
        remain, middle = s.sb("remain", [3 * SLOT, TILE]), s.sb("middle", [3 * SLOT, TILE], BF16)
        capped = two("capped", [P, TILE])
        decay, drive, seen = two("decay", [P, TILE]), two("drive", [P, TILE]), two("seen", [P, TILE])
        state = [[s.sb(f"state{u}{n}", [P, TILE]) for n in range(STATES)] for u in range(2)]
        w2_act, y, yz = two("w2_act", [P, TILE]), two("y", [P, TILE]), two("yz", [P, TILE])
        x2, x3 = two("x2", [P, TB, C]), two("x3", [P, TB, C])
        stats, mv, vv, scale, shift = (s.sb("stats", [P, TB, 6]), s.sb("mv", [P, TB, 2]), s.sb("vv", [P, TB]),
                                       s.sb("scale", [P, TB]), s.sb("shift", [P, TB]))
        normed, affine, fused = s.sb("normed", [P, TB, C]), s.sb("affine", [P, TILE]), s.sb("fused", [P, TILE])

        b_ps, c_ps, sum_ps, conv_ps, w2_ps, u_ps, z_ps, tail_ps = (
            s.bank(n) for n in ("b", "c", "sum", "conv", "w2", "u", "z", "tail"))
        x_ps, d_ps = conv_ps, u_ps

        names = ("params blank placed scaled_taps w_turned w_kept d_made a_made a_held ready selector passed "
                 "conv_done conv_ready w2_done w2_ready u_done raw_ready bent0 bent1 bent2 u_ready z_done z_ready "
                 "x_done d_done high_ready remain_ready mid_ready middle_ready parts_ready size_ready ex_ready "
                 "log_ready over_ready back_ready rest_ready sum1 delta_ready du_ready "
                 "b_done c_done driven capped decayed scanned seen_ready summed "
                 "y_ready yz_ready out_done tail_step vv_ready scale_ready shift_ready normed_ready n_turned "
                 "affine_ready fused_ready o_done x3_ready").split()
        S = {n: s.sem(n) for n in names}
        win_loaded = [s.sem(f"win_loaded{u}") for u in range(2)]
        x2_loaded = [s.sem(f"x2_loaded{u}") for u in range(2)]
        stored = [s.sem(f"stored{u}") for u in range(2)]

        PARAMS = 3 * groups + 3 + 11 + 2

        def windows(eng, window):
            window(-1, 1, -1, True, False, False)
            window(0, 0, 0, True, True, False)
            with eng.Fori(0, TILES // 2 - 1) as i:
                window(2 * i + 1, 1, i, True, True, True)
                window(2 * i + 2, 0, i + 1, True, True, True)
            window(TILES - 1, 1, TILES // 2 - 1, False, True, True)
            window(TILES, 0, TILES // 2, False, False, True)


        with nc.Block() as block:
            @block.sync
            def _(sp):
                n = 0
                sp.wait_ge(S["blank"], 4)
                for w, name in ((w1n, "w1"), (w2n, "w2"), (won, "wout")):
                    for k in range(groups):
                        sp.dma_start(w[k * G:(k + 1) * G, k * G:(k + 1) * G], par[name][k]).then_inc(S["params"], 16)
                        n += 1
                for k in range(3):
                    sp.dma_start(xpn[k * SLOT:k * SLOT + 2 * STATES, :],
                                 par["x_proj_w"][RANK:RANK + 2 * STATES, :]).then_inc(S["params"], 16)
                    n += 1
                for dst, src in ((inn_u, par["in_proj_w"][0:C, :]), (inn_z, par["in_proj_w"][C:2 * C, :]),
                                 (outn, par["out_proj_w"]), (xp_dt, par["x_proj_w"][0:RANK, :]),
                                 (cw, par["conv1d_w"]), (a_log, par["A_log"]),
                                 (cb, column(par["conv1d_b"])), (dtb, column(par["dt_proj_b"])),
                                 (dpar, column(par["D_param"])), (gamma, column(par["gamma"])),
                                 (beta, column(par["beta"]))):
                    sp.dma_start(dst[:, :], src).then_inc(S["params"], 16)
                    n += 1
                with nc.allow_non_contiguous_dma(reason="small weights, once"):
                    sp.dma_start(dt_t[:, :], par["dt_proj_w"].rearrange("d r -> r d")).then_inc(S["params"], 16)
                    sp.dma_start(dw[:, :], par["dw"].rearrange("a b c d -> d (a b c)")).then_inc(S["params"], 16)
                n += 2
                assert n == PARAMS, n

                def window(t, u, half_t, front, scan, back):
                    if front:
                        f, v = t + 1, 1 - u
                        sp.wait_ge(S["w2_done"], f + 1)
                        sp.dma_start(win[v][:, :, 1:1 + SIDE],
                                     io["hT"][:, bass.ds(ROWS * f, ROWS + 2), :]).then_inc(win_loaded[v], 16)
                    if scan:
                        sp.wait_ge(S["x3_ready"], t + 1)
                        sp.dma_start(x2[u][:, :, :], x2_v[t]).then_inc(x2_loaded[u], 16)
                    if back:
                        sp.wait_ge(S["x3_ready"], t + AHEAD)
                        sp.dma_start(x3_v[t - 1], x3[1 - u][:, :, :]).then_inc(stored[1 - u], 16)

                windows(sp, window)
                for u in range(2):
                    sp.wait_ge(stored[u], 16 * (TILES // 2))

            @block.tensor
            def _(pe):
                ident = keep["ident"][:, :]
                pe.wait_ge(S["params"], 16 * PARAMS)
                pe.wait_ge(S["scaled_taps"], 1)
                turns = [(w2n, P), (won, P), (inn_u, P), (inn_z, P), (outn, P)] \
                    + [(tapn[:, k, :], P) for k in range(TAPS * TAPS)] + [(xpn, 3 * SLOT)]
                for k, (w, rows) in enumerate(turns):
                    pe.wait_ge(S["w_kept"], k)
                    src = w if k >= 5 and k < 5 + TAPS * TAPS else w[:, :]
                    nc.tensor.transpose(conv_ps[:, 0:rows], src, ident[0:rows, 0:rows]).then_inc(S["w_turned"], 1)
                pe.wait_ge(S["w_kept"], len(turns))
                nc.tensor.matmul(conv_ps[:, 0:C], xp_dt[:, :], dt_t[:, :], start=True, stop=True
                                 ).then_inc(S["w_turned"], 1)
                pe.wait_ge(S["w_kept"], len(turns) + 1)
                pe.wait_ge(S["selector"], 4)
                pe.sem_inc(S["w2_done"], AHEAD)
                pe.sem_inc(S["summed"], AHEAD)

                def window(t, u, half_t, front, scan, back):
                    f, v, b = t + 1, 1 - u, t - 1
                    loads_f = half_t + (1 if u == 1 else 0)

                    def taps(ks):
                        if ks[0] == 0:
                            pe.wait_ge(win_loaded[v], 16 * loads_f + 16)
                            pe.wait_ge(S["remain_ready"], f + 2)
                        for k in ks:
                            dy, dx = divmod(k, TAPS)
                            last = nc.tensor.matmul(conv_ps[:, :].rearrange("p (r w) -> p r w", r=ROWS),
                                                    tap_t[:, k, :], win[v][:, dy:dy + ROWS, dx:dx + SIDE],
                                                    start=k == 0, stop=k == TAPS * TAPS - 1)
                        if ks[-1] == TAPS * TAPS - 1:
                            last.then_inc(S["conv_done"], 1)

                    for n in range(STATES):
                        q = STATES * t + n
                        if scan:
                            if n == 0:
                                pe.wait_ge(S["parts_ready"], t + 1)
                            pe.wait_ge(S["driven"], q)
                            nc.tensor.matmul(b_ps[:, :], select[:, n, :], parts[u][:, :], start=True,
                                             stop=True).then_inc(S["b_done"], 1)
                        if front and n < 3:
                            taps(range(3 * n, 3 * n + 3))
                        if n == 2 and back:
                            pe.wait_ge(S["yz_ready"], b + 1 + AHEAD)
                            pe.wait_ge(S["x3_ready"], b + 2)
                            for k in range(TB):
                                last = nc.tensor.matmul(tail_ps[:, k * C:(k + 1) * C], yz[1 - u][:, k * P:(k + 1) * P],
                                                        out_t[:, :], start=True, stop=True)
                            last.then_inc(S["out_done"], 1)
                        if n == 3 and scan:
                            pe.wait_ge(S["w2_ready"], t + 1 + 1)
                            nc.tensor.matmul(w2_ps[:, :].rearrange("p (r w) -> p r w", r=ROWS), w2_t[:, :],
                                             win[u][:, 1:1 + ROWS, 1:1 + SIDE], start=True,
                                             stop=True).then_inc(S["w2_done"], 1)
                        if n == 3 and front:
                            pe.wait_ge(S["over_ready"], f + 2)
                            pe.wait_ge(S["conv_ready"], f + 1)
                            nc.tensor.matmul(u_ps[:, :], in_u_t[:, :], conv[:, :], start=True,
                                             stop=True).then_inc(S["u_done"], 1)
                        if n == 4 and front:
                            pe.wait_ge(S["z_ready"], f + 2)
                            nc.tensor.matmul(z_ps[:, :], in_z_t[:, :], conv[:, :], start=True,
                                             stop=True).then_inc(S["z_done"], 1)
                        if n == 6 and back:
                            pe.wait_ge(S["normed_ready"], b + 1)
                            for k in range(TB):
                                last = nc.tensor.transpose(tail_ps[:, k * P:(k + 1) * P], normed[:, k, :], ident)
                            last.then_inc(S["n_turned"], 1)
                        if n == 6 and front:
                            pe.wait_ge(S["u_ready"], f + 1)
                            nc.tensor.matmul(x_ps[0:3 * SLOT, :], xp_t[:, :], u_act[v][:, :], start=True,
                                             stop=True).then_inc(S["x_done"], 1)
                            nc.tensor.matmul(d_ps[:, :], d_t[:, :], u_act[v][:, :], start=True,
                                             stop=True).then_inc(S["d_done"], 1)
                        if n == 7 and back:
                            pe.wait_ge(S["fused_ready"], b + 1 + AHEAD)
                            for k in range(TB):
                                last = nc.tensor.matmul(tail_ps[:, k * C:(k + 1) * C], fused[:, k * P:(k + 1) * P],
                                                        wo_t[:, :], start=True, stop=True)
                            last.then_inc(S["o_done"], 1)
                        if scan:
                            pe.wait_ge(S["seen_ready"], q)
                            nc.tensor.matmul(c_ps[:, :], select[:, STATES + n, :], parts[u][:, :], start=True,
                                             stop=True).then_inc(S["c_done"], 1)
                            if n:
                                add_state(t, n - 1)
                    if scan:
                        add_state(t, STATES - 1)

                def add_state(t, n):
                    pe.wait_ge(S["seen_ready"], STATES * t + n + 1)
                    if n == 0:
                        pe.wait_ge(S["y_ready"], t + 2)
                    nc.tensor.matmul(sum_ps[:, :], ident, seen[n % 2][:, :], start=n == 0,
                                     stop=n == STATES - 1).then_inc(S["summed"], 1)

                windows(pe, window)

            @block.scalar
            def _(act):
                act.wait_ge(S["params"], 16 * PARAMS)
                keeps = [w2_t[:, :], wo_t[:, :], in_u_t[:, :], in_z_t[:, :], out_t[:, :]] \
                    + [tap_t[:, k, :] for k in range(TAPS * TAPS)] + [xp_t[:, :], d_t[:, :]]
                for k, dst in enumerate(keeps):
                    act.wait_ge(S["w_turned"], k + 1)
                    nc.scalar.activation(dst, conv_ps[:, 0:dst.shape[-1]], ACT.Copy).then_inc(S["w_kept"], 1)
                act.preload_act_table_set("natural_log_exp_and_others")
                act.wait_ge(S["a_held"], 3)
                nc.scalar.activation(a_exp[:, :], a_low[:, :], ACT.Exp).then_inc(S["a_made"], 1)
                act.wait_ge(S["a_made"], 1)
                nc.scalar.activation(a_neg[:, :], a_exp[:, :], ACT.Copy, scale=-1.0).then_inc(S["a_made"], 1)
                act.wait_ge(S["a_made"], 2)
                act.wait_ge(S["ready"], 4)
                act.sem_inc(S["w2_ready"], AHEAD)
                act.sem_inc(S["decayed"], AHEAD)
                act.sem_inc(S["over_ready"], AHEAD)
                act.sem_inc(S["z_ready"], AHEAD)

                def window(t, u, half_t, front, scan, back):
                    f, v, b = t + 1, 1 - u, t - 1
                    for n in range(STATES):
                        q = STATES * t + n
                        if scan:
                            act.wait_ge(S["capped"], q + 1)
                            act.wait_ge(S["scanned"], q + 1)
                            nc.scalar.activation(decay[n % 2][:, :], capped[n % 2][:, :], ACT.Exp,
                                                 bias=a_gone[:, n:n + 1], scale=a_neg[:, n:n + 1]).then_inc(S["decayed"], 1)
                        if n == 3 and (front or scan):
                            act.preload_act_table_set("silu_and_others")
                            if front:
                                act.wait_ge(S["conv_done"], f + 1)
                                nc.scalar.activation(conv[:, :], conv_ps[:, :], ACT.Silu).then_inc(S["conv_ready"], 1)
                            if scan:
                                act.wait_ge(S["fused_ready"], t + 1)
                                act.wait_ge(S["w2_done"], t + 1 + AHEAD)
                                nc.scalar.activation(w2_act[u][:, :], w2_ps[:, :], ACT.Silu).then_inc(S["w2_ready"], 1)
                            act.preload_act_table_set("natural_log_exp_and_others")
                        if n == 4 and front:
                            act.wait_ge(S["u_done"], f + 1)
                            nc.scalar.activation(raw[v][:, 2:2 + TILE], u_ps[:, :], ACT.Copy).then_inc(S["raw_ready"], 1)
                            nc.scalar.activation(raw[1 - v][:, 0:2], u_ps[:, TILE - 2:TILE], ACT.Copy)
                            act.wait_ge(S["raw_ready"], f + 1)
                            nc.scalar.activation(bent[:, :], raw[v][:, 0:TILE], ACT.Identity, bias=cb[:, :],
                                                 scale=cw[:, 0:1]).then_inc(S["bent0"], 1)
                        if n == 5 and back:
                            act.wait_ge(S["shift_ready"], b + 1)
                            for k in range(TB):
                                last = nc.scalar.activation(normed[:, k, :], tail_ps[:, k * C:(k + 1) * C],
                                                            ACT.Identity, bias=shift[:, k:k + 1],
                                                            scale=scale[:, k:k + 1])
                            last.then_inc(S["normed_ready"], 1)
                        if n == 5 and front:
                            act.preload_act_table_set("silu_and_others")
                            act.wait_ge(S["y_ready"], f + 1)
                            act.wait_ge(S["bent2"], f + 1)
                            nc.scalar.activation(u_act[v][:, :], bent[:, :], ACT.Silu).then_inc(S["u_ready"], 1)
                            act.wait_ge(S["yz_ready"], f + 1)
                            act.wait_ge(S["z_done"], f + 1)
                            nc.scalar.activation(z_act[v][:, :], z_ps[:, :], ACT.Silu).then_inc(S["z_ready"], 1)
                            act.preload_act_table_set("natural_log_exp_and_others")
                        if n == 6 and back:
                            act.wait_ge(S["fused_ready"], b + 2)
                            act.wait_ge(S["n_turned"], b + 1)
                            nc.scalar.activation(affine[:, :], tail_ps[:, :], ACT.Identity, bias=beta[:, :],
                                                 scale=gamma[:, :]).then_inc(S["affine_ready"], 1)
                        if n == 6 and front:
                            act.wait_ge(S["x_done"], f + 1)
                            nc.scalar.activation(parts[v][:, :], x_ps[0:3 * SLOT, :], ACT.Copy
                                                 ).then_inc(S["high_ready"], 1)
                            act.wait_ge(S["d_done"], f + 1)
                            nc.scalar.activation(size[:, :], d_ps[:, :], ACT.Abs, bias=dtb[:, :]).then_inc(S["size_ready"], 1)
                            nc.scalar.activation(over[:, :], d_ps[:, :], ACT.Relu, bias=dtb[:, :]).then_inc(S["over_ready"], 1)
                            act.wait_ge(S["size_ready"], f + 1)
                            nc.scalar.activation(ex[:, :], size[:, :], ACT.Exp, scale=-1.0).then_inc(S["ex_ready"], 1)
                            act.wait_ge(S["ex_ready"], f + 1)
                            nc.scalar.activation(logs[:, :], ex[:, :], ACT.Ln, bias=one[:, :]).then_inc(S["log_ready"], 1)

                windows(act, window)

            @block.vector
            def _(dve):
                for w in (w1n, w2n, won):
                    nc.vector.memset(w[:, :], 0.0).then_inc(S["blank"], 1)
                nc.vector.memset(xpn[:, :], 0.0).then_inc(S["blank"], 1)
                for u in range(2):
                    nc.vector.memset(win[u][:, :, 0:1], 0.0)
                    nc.vector.memset(win[u][:, :, PAD - 1:PAD], 0.0)
                nc.vector.memset(raw[0][:, 0:2], 0.0).then_inc(S["ready"], 1)
                nc.vector.memset(one[:, :], 1.0).then_inc(S["ready"], 1)
                for n in range(STATES):
                    nc.vector.memset(state[1][n][:, TILE - 1:TILE], 0.0)
                nc.vector.memset(half[:, :], -0.5).then_inc(S["ready"], 2)
                dve.wait_ge(S["params"], 16 * PARAMS)
                nc.vector.tensor_scalar(a_low[:, :], a_log[:, :], BELOW, None, ALU.min
                                        ).then_inc(S["a_held"], 1)
                nc.vector.tensor_scalar(a_gone[:, :], a_log[:, :], OVERFLOW, -1000.0, ALU.is_ge, ALU.mult
                                        ).then_inc(S["a_held"], 2)
                for k in range(TAPS * TAPS):
                    last = nc.vector.tensor_scalar(tapn[:, k, :], w1n[:, :], dw[:, k:k + 1], None, ALU.mult)
                last.then_inc(S["scaled_taps"], 1)
                dve.wait_ge(S["a_made"], 1)
                nc.vector.tensor_scalar(a_mil[:, :], a_exp[:, :], 1e-34, 1e-3, ALU.max, ALU.mult
                                        ).then_inc(S["a_held"], 1)
                dve.wait_ge(S["a_held"], 4)
                nc.vector.reciprocal(limit[:, :], a_mil[:, :]).then_inc(S["a_held"], 1)
                dve.wait_ge(S["ready"], 4)
                dve.sem_inc(S["remain_ready"], AHEAD)
                dve.sem_inc(S["y_ready"], AHEAD)
                dve.sem_inc(S["x3_ready"], AHEAD)
                dve.sem_inc(S["scanned"], AHEAD)

                def window(t, u, half_t, front, scan, back):
                    f, v, b = t + 1, 1 - u, t - 1
                    for n in range(STATES):
                        q = STATES * t + n
                        if scan:
                            if n == 0:
                                dve.wait_ge(S["du_ready"], t + 1)
                            dve.wait_ge(S["b_done"], q + 1)
                            nc.vector.tensor_tensor(drive[n % 2][:, :], du[u][:, :], b_ps[:, :],
                                                    ALU.mult).then_inc(S["driven"], 1)
                            hold(dve, S["decayed"], q + 1 + AHEAD, S["passed"])
                            dve.wait_ge(S["driven"], q + 1)
                            nc.vector.tensor_tensor_scan(state[u][n][:, :], decay[n % 2][:, :], drive[n % 2][:, :],
                                                         initial=state[1 - u][n][:, TILE - 1:TILE],
                                                         op0=ALU.mult, op1=ALU.add).then_inc(S["scanned"], 1)
                        if n == 0 and back:
                            dve.wait_ge(S["summed"], STATES * t + AHEAD)
                            nc.vector.scalar_tensor_tensor(y[1 - u][:, :], u_act[1 - u][:, :], dpar[:, :], sum_ps[:, :],
                                                           ALU.mult, ALU.add).then_inc(S["y_ready"], 1)
                        if n == 3 and back:
                            dve.wait_ge(S["out_done"], b + 1)
                            for k in range(TB):
                                last = nc.vector.bn_stats(stats[:, k, :], tail_ps[:, k * C:(k + 1) * C])
                            last.then_inc(S["tail_step"], 1)
                            hold(dve, S["tail_step"], 2 * b + 1, S["passed"])
                            for k in range(TB):
                                last = nc.vector.bn_aggr(mv[:, k, :], stats[:, k, :])
                            last.then_inc(S["tail_step"], 1)
                            dve.wait_ge(S["tail_step"], 2 * b + 2)
                            nc.vector.tensor_scalar(vv[:, :], mv[:, :, 1], 1.0, 1e-5, ALU.mult,
                                                    ALU.add).then_inc(S["vv_ready"], 1)
                        if n == 4 and back:
                            dve.wait_ge(S["scale_ready"], b + 1)
                            nc.vector.scalar_tensor_tensor(shift[:, :], mv[:, :, 0], -1.0, scale[:, :], ALU.mult,
                                                           ALU.mult).then_inc(S["shift_ready"], 1)
                        if scan:
                            hold(dve, S["summed"], q + 1, S["passed"])
                            hold(dve, S["scanned"], q + 1 + AHEAD, S["passed"])
                            dve.wait_ge(S["c_done"], q + 1)
                            nc.vector.tensor_tensor(seen[n % 2][:, :], state[u][n][:, :], c_ps[:, :],
                                                    ALU.mult).then_inc(S["seen_ready"], 1)
                        if n == 4 and front:
                            dve.wait_ge(S["bent0"], f + 1)
                            nc.vector.scalar_tensor_tensor(bent[:, :], raw[v][:, 1:1 + TILE], cw[:, 1:2], bent[:, :],
                                                           ALU.mult, ALU.add).then_inc(S["bent1"], 1)
                            dve.wait_ge(S["bent1"], f + 1)
                            nc.vector.scalar_tensor_tensor(bent[:, :], raw[v][:, 2:2 + TILE], cw[:, 2:3], bent[:, :],
                                                           ALU.mult, ALU.add).then_inc(S["bent2"], 1)
                        if n == 7 and front:
                            dve.wait_ge(S["high_ready"], f + 1)
                            nc.vector.tensor_tensor(remain[:, :], x_ps[0:3 * SLOT, :], parts[v][:, :],
                                                    ALU.subtract).then_inc(S["remain_ready"], 1)
                            dve.wait_ge(S["ex_ready"], f + 1)
                            nc.vector.tensor_scalar(rest[:, :], ex[:, :], 1.0, -1.0, ALU.add,
                                                    ALU.add).then_inc(S["back_ready"], 1)
                        if n == 7 and back:
                            hold(dve, stored[1 - u], 16 * (half_t if u == 1 else half_t - 1), S["passed"])
                            hold(dve, x2_loaded[1 - u], 16 * (half_t if u == 1 else half_t - 1) + 16, S["passed"])
                            dve.wait_ge(S["o_done"], b + 1)
                            nc.vector.tensor_tensor(x3[1 - u][:, :, :], x2[1 - u][:, :, :],
                                                    tail_ps[:, :].rearrange("p (b c) -> p b c", b=TB),
                                                    ALU.add).then_inc(S["x3_ready"], 1)

                windows(dve, window)

            @block.gpsimd
            def _(pool):
                pool.memset(select[:, :, :], 0.0).then_inc(S["selector"], 1)
                for k in range(3):
                    pool.wait_ge(S["selector"], k + 1)
                    pool.affine_select(out=select[:, :, :], in_=select[:, :, :], compare_op=ALU.not_equal,
                                       fill=1.0, base=-k * SLOT, pattern=[[-1, 2 * STATES], [0, P]],
                                       channel_multiplier=1).then_inc(S["selector"], 1)
                pool.wait_ge(S["ready"], 4)
                pool.wait_ge(S["a_held"], 5)
                pool.sem_inc(S["yz_ready"], AHEAD)
                pool.sem_inc(S["fused_ready"], AHEAD)

                def window(t, u, half_t, front, scan, back):
                    f, v, b = t + 1, 1 - u, t - 1

                    def cap(states):
                        for n in states if scan else ():
                            hold(pool, S["decayed"], STATES * t + n + 1, S["passed"])
                            nc.gpsimd.tensor_scalar(capped[n % 2][:, :], delta[u][:, :], limit[:, n:n + 1], 0.0,
                                                    ALU.min, ALU.max).then_inc(S["capped"], 1)

                    cap(range(0, 2))
                    if back:
                        pool.wait_ge(S["y_ready"], b + 1 + AHEAD)
                        nc.gpsimd.tensor_tensor(yz[1 - u][:, :], y[1 - u][:, :], z_act[1 - u][:, :],
                                                ALU.mult).then_inc(S["yz_ready"], 1)
                    cap(range(2, 4))
                    if back:
                        pool.wait_ge(S["vv_ready"], b + 1)
                        nc.gpsimd.tensor_tensor(scale[:, :], vv[:, :], half[:, :], ALU.pow
                                                ).then_inc(S["scale_ready"], 1)
                    cap(range(4, 8))
                    if back:
                        hold(pool, S["w2_ready"], b + 1 + AHEAD, S["passed"])
                        pool.wait_ge(S["affine_ready"], b + 1)
                        nc.gpsimd.tensor_tensor(fused[:, :], affine[:, :], w2_act[1 - u][:, :],
                                                ALU.mult).then_inc(S["fused_ready"], 1)
                    if front:
                        if scan:
                            hold(pool, S["capped"], STATES * t + STATES, S["passed"])
                        lo, mid = slice(2 * SLOT, 3 * SLOT), slice(SLOT, 2 * SLOT)
                        if back:
                            hold(pool, S["scale_ready"], b + 1, S["passed"])
                            hold(pool, S["fused_ready"], b + 1 + AHEAD, S["passed"])
                        elif scan:
                            hold(pool, S["du_ready"], f, S["passed"])
                        hold(pool, S["remain_ready"], f + 1 + AHEAD, S["passed"])
                        nc.gpsimd.tensor_copy(parts[v][mid, :], remain[mid, :]).then_inc(S["mid_ready"], 1)
                        hold(pool, S["mid_ready"], f + 1, S["passed"])
                        nc.gpsimd.tensor_copy(middle[lo, :], remain[lo, :]).then_inc(S["middle_ready"], 1)
                        pool.wait_ge(S["middle_ready"], f + 1)
                        nc.gpsimd.tensor_tensor(parts[v][lo, :], remain[lo, :], middle[lo, :],
                                                ALU.subtract).then_inc(S["parts_ready"], 1)
                        hold(pool, S["parts_ready"], f + 1, S["passed"])
                        pool.wait_ge(S["back_ready"], f + 1)
                        nc.gpsimd.tensor_tensor(rest[:, :], ex[:, :], rest[:, :],
                                                ALU.subtract).then_inc(S["rest_ready"], 1)
                        hold(pool, S["log_ready"], f + 1, S["passed"])
                        pool.wait_ge(S["rest_ready"], f + 1)
                        nc.gpsimd.tensor_tensor(rest[:, :], rest[:, :], logs[:, :], ALU.add).then_inc(S["sum1"], 1)
                        hold(pool, S["over_ready"], f + 1 + AHEAD, S["passed"])
                        pool.wait_ge(S["sum1"], f + 1)
                        nc.gpsimd.tensor_tensor(delta[v][:, :], rest[:, :], over[:, :],
                                                ALU.add).then_inc(S["delta_ready"], 1)
                        pool.wait_ge(S["delta_ready"], f + 1)
                        nc.gpsimd.tensor_tensor(du[v][:, :], delta[v][:, :], u_act[v][:, :],
                                                ALU.mult).then_inc(S["du_ready"], 1)

                windows(pool, window)
        s.clear()


def phase_experts(nc, io, keep):
    E = 8
    EB = BANK // C
    x3_v = io["x3"].rearrange("(t b p) c -> t p b c", b=TB, p=P)
    out_v = io["out"].rearrange("a r w c -> (a r w) c").rearrange("(t b p) c -> t p b c", b=TB, p=P)
    with ExitStack() as ctx:
        s = Space(nc, ctx, "moe")

        def two(name, shape, dt=F32):
            return [s.sb(f"{name}{u}", shape, dt) for u in range(2)]

        rw, ew, eb = s.sb("rw", [P, E]), s.sb("ew", [P, E, C]), s.sb("eb", [E, C])
        rb, count, half = s.sb("rb", [P, TB, E]), s.sb("count", [P, TB, E]), s.sb("half", [P, TB])
        x3, out = two("x3", [P, TB, C]), two("out", [P, TB, C])
        even, odd = two("even", [P, TB, C]), two("odd", [P, TB, C])
        stats, mv, vv, scale, shift = (s.sb("stats", [P, TB, 6]), s.sb("mv", [P, TB, 2]), s.sb("vv", [P, TB]),
                                       s.sb("scale", [P, TB]), s.sb("shift", [P, TB]))
        h, hT, weight = s.sb("h", [P, TB, C]), two("hT", [P, TILE]), two("weight", [P, TB, E])
        logit, best, place = s.sb("logit", [P, TB, E]), s.sb("best", [P, TB, E]), s.sb("place", [P, TB, E], U32)
        placef, lead, ex, total, first, second = (s.sb("placef", [P, TB, 2]), *(s.sb(n, [P, TB]) for n in (
            "lead", "ex", "total", "first", "second")))
        hit0, hit1 = s.sb("hit0", [P, TB, E]), s.sb("hit1", [P, TB, E])
        wT = s.sb("wT", [E, TILE])
        e_ps = [s.bank(f"e{u}", 2) for u in range(2)]
        h_ps, l_ps, wT_ps, bias_ps = (s.bank(n) for n in ("h", "l", "wT", "bias"))

        S = {n: s.sem(n) for n in (
            "params ready passed step vv_ready scale_ready shift_ready h_ready h_turned hT_ready l_done logit_ready "
            "best_ready place_ready lead_ready ex_ready total_ready first_ready second_ready placed hits weight_ready "
            "w_turned wT_ready bias_done e_done mixed biased out_ready").split()}
        x3_loaded = [s.sem(f"x3_loaded{u}") for u in range(2)]
        stored = [s.sem(f"stored{u}") for u in range(2)]
        PARAMS = 3 + TB
        STEPS = TB * E

        def windows(eng, window):
            window(-1, 1, -1, True, False)
            with eng.Fori(0, TILES // 2 - 1) as i:
                window(2 * i, 0, i, True, True)
                window(2 * i + 1, 1, i, True, True)
            window(TILES - 2, 0, TILES // 2 - 1, True, True)
            window(TILES - 1, 1, TILES // 2 - 1, False, True)

        with nc.Block() as block:
            @block.sync
            def _(sp):
                sp.dma_start(rw[:, :], io["L1_ffn_router_w"]).then_inc(S["params"], 16)
                sp.dma_start(ew[:, :, :], io["L1_ffn_expert_w"].rearrange("e d c -> d e c")).then_inc(S["params"], 16)
                sp.dma_start(eb[:, :], io["L1_ffn_expert_b"]).then_inc(S["params"], 16)
                for k in range(TB):
                    sp.dma_start(rb[:, k, :], io["L1_ffn_router_b"].partition_broadcast(P)).then_inc(S["params"], 16)

                def window(t, u, half_t, front, back):
                    if front:
                        f, v = t + 1, 1 - u
                        if back:
                            sp.wait_ge(S["mixed"], STEPS * t + 2 * E)
                        sp.dma_start(x3[v][:, :, :], x3_v[f]).then_inc(x3_loaded[v], 16)
                    if back:
                        sp.wait_ge(S["out_ready"], t + 1 + AHEAD)
                        sp.dma_start(out_v[t], out[u][:, :, :]).then_inc(stored[u], 16)

                windows(sp, window)
                for u in range(2):
                    sp.wait_ge(stored[u], 16 * (TILES // 2))

            @block.tensor
            def _(pe):
                ident = keep["ident"][:, :]
                pe.wait_ge(S["params"], 16 * PARAMS)

                def window(t, u, half_t, front, back):
                    f, v = t + 1, 1 - u

                    def experts(k):
                        pe.wait_ge(S["mixed"], STEPS * t + E * k + E)
                        for j in range(E // EB):
                            last = nc.tensor.matmul(
                                e_ps[k % 2][:, j * BANK:(j + 1) * BANK], hT[u][:, k * P:(k + 1) * P],
                                ew[:, j * EB:(j + 1) * EB, :].rearrange("p e c -> p (e c)"), start=True, stop=True)
                        last.then_inc(S["e_done"], 1)

                    if back:
                        pe.wait_ge(S["hT_ready"], t + 1)
                        experts(0)
                        pe.wait_ge(S["weight_ready"], t + 1)
                        for k in range(TB):
                            last = nc.tensor.transpose(wT_ps[0:E, k * P:(k + 1) * P], weight[u][:, k, :], ident)
                        last.then_inc(S["w_turned"], 1)
                        experts(1)
                        pe.wait_ge(S["wT_ready"], t + 1)
                        pe.wait_ge(S["biased"], t)
                        for k in range(TB):
                            last = nc.tensor.matmul(bias_ps[:, k * C:(k + 1) * C], wT[:, k * P:(k + 1) * P], eb[:, :],
                                                    start=True, stop=True)
                        last.then_inc(S["bias_done"], 1)
                        experts(2)
                    if front:
                        pe.wait_ge(S["h_ready"], f + 1)
                        for k in range(TB):
                            last = nc.tensor.transpose(h_ps[:, k * P:(k + 1) * P], h[:, k, :], ident)
                        last.then_inc(S["h_turned"], 1)
                    if back:
                        experts(3)
                    if front:
                        pe.wait_ge(S["hT_ready"], f + 1)
                        for k in range(TB):
                            last = nc.tensor.matmul(l_ps[:, k * E:(k + 1) * E], hT[v][:, k * P:(k + 1) * P], rw[:, :],
                                                    start=True, stop=True)
                        last.then_inc(S["l_done"], 1)

                windows(pe, window)

            @block.scalar
            def _(act):
                act.preload_act_table_set("exp_and_others")

                def window(t, u, half_t, front, back):
                    f, v = t + 1, 1 - u
                    if back:
                        act.wait_ge(S["w_turned"], t + 1)
                        nc.scalar.activation(wT[:, :], wT_ps[0:E, :], ACT.Copy).then_inc(S["wT_ready"], 1)
                    if front:
                        act.wait_ge(S["h_turned"], f + 1)
                        nc.scalar.activation(hT[v][:, :], h_ps[:, :], ACT.Copy).then_inc(S["hT_ready"], 1)
                        act.wait_ge(S["lead_ready"], f + 1)
                        nc.scalar.activation(ex[:, :], lead[:, :], ACT.Exp).then_inc(S["ex_ready"], 1)

                windows(act, window)

            @block.vector
            def _(dve):
                for e in range(E):
                    nc.vector.memset(count[:, :, e:e + 1], float(e)).then_inc(S["ready"], 1)
                nc.vector.memset(half[:, :], -0.5).then_inc(S["ready"], 1)
                dve.wait_ge(S["ready"], E + 1)
                dve.wait_ge(S["params"], 16 * PARAMS)
                dve.sem_inc(S["mixed"], 2 * E)

                def window(t, u, half_t, front, back):
                    f, v = t + 1, 1 - u

                    def mix(k):
                        hold(dve, S["e_done"], TB * t + k + 1, S["passed"])
                        for e in range(E):
                            p = e_ps[k % 2][:, e * C:(e + 1) * C]
                            w = weight[u][:, k, e:e + 1]
                            if e >= 2:
                                dve.wait_ge(S["mixed"], STEPS * t + E * k + e - 1 + 2 * E)
                            if e == 1:
                                last = nc.vector.tensor_scalar(odd[u][:, k, :], p, w, None, ALU.mult)
                            else:
                                side = (even, odd)[e % 2][u][:, k, :]
                                last = nc.vector.scalar_tensor_tensor(side, p, w, x3[u][:, k, :] if e == 0 else side,
                                                                      ALU.mult, ALU.add)
                            last.then_inc(S["mixed"], 1)

                    if front:
                        dve.wait_ge(x3_loaded[v], 16 * (half_t + (1 if u == 1 else 0)) + 16)
                        for k in range(TB):
                            last = nc.vector.bn_stats(stats[:, k, :], x3[v][:, k, :])
                        last.then_inc(S["step"], 1)
                        hold(dve, S["step"], 2 * f + 1, S["passed"])
                        for k in range(TB):
                            last = nc.vector.bn_aggr(mv[:, k, :], stats[:, k, :])
                        last.then_inc(S["step"], 1)
                        dve.wait_ge(S["step"], 2 * f + 2)
                        nc.vector.tensor_scalar(vv[:, :], mv[:, :, 1], 1.0, 1e-5, ALU.mult,
                                                ALU.add).then_inc(S["vv_ready"], 1)
                    if back:
                        hold(dve, S["out_ready"], t + 1, S["passed"])
                        mix(0)
                    if front:
                        dve.wait_ge(S["scale_ready"], f + 1)
                        nc.vector.scalar_tensor_tensor(shift[:, :], mv[:, :, 0], -1.0, scale[:, :], ALU.mult,
                                                       ALU.mult).then_inc(S["shift_ready"], 1)
                    if back:
                        mix(1)
                        mix(2)
                        mix(3)
                        hold(dve, S["bias_done"], t + 1, S["passed"])
                        dve.wait_ge(S["mixed"], STEPS * (t + 1) + 2 * E)
                        nc.vector.tensor_tensor(even[u][:, :, :], even[u][:, :, :],
                                                bias_ps[:, :].rearrange("p (b c) -> p b c", b=TB),
                                                ALU.add).then_inc(S["biased"], 1)
                    if front:
                        dve.wait_ge(S["l_done"], f + 1)
                        nc.vector.tensor_tensor(logit[:, :, :], l_ps[:, 0:TB * E].rearrange("p (b e) -> p b e", b=TB),
                                                rb[:, :, :], ALU.add).then_inc(S["logit_ready"], 1)
                        hold(dve, S["logit_ready"], f + 1, S["passed"])
                        for k in range(TB):
                            last = nc.vector.max(best[:, k, :], logit[:, k, :])
                        last.then_inc(S["best_ready"], 1)
                        dve.wait_ge(S["best_ready"], f + 1)
                        nc.vector.tensor_tensor(lead[:, :], best[:, :, 1], best[:, :, 0],
                                                ALU.subtract).then_inc(S["lead_ready"], 1)
                        for k in range(TB):
                            last = nc.vector.max_index(place[:, k, :], best[:, k, :], logit[:, k, :])
                        last.then_inc(S["place_ready"], 1)
                        dve.wait_ge(S["place_ready"], f + 1)
                        nc.vector.tensor_copy(placef[:, :, :], place[:, :, 0:2]).then_inc(S["placed"], 1)
                        dve.wait_ge(S["ex_ready"], f + 1)
                        nc.vector.tensor_scalar(total[:, :], ex[:, :], 1.0, None, ALU.add).then_inc(S["total_ready"], 1)
                        dve.wait_ge(S["total_ready"], f + 1)
                        nc.vector.reciprocal(first[:, :], total[:, :]).then_inc(S["first_ready"], 1)
                        dve.wait_ge(S["first_ready"], f + 1)
                        nc.vector.tensor_tensor(second[:, :], ex[:, :], first[:, :], ALU.mult
                                                ).then_inc(S["second_ready"], 1)
                        dve.wait_ge(S["placed"], f + 1)
                        for j, hit in enumerate((hit0, hit1)):
                            nc.vector.tensor_tensor(hit[:, :, :], count[:, :, :],
                                                    placef[:, :, j].unsqueeze(2).broadcast_to([P, TB, E]),
                                                    ALU.is_equal).then_inc(S["hits"], 1)
                        dve.wait_ge(S["second_ready"], f + 1)
                        for j, (hit, w) in enumerate(((hit0, first), (hit1, second))):
                            dve.wait_ge(S["hits"], 4 * f + 1 + j)
                            nc.vector.tensor_tensor(hit[:, :, :], hit[:, :, :],
                                                    w[:, :].unsqueeze(2).broadcast_to([P, TB, E]),
                                                    ALU.mult).then_inc(S["hits"], 1)
                        dve.wait_ge(S["hits"], 4 * f + 4)
                        nc.vector.tensor_tensor(weight[v][:, :, :], hit0[:, :, :], hit1[:, :, :],
                                                ALU.add).then_inc(S["weight_ready"], 1)
                        dve.wait_ge(S["weight_ready"], f + 1)

                windows(dve, window)

            @block.gpsimd
            def _(pool):
                pool.wait_ge(S["ready"], E + 1)
                pool.sem_inc(S["out_ready"], AHEAD)

                def window(t, u, half_t, front, back):
                    f, v = t + 1, 1 - u
                    if front:
                        pool.wait_ge(S["vv_ready"], f + 1)
                        nc.gpsimd.tensor_tensor(scale[:, :], vv[:, :], half[:, :], ALU.pow
                                                ).then_inc(S["scale_ready"], 1)
                        hold(pool, S["shift_ready"], f + 1, S["passed"])
                        for k in range(TB):
                            last = nc.gpsimd.tensor_scalar(h[:, k, :], x3[v][:, k, :], scale[:, k:k + 1],
                                                           shift[:, k:k + 1], ALU.mult, ALU.add)
                        last.then_inc(S["h_ready"], 1)
                    if back:
                        hold(pool, stored[u], 16 * half_t, S["passed"])
                        pool.wait_ge(S["biased"], t + 1)
                        nc.gpsimd.tensor_tensor(out[u][:, :, :], even[u][:, :, :], odd[u][:, :, :],
                                                ALU.add).then_inc(S["out_ready"], 1)

                windows(pool, window)
        s.clear()


def metaformer(nc, io):
    io["x1"] = nc.dram_tensor("x1_map", (TOKENS, C), F32).ap()
    io["wx"] = nc.dram_tensor("wx_map", (C, TOKENS), F32).ap()
    io["yT"] = nc.dram_tensor("y_map", (C, TOKENS), F32).ap()
    io["x2"] = nc.dram_tensor("x2_map", (TOKENS, C), F32).ap()
    io["hT"] = nc.dram_tensor("h_map", (C, SIDE + 2, SIDE), F32).ap()
    io["x3"] = nc.dram_tensor("x3_map", (TOKENS, C), F32).ap()
    with ExitStack() as ctx:
        s = Space(nc, ctx, "keep")
        keep = {"ident": s.sb("ident", [P, P]), "bn_scale": s.sb("bn_scale", [P, 1]),
                "bn_shift": s.sb("bn_shift", [P, 1])}
        with ExitStack() as attention:
            a = Space(nc, attention, "keep")
            keep["bias"] = a.sb("bias", [P, HEADS, RB, SIDE])
            keep["scale"] = a.sb("scale", [P, TOKENS // P])
            keep["shift"] = a.sb("shift", [P, TOKENS // P])
            phase_bias(nc, io, keep)
            phase_attention(nc, io, keep)
        phase_batchnorm(nc, io, keep)
        phase_recurrence(nc, io, keep)
        phase_join(nc, io, keep)
        phase_mamba(nc, io, keep)
        phase_experts(nc, io, keep)


def kernel(**inputs):
    import numpy as _np
    import concourse.bacc as _bacc
    from concourse import mybir as _mybir
    from concourse.bass_utils import run_bass_kernel_spmd as _run

    nc = _bacc.Bacc("TRN2", target_bir_lowering=False, num_devices=1)
    arrays, io = {}, {}
    for name, value in inputs.items():
        a = _np.ascontiguousarray(value)
        arrays[f"in_{name}_dram"] = a
        io[name] = nc.dram_tensor(f"in_{name}_dram", a.shape, _mybir.dt.from_np(a.dtype), kind="ExternalInput").ap()
    io["out"] = nc.dram_tensor("out_dram", (1, SIDE, SIDE, C), _mybir.dt.float32, kind="ExternalOutput").ap()
    metaformer(nc, io)
    r = _run(nc, [arrays], core_ids=[0])
    return r.results[0]["out_dram"]
```

```python
from contextlib import ExitStack

import concourse.bass as bass
from concourse import mybir

F32 = mybir.dt.float32
BF16 = mybir.dt.bfloat16
I32 = mybir.dt.int32
U32 = mybir.dt.uint32
ALU = mybir.AluOpType
ACT = mybir.ActivationFunctionType
AX = mybir.AxisListType

P = 128
C = 128
SIDE = 256
TOKENS = SIDE * SIDE
BANK = 512
HEADS = 4
HID = C // HEADS
AHEAD = 2
RB = SIDE // P


class Space:

    def __init__(self, nc, ctx, name):
        self.nc, self.ctx, self.name = nc, ctx, name
        self.sems = []

    def sb(self, name, shape, dt=F32):
        return self.ctx.enter_context(self.nc.sbuf_tensor(f"{self.name}_{name}", shape, dt))

    def bank(self, name, n=1):
        return self.ctx.enter_context(self.nc.psum_tensor(f"{self.name}_{name}_bank", [P, n * BANK], F32))

    def sem(self, name):
        self.sems.append(self.nc.alloc_semaphore(name=f"{self.name}_{name}"))
        return self.sems[-1]

    def clear(self):
        self.nc.clear_and_free_semaphores(self.sems)
        self.nc.all_engine_barrier()


def column(v):
    return v.rearrange("(p a) -> p a", a=1)


def hold(eng, sem, value, passed):
    eng.wait_ge(sem, value)
    eng.sem_inc(passed, 1)


def stages(eng, window, tiles, ahead, behind, start):
    rounds = (tiles - ahead - start) // 4
    for t in range(-ahead, start):
        window(t, t % 4, t // 4)
    with eng.Fori(0, rounds) as i:
        for k in range(start, start + 4):
            window(4 * i + k, k % 4, i + k // 4)
    for t in range(start + 4 * rounds, tiles + behind):
        window(t, t % 4, t // 4)


def is_tile(t, tiles, least=0):
    return not isinstance(t, int) or least <= t < tiles


def make_identity(pool, ident, zeroed, done):
    pool.memset(ident[:, :], 0.0).then_inc(zeroed, 1)
    pool.wait_ge(zeroed, 1)
    pool.affine_select(out=ident[:, :], in_=ident[:, :], compare_op=ALU.not_equal, fill=1.0,
                       base=0, pattern=[[-1, P]], channel_multiplier=1).then_inc(done, 1)


def phase_bias(nc, io, keep):
    ROWS = 4
    NB = ROWS * RB
    TILES = SIDE // ROWS
    HALF = NB // 2
    x_v = io["x"].rearrange("a (t r) (b p) c -> (a t) p (r b) c", r=ROWS, p=P)
    with ExitStack() as ctx:
        s = Space(nc, ctx, "bias")

        def two(name, shape):
            return [s.sb(f"{name}{u}", shape) for u in range(2)]

        x = [s.sb(f"x{n}", [P, NB, C]) for n in range(4)]
        h, stats, mv = two("h", [P, NB, C]), two("stats", [P, NB, 6]), two("mv", [P, NB, 2])
        vv, scale, shift = (two(n, [P, NB]) for n in ("vv", "scale", "shift"))
        xT = two("xT", [P, NB * P])
        half = s.sb("half", [P, NB])
        wb = s.sb("wb", [P, HEADS])
        g, b = s.sb("g", [P, 1]), s.sb("b", [P, 1])
        t_ps = [s.bank(f"t{u}", 2) for u in range(2)]
        b_ps = [s.bank(f"b{u}") for u in range(2)]

        params = s.sem("params")
        zeroed, ident_ready = s.sem("zeroed"), s.sem("ident_ready")
        x_loaded = [s.sem(f"x_loaded{n}") for n in range(4)]
        step, vv_ready, scale_ready, shift_ready = (s.sem(n) for n in ("step", "vv_ready", "scale_ready", "shift_ready"))
        low_ready, high_ready, kept, passed = (s.sem(n) for n in ("low_ready", "high_ready", "kept", "passed"))
        turned, xT_ready, b_ready, b_kept = (s.sem(n) for n in ("turned", "xT_ready", "b_ready", "b_kept"))

        def windows(eng, window):
            stages(eng, window, TILES, 3, 1, 3)

        with nc.Block() as block:
            @block.sync
            def _(sp):
                sp.dma_start(wb[:, :], io["L0_conv_Wb"]).then_inc(params, 16)
                sp.dma_start(g[:, :], column(io["L0_conv_ln_g"])).then_inc(params, 16)
                sp.dma_start(b[:, :], column(io["L0_conv_ln_b"])).then_inc(params, 16)

                def window(t, m, q):
                    if is_tile(t + 3, TILES):
                        n = (m + 3) % 4
                        if is_tile(t + 3, TILES, 4):
                            sp.wait_ge(low_ready, t)
                            sp.wait_ge(high_ready, t)
                        sp.dma_start(x[n][:, :, :], x_v[t + 3]).then_inc(x_loaded[n], 16)

                windows(sp, window)

            @block.vector
            def _(dve):
                def window(t, m, q):
                    if is_tile(t + 2, TILES):
                        e, o, v = t + 2, (m + 2) % 4, m % 2
                        dve.wait_ge(x_loaded[o], 16 * (q + (m + 2) // 4) + 16)
                        for k in range(NB):
                            last = nc.vector.bn_stats(stats[v][:, k, :], x[o][:, k, :])
                        last.then_inc(step, 1)
                    if is_tile(t + 1, TILES):
                        f, n, u = t + 1, (m + 1) % 4, (m + 1) % 2
                        if is_tile(f, TILES, 2):
                            dve.wait_ge(kept, f - 1)
                            dve.wait_ge(high_ready, f - 1)
                        dve.wait_ge(scale_ready, f + 1)
                        nc.vector.scalar_tensor_tensor(shift[u][:, :], mv[u][:, :, 0], -1.0, scale[u][:, :],
                                                       ALU.mult, ALU.mult).then_inc(shift_ready, 1)
                        if is_tile(f, TILES, 2):
                            hold(dve, turned, f - 1, passed)
                        dve.wait_ge(shift_ready, f + 1)
                        for k in range(HALF):
                            last = nc.vector.tensor_scalar(h[u][:, k, :], x[n][:, k, :], scale[u][:, k:k + 1],
                                                           shift[u][:, k:k + 1], ALU.mult, ALU.add)
                        last.then_inc(low_ready, 1)
                    if is_tile(t + 2, TILES):
                        hold(dve, step, 2 * e + 1, passed)
                        for k in range(NB):
                            last = nc.vector.bn_aggr(mv[v][:, k, :], stats[v][:, k, :])
                        last.then_inc(step, 1)
                        dve.wait_ge(step, 2 * e + 2)
                        nc.vector.tensor_scalar(vv[v][:, :], mv[v][:, :, 1], 1.0 + 1e-5, 1e-11,
                                                ALU.mult, ALU.add).then_inc(vv_ready, 1)

                windows(dve, window)

            @block.gpsimd
            def _(pool):
                make_identity(pool, keep["ident"], zeroed, ident_ready)
                pool.memset(half[:, :], -0.5).then_inc(zeroed, 1)
                pool.wait_ge(zeroed, 2)

                def window(t, m, q):
                    if is_tile(t + 1, TILES):
                        f, n, u = t + 1, (m + 1) % 4, (m + 1) % 2
                        hold(pool, shift_ready, f + 1, passed)
                        if is_tile(f, TILES, 2):
                            hold(pool, turned, f - 1, passed)
                        for k in range(HALF, NB):
                            last = nc.gpsimd.tensor_scalar(h[u][:, k, :], x[n][:, k, :], scale[u][:, k:k + 1],
                                                           shift[u][:, k:k + 1], ALU.mult, ALU.add)
                        last.then_inc(high_ready, 1)
                        nc.gpsimd.tensor_copy(keep["scale"][:, bass.ds(f * NB, NB)], scale[u][:, :])
                        nc.gpsimd.tensor_copy(keep["shift"][:, bass.ds(f * NB, NB)],
                                              shift[u][:, :]).then_inc(kept, 1)
                    if is_tile(t + 2, TILES):
                        e, v = t + 2, m % 2
                        if is_tile(e, TILES, 2):
                            hold(pool, kept, e - 1, passed)
                            hold(pool, low_ready, e - 1, passed)
                        pool.wait_ge(vv_ready, e + 1)
                        nc.gpsimd.tensor_tensor(scale[v][:, :], vv[v][:, :], half[:, :],
                                                ALU.pow).then_inc(scale_ready, 1)

                windows(pool, window)

            @block.tensor
            def _(pe):
                pe.wait_ge(ident_ready, 1)
                pe.wait_ge(params, 48)

                def window(t, m, q):
                    if is_tile(t, TILES):
                        u = m % 2
                        if is_tile(t, TILES, 2):
                            pe.wait_ge(xT_ready, 2 * t - 2)
                        pe.wait_ge(low_ready, t + 1)
                        pe.wait_ge(high_ready, t + 1)
                        for k in range(NB):
                            last = nc.tensor.transpose(t_ps[u][:, k * P:(k + 1) * P], h[u][:, k, :],
                                                       keep["ident"][:, :])
                        last.then_inc(turned, 1)
                    if is_tile(t - 1, TILES):
                        d, u = t - 1, (m - 1) % 2
                        if is_tile(d, TILES, 2):
                            pe.wait_ge(b_kept, d - 1)
                        pe.wait_ge(xT_ready, 2 * d + 2)
                        for k in range(NB):
                            last = nc.tensor.matmul(b_ps[u][:, k * HEADS:(k + 1) * HEADS],
                                                    xT[u][:, k * P:(k + 1) * P], wb[:, :],
                                                    start=True, stop=True)
                        last.then_inc(b_ready, 1)

                windows(pe, window)

            @block.scalar
            def _(act):
                act.preload_act_table_set("exp_and_others")
                act.wait_ge(params, 48)

                def window(t, m, q):
                    if is_tile(t, TILES):
                        u = m % 2
                        if is_tile(t, TILES, 2):
                            act.wait_ge(b_ready, t - 1)
                        act.wait_ge(turned, t + 1)
                        for k in range(2):
                            nc.scalar.activation(xT[u][:, k * BANK:(k + 1) * BANK],
                                                 t_ps[u][:, k * BANK:(k + 1) * BANK], ACT.Identity,
                                                 bias=b[:, :], scale=g[:, :]).then_inc(xT_ready, 1)
                    if is_tile(t - 1, TILES):
                        d, u = t - 1, (m - 1) % 2
                        act.wait_ge(b_ready, d + 1)
                        nc.scalar.activation(
                            keep["bias"][:, :, :, bass.ds(d * ROWS, ROWS)].rearrange("p n b r -> p r b n"),
                            b_ps[u][:, 0:NB * HEADS].rearrange("p (r b n) -> p r b n", r=ROWS, b=RB),
                            ACT.Copy, scale=-1.0).then_inc(b_kept, 1)

                windows(act, window)
        s.clear()


def phase_attention(nc, io, keep):
    PAIRS = SIDE // 2
    UNITS = 2 * HEADS
    NB = 2 * RB
    PARAMS = 5 + 3 + NB
    TURN, VALUE = 2, 3
    x_v = io["x"].rearrange("a (i r) (b p) c -> (a i) p (r b) c", r=2, p=P)
    x1_v = io["x1"].rearrange("(i b p) c -> i p b c", i=PAIRS, p=P)
    with ExitStack() as ctx:
        s = Space(nc, ctx, "attn")

        def two(name, shape):
            return [s.sb(f"{name}{u}", shape) for u in range(2)]

        wq, wk, wv, wg, wo = (s.sb(n, [P, C]) for n in ("wq", "wk", "wv", "wg", "wo"))
        g, b, bg, hbg = (s.sb(n, [P, 1]) for n in ("g", "b", "bg", "hbg"))
        bo = s.sb("bo", [P, NB, C])
        ln = two("ln", [P, 2 * NB])
        h, xT = s.sb("h", [P, NB, C]), s.sb("xT", [P, NB * P])
        x, xb, x1 = (two(n, [P, NB, C]) for n in ("x", "xb", "x1"))
        qT, kT, gate = (two(n, [P, NB * P]) for n in ("qT", "kT", "gate"))
        v = two("v", [P, NB, HEADS, HID + 1])
        biased, probs, probsT = (two(n, [P, RB, SIDE]) for n in ("biased", "probs", "probsT"))
        low = two("low", [P, RB])
        half_inv = two("half_inv", [P, RB * HEADS])
        o, oT = s.sb("o", [P, NB, HEADS, HID]), s.sb("oT", [P, NB * P])

        s_ps = [s.bank(f"s{k}") for k in range(2)]
        p_ps = [s.bank(f"p{k}") for k in range(2)]
        o_ps = [s.bank(f"o{k}") for k in range(2)]
        first_ps, second_ps = s.bank("first"), s.bank("second")
        x_ps = k_ps = oT_ps = y_ps = first_ps
        q_ps = v_ps = g_ps = second_ps

        def o_view(u):
            return o_ps[u][:, 0:RB * HEADS * (HID + 1)].rearrange("p (b n d) -> p b n d", b=RB, n=HEADS)

        params, hbg_ready, ones_ready = s.sem("params"), s.sem("hbg_ready"), s.sem("ones_ready")
        passed = s.sem("passed")
        x_loaded = [s.sem(f"x_loaded{u}") for u in range(2)]
        stored = [s.sem(f"stored{u}") for u in range(2)]
        ln_copied, h_ready, xb_ready = s.sem("ln_copied"), s.sem("h_ready"), s.sem("xb_ready")
        x_turned, xT_ready = s.sem("x_turned"), s.sem("xT_ready")
        q_done, k_done, v_done, g_done = (s.sem(n) for n in ("q_done", "k_done", "v_done", "g_done"))
        q_ready, k_ready, v_ready, g_ready = (s.sem(n) for n in ("q_ready", "k_ready", "v_ready", "g_ready"))
        scored, lowered, exped, turned = (s.sem(n) for n in ("scored", "lowered", "exped", "turned"))
        copied, valued = s.sem("copied"), s.sem("valued")
        inv_ready, o_turned, oT_ready = (s.sem(n) for n in ("inv_ready", "o_turned", "oT_ready"))
        o_ready = [s.sem(f"o_ready{u}") for u in range(2)]
        y_done, x1_ready = s.sem("y_done"), s.sem("x1_ready")

        def windows(eng, window):
            window(-2, 0, -1, True, False, False, False)
            window(-1, 1, -1, True, True, False, False)
            window(0, 0, 0, True, True, True, False)
            with eng.Fori(0, PAIRS // 2 - 2) as i:
                window(2 * i + 1, 1, i, True, True, True, True)
                window(2 * i + 2, 0, i + 1, True, True, True, True)
            last = PAIRS // 2 - 2
            window(PAIRS - 3, 1, last, True, True, True, True)
            window(PAIRS - 2, 0, last + 1, False, True, True, True)
            window(PAIRS - 1, 1, last + 1, False, False, True, True)
            window(PAIRS, 0, last + 2, False, False, False, True)

        with nc.Block() as block:
            @block.sync
            def _(sp):
                for w, name in ((wq, "Wq"), (wk, "Wk"), (wv, "Wv"), (wg, "Wg"), (wo, "Wo")):
                    sp.dma_start(w[:, :], io[f"L0_conv_{name}"]).then_inc(params, 16)
                for w, name in ((g, "ln_g"), (b, "ln_b"), (bg, "bg")):
                    sp.dma_start(w[:, :], column(io[f"L0_conv_{name}"])).then_inc(params, 16)
                for k in range(NB):
                    sp.dma_start(bo[:, k, :], io["L0_conv_bo"].partition_broadcast(P)).then_inc(params, 16)

                def window(i, e, half_i, load, prep, units, tail):
                    if load:
                        if units:
                            sp.wait_ge(xb_ready, i + 1)
                        sp.dma_start(x[e][:, :, :], x_v[i + 2]).then_inc(x_loaded[e], 16)
                    if tail:
                        sp.wait_ge(x1_ready, i + AHEAD)
                        sp.dma_start(x1_v[i - 1], x1[1 - e][:, :, :]).then_inc(stored[1 - e], 16)

                windows(sp, window)
                for e in range(2):
                    sp.wait_ge(stored[e], 16 * (PAIRS // 2))

            @block.gpsimd
            def _(pool):
                for e in range(2):
                    pool.memset(v[e][:, :, :, HID:HID + 1], 2.0).then_inc(ones_ready, 1)
                pool.wait_ge(params, 16 * PARAMS)

                def window(i, e, half_i, load, prep, units, tail):
                    if units:
                        pool.wait_ge(x1_ready, i + 1)
                        nc.gpsimd.tensor_tensor(xb[e][:, :, :], x[e][:, :, :], bo[:, :, :],
                                                ALU.add).then_inc(xb_ready, 1)
                    if load:
                        nc.gpsimd.tensor_copy(ln[e][:, 0:NB], keep["scale"][:, bass.ds((i + 2) * NB, NB)])
                        nc.gpsimd.tensor_copy(ln[e][:, NB:2 * NB],
                                              keep["shift"][:, bass.ds((i + 2) * NB, NB)]).then_inc(ln_copied, 1)
                        hold(pool, ln_copied, i + 3, passed)
                        hold(pool, x_loaded[e], 16 * half_i + 32, passed)
                        if prep:
                            hold(pool, x_turned, i + 2, passed)
                        for k in range(NB):
                            last = nc.gpsimd.tensor_scalar(h[:, k, :], x[e][:, k, :], ln[e][:, k:k + 1],
                                                           ln[e][:, NB + k:NB + k + 1], ALU.mult, ALU.add)
                        last.then_inc(h_ready, 1)

                windows(pool, window)

            @block.tensor
            def _(pe):
                pe.sem_inc(turned, AHEAD)
                pe.sem_inc(valued, AHEAD)
                pe.wait_ge(params, 16 * PARAMS)
                ident = keep["ident"][:, :]

                def score(i, e, k):
                    u, n = divmod(k, HEADS)
                    rows = slice(n * HID, (n + 1) * HID)
                    if k == 0:
                        pe.wait_ge(k_ready, i + 1)
                    pe.wait_ge(lowered, UNITS * i + k + 1)
                    for j in range(RB):
                        last = nc.tensor.matmul(s_ps[k % 2][:, j * SIDE:(j + 1) * SIDE],
                                                qT[e][rows, (u * RB + j) * P:(u * RB + j + 1) * P],
                                                kT[e][rows, u * SIDE:(u + 1) * SIDE], start=True, stop=True)
                    last.then_inc(scored, 1)

                def turn(i, k):
                    q = UNITS * i + k
                    pe.wait_ge(copied, q + 1)
                    pe.wait_ge(exped, q + 1 + AHEAD)
                    for j in range(RB):
                        for kb in range(RB):
                            last = nc.tensor.transpose(
                                p_ps[k % 2][:, kb * SIDE + j * P:kb * SIDE + (j + 1) * P],
                                probs[k % 2][:, j, kb * P:(kb + 1) * P], ident)
                    last.then_inc(turned, 1)

                def value(i, e, k):
                    u, n = divmod(k, HEADS)
                    if k == 0:
                        pe.wait_ge(v_ready, i + 1)
                    if n == 0:
                        pe.wait_ge(o_ready[u], i + AHEAD)
                    pe.wait_ge(copied, UNITS * i + k + 1 + AHEAD)
                    for j in range(RB):
                        for kb in range(RB):
                            last = nc.tensor.matmul(o_view(u)[:, j, n, :],
                                                    probsT[k % 2][:, kb, j * P:(j + 1) * P],
                                                    v[e][:, u * RB + kb, n, :], start=kb == 0, stop=kb == RB - 1)
                    last.then_inc(valued, 1)

                def window(i, e, half_i, load, prep, units, tail):
                    a, d = i + 1, i - 1
                    for k in range(UNITS):
                        if units:
                            score(i, e, k)
                        if tail if k < TURN else units:
                            turn(d if k < TURN else i, (k - TURN) % UNITS)
                        if tail if k < VALUE else units:
                            value(d if k < VALUE else i, 1 - e if k < VALUE else e, (k - VALUE) % UNITS)
                        if k == 1 and prep:
                            if units:
                                pe.wait_ge(x1_ready, a)
                            pe.wait_ge(h_ready, a + 1)
                            for m in range(NB):
                                last = nc.tensor.transpose(x_ps[:, m * P:(m + 1) * P], h[:, m, :], ident)
                            last.then_inc(x_turned, 1)
                        if k == 3 and prep:
                            if units:
                                pe.wait_ge(g_ready, a)
                            pe.wait_ge(xT_ready, a + 1)
                            nc.tensor.matmul(q_ps[:, :], wq[:, :], xT[:, :], start=True, stop=True
                                             ).then_inc(q_done, 1)
                        if k == 4 and prep:
                            nc.tensor.matmul(k_ps[:, :], wk[:, :], xT[:, :], start=True, stop=True
                                             ).then_inc(k_done, 1)
                            pe.wait_ge(q_ready, a + 1)
                            for m in range(NB):
                                last = nc.tensor.matmul(v_ps[:, m * C:(m + 1) * C], xT[:, m * P:(m + 1) * P],
                                                        wv[:, :], start=True, stop=True)
                            last.then_inc(v_done, 1)
                        if k == 5 and tail:
                            if prep:
                                pe.wait_ge(k_ready, a + 1)
                            pe.wait_ge(o_ready[0], d + 1 + AHEAD)
                            pe.wait_ge(o_ready[1], d + 1 + AHEAD)
                            for m in range(NB):
                                last = nc.tensor.transpose(oT_ps[:, m * P:(m + 1) * P],
                                                           o[:, m, :, :].rearrange("p n d -> p (n d)"), ident)
                            last.then_inc(o_turned, 1)
                        if k == 6 and prep:
                            pe.wait_ge(v_ready, a + 1)
                            nc.tensor.matmul(g_ps[:, :], wg[:, :], xT[:, :], start=True, stop=True
                                             ).then_inc(g_done, 1)
                        if k == 7 and tail:
                            pe.wait_ge(oT_ready, d + 1)
                            for m in range(NB):
                                last = nc.tensor.matmul(y_ps[:, m * C:(m + 1) * C], oT[:, m * P:(m + 1) * P],
                                                        wo[:, :], start=True, stop=True)
                            last.then_inc(y_done, 1)

                windows(pe, window)

            @block.scalar
            def _(act):
                act.preload_act_table_set("exp_and_others")
                act.wait_ge(params, 16 * PARAMS)
                nc.scalar.activation(hbg[:, :], bg[:, :], ACT.Copy, scale=0.5).then_inc(hbg_ready, 1)
                act.wait_ge(hbg_ready, 1)
                act.wait_ge(ones_ready, 2)
                act.sem_inc(exped, AHEAD)

                def window(i, e, half_i, load, prep, units, tail):
                    a, f = i + 1, 1 - e
                    for k in range(UNITS):
                        if k == 1 and prep:
                            act.wait_ge(x_turned, a + 1)
                            nc.scalar.activation(xT[:, :], x_ps[:, :], ACT.Identity, bias=b[:, :],
                                                 scale=g[:, :]).then_inc(xT_ready, 1)
                        if k == 3 and prep:
                            act.wait_ge(q_done, a + 1)
                            nc.scalar.activation(qT[f][:, :], q_ps[:, :], ACT.Copy, scale=-(HID ** -0.5)
                                                 ).then_inc(q_ready, 1)
                        if k == 4 and prep:
                            act.wait_ge(k_done, a + 1)
                            nc.scalar.activation(kT[f][:, :], k_ps[:, :], ACT.Copy).then_inc(k_ready, 1)
                            act.wait_ge(v_done, a + 1)
                            nc.scalar.activation(v[f][:, :, :, 0:HID],
                                                 v_ps[:, :].rearrange("p (b n d) -> p b n d", b=NB, n=HEADS),
                                                 ACT.Copy).then_inc(v_ready, 1)
                        if k == 6 and prep:
                            if tail:
                                act.wait_ge(oT_ready, i)
                            act.wait_ge(g_done, a + 1)
                            nc.scalar.activation(gate[f][:, :], g_ps[:, :], ACT.Tanh,
                                                 bias=hbg[:, :], scale=0.5).then_inc(g_ready, 1)
                        if units:
                            q = UNITS * i + k
                            act.wait_ge(turned, q + 1)
                            act.wait_ge(lowered, q + 1 + AHEAD)
                            for j in range(RB):
                                last = nc.scalar.activation(probs[k % 2][:, j, :], biased[k % 2][:, j, :],
                                                            ACT.Exp, bias=low[k % 2][:, j:j + 1], scale=-1.0)
                            last.then_inc(exped, 1)

                windows(act, window)

            @block.vector
            def _(dve):
                dve.sem_inc(lowered, AHEAD)
                dve.sem_inc(x1_ready, AHEAD)
                dve.sem_inc(copied, AHEAD)
                for u in range(2):
                    dve.sem_inc(o_ready[u], AHEAD)

                def lower(i, k):
                    q = UNITS * i + k
                    hold(dve, exped, q + 1, passed)
                    hold(dve, scored, q + 1, passed)
                    for j in range(RB):
                        last = nc.vector.tensor_tensor_reduce(
                            out=biased[k % 2][:, j, :], in0=s_ps[k % 2][:, j * SIDE:(j + 1) * SIDE],
                            in1=keep["bias"][:, k % HEADS, j, :], scale=1.0, scalar=3.4e38,
                            op0=ALU.add, op1=ALU.min, accum_out=low[k % 2][:, j:j + 1])
                    last.then_inc(lowered, 1)

                def copy(i, k):
                    q = UNITS * i + k
                    dve.wait_ge(valued, q + 1)
                    dve.wait_ge(turned, q + 1 + AHEAD)
                    nc.vector.tensor_copy(probsT[k % 2][:, :, :].rearrange("p b j -> p (b j)"),
                                          p_ps[k % 2][:, :]).then_inc(copied, 1)

                def divide(i, u, o_turned_wait):
                    dve.wait_ge(valued, UNITS * i + HEADS * (u + 1) + AHEAD)
                    nc.vector.reciprocal(half_inv[u][:, :].rearrange("p (b n) -> p b n", b=RB),
                                         o_view(u)[:, :, :, HID]).then_inc(inv_ready, 1)
                    if o_turned_wait:
                        dve.wait_ge(o_turned, i)
                    dve.wait_ge(inv_ready, 2 * i + u + 1)
                    nc.vector.tensor_tensor(
                        o[:, u * RB:(u + 1) * RB, :, :], o_view(u)[:, :, :, 0:HID],
                        half_inv[u][:, :].rearrange("p (b n) -> p b n", b=RB).unsqueeze(3)
                        .broadcast_to([P, RB, HEADS, HID]), ALU.mult).then_inc(o_ready[u], 1)

                def window(i, e, half_i, load, prep, units, tail):
                    d, f = i - 1, 1 - e
                    for k in range(UNITS):
                        if units:
                            lower(i, k)
                        if tail if k < TURN else units:
                            copy(d if k < TURN else i, (k - TURN) % UNITS)
                        if k == VALUE - 1 and tail:
                            divide(d, 1, False)
                        if k == VALUE + HEADS - 1 and units:
                            divide(i, 0, tail)
                        if k == 5 and tail:
                            dve.wait_ge(g_ready, d + 1)
                            dve.wait_ge(o_turned, d + 1)
                            nc.vector.scalar_tensor_tensor(oT[:, :], gate[f][:, :], 1.0, oT_ps[:, :],
                                                           ALU.add, ALU.mult).then_inc(oT_ready, 1)
                        if k == 7 and tail:
                            hold(dve, stored[f], 16 * (half_i if e == 1 else half_i - 1), passed)
                            hold(dve, xb_ready, d + 1, passed)
                            dve.wait_ge(y_done, d + 1)
                            nc.vector.tensor_tensor(x1[f][:, :, :], xb[f][:, :, :],
                                                    y_ps[:, :].rearrange("p (b c) -> p b c", b=NB),
                                                    ALU.add).then_inc(x1_ready, 1)

                windows(dve, window)
        s.clear()


TB = 4
TILE = TB * P
TILES = TOKENS // TILE


def phase_batchnorm(nc, io, keep):
    x1_v = io["x1"].rearrange("(t b p) c -> t p b c", b=TB, p=P)
    with ExitStack() as ctx:
        s = Space(nc, ctx, "bn")

        def two(name, shape):
            return [s.sb(f"{name}{u}", shape) for u in range(2)]

        w, wT = s.sb("w", [P, C]), s.sb("wT", [P, C])
        gamma, beta = s.sb("gamma", [P, 1]), s.sb("beta", [P, 1])
        x, h = [s.sb(f"x{m}", [P, TB, C]) for m in range(4)], two("h", [P, TB, C])
        stats, mv = two("stats", [P, TB, 6]), two("mv", [P, TB, 2])
        vv, root, scale, shift = (two(n, [P, TB]) for n in ("vv", "root", "scale", "shift"))
        hT, wx = two("hT", [P, TILE]), two("wx", [P, TILE])
        all_stats, all_mv = s.sb("all_stats", [P, TILES, 6]), s.sb("all_mv", [P, 2])
        all_vv, all_root, all_inv, down = (s.sb(n, [P, 1]) for n in ("all_vv", "all_root", "all_inv", "down"))
        h_ps = [s.bank(f"h{u}") for u in range(2)]
        w_ps = [s.bank(f"w{u}") for u in range(2)]

        params, w_turned, wT_ready, passed = (s.sem(n) for n in ("params", "w_turned", "wT_ready", "passed"))
        x_loaded = [s.sem(f"x_loaded{m}") for m in range(4)]
        stored = [s.sem(f"stored{u}") for u in range(2)]
        step, vv_ready, root_ready, scaled, h_ready = (
            s.sem(n) for n in ("step", "vv_ready", "root_ready", "scaled", "h_ready"))
        h_turned, hT_ready, wx_done, wx_ready, counted = (
            s.sem(n) for n in ("h_turned", "hT_ready", "wx_done", "wx_ready", "counted"))
        final, final_vv, final_root = s.sem("final"), s.sem("final_vv"), s.sem("final_root")

        def windows(eng, window):
            stages(eng, window, TILES, 3, 2, 3)

        with nc.Block() as block:
            @block.sync
            def _(sp):
                sp.dma_start(w[:, :], io["L0_ffn_W"]).then_inc(params, 16)
                sp.dma_start(gamma[:, :], column(io["L0_ffn_gamma"])).then_inc(params, 16)
                sp.dma_start(beta[:, :], column(io["L0_ffn_beta"])).then_inc(params, 16)

                def window(t, m, q):
                    if is_tile(t + 3, TILES):
                        n = (m + 3) % 4
                        if is_tile(t + 3, TILES, 4):
                            sp.wait_ge(h_ready, t)
                        sp.dma_start(x[n][:, :, :], x1_v[t + 3]).then_inc(x_loaded[n], 16)
                    if is_tile(t - 1, TILES):
                        u = (m - 1) % 2
                        sp.wait_ge(wx_ready, t)
                        sp.dma_start(io["wx"][:, bass.ds((t - 1) * TILE, TILE)], wx[u][:, :]).then_inc(stored[u], 16)

                windows(sp, window)
                for u in range(2):
                    sp.wait_ge(stored[u], 16 * (TILES // 2))

            @block.vector
            def _(dve):
                def window(t, m, q):
                    if is_tile(t + 1, TILES):
                        f, u = t + 1, (m + 1) % 2
                        if is_tile(f, TILES, 2):
                            dve.wait_ge(h_ready, f - 1)
                        dve.wait_ge(root_ready, f + 1)
                        nc.vector.reciprocal(scale[u][:, :], root[u][:, :]).then_inc(scaled, 1)
                        dve.wait_ge(scaled, 2 * f + 1)
                        nc.vector.scalar_tensor_tensor(shift[u][:, :], mv[u][:, :, 0], -1.0, scale[u][:, :],
                                                       ALU.mult, ALU.mult).then_inc(scaled, 1)
                    if is_tile(t + 2, TILES):
                        f, n, u = t + 2, (m + 2) % 4, m % 2
                        dve.wait_ge(x_loaded[n], 16 * (q + (m + 2) // 4) + 16)
                        for k in range(TB):
                            last = nc.vector.bn_stats(stats[u][:, k, :], x[n][:, k, :])
                        last.then_inc(step, 1)
                    if is_tile(t - 2, TILES):
                        dve.wait_ge(wx_ready, t - 1)
                        nc.vector.bn_stats(all_stats[:, bass.ds(t - 2, 1), :].rearrange("p a s -> p (a s)"),
                                           wx[m % 2][:, :]).then_inc(counted, 1)
                    if is_tile(t + 2, TILES):
                        hold(dve, step, 2 * f + 1, passed)
                        for k in range(TB):
                            last = nc.vector.bn_aggr(mv[u][:, k, :], stats[u][:, k, :])
                        last.then_inc(step, 1)
                        dve.wait_ge(step, 2 * f + 2)
                        nc.vector.tensor_scalar(vv[u][:, :], mv[u][:, :, 1], 1.0, 1e-5,
                                                ALU.mult, ALU.add).then_inc(vv_ready, 1)

                windows(dve, window)
                hold(dve, counted, TILES, passed)
                nc.vector.bn_aggr(all_mv[:, :], all_stats[:, :, :].rearrange("p t s -> p (t s)")).then_inc(final, 1)
                dve.wait_ge(final, 1)
                nc.vector.tensor_scalar(all_vv[:, :], all_mv[:, 1:2], 1.0, 1e-5, ALU.mult,
                                        ALU.add).then_inc(final_vv, 1)
                dve.wait_ge(final_root, 1)
                nc.vector.reciprocal(all_inv[:, :], all_root[:, :]).then_inc(final, 1)
                dve.wait_ge(final, 2)
                nc.vector.tensor_tensor(keep["bn_scale"][:, :], all_inv[:, :], gamma[:, :],
                                        ALU.mult).then_inc(final, 1)
                dve.wait_ge(final, 3)
                nc.vector.tensor_tensor(down[:, :], all_mv[:, 0:1], keep["bn_scale"][:, :],
                                        ALU.mult).then_inc(final, 1)
                dve.wait_ge(final, 4)
                nc.vector.tensor_tensor(keep["bn_shift"][:, :], beta[:, :], down[:, :], ALU.subtract)

            @block.gpsimd
            def _(pool):
                def window(t, m, q):
                    if is_tile(t + 1, TILES):
                        f, n, u = t + 1, (m + 1) % 4, (m + 1) % 2
                        hold(pool, scaled, 2 * f + 2, passed)
                        if is_tile(f, TILES, 2):
                            hold(pool, h_turned, f - 1, passed)
                        for k in range(TB):
                            last = nc.gpsimd.tensor_scalar(h[u][:, k, :], x[n][:, k, :],
                                                           scale[u][:, k:k + 1], shift[u][:, k:k + 1],
                                                           ALU.mult, ALU.add)
                        last.then_inc(h_ready, 1)

                windows(pool, window)

            @block.tensor
            def _(pe):
                pe.wait_ge(params, 48)
                nc.tensor.transpose(w_ps[0][:, 0:C], w[:, :], keep["ident"][:, :]).then_inc(w_turned, 1)
                pe.wait_ge(wT_ready, 1)

                def window(t, m, q):
                    if is_tile(t, TILES):
                        u = m % 2
                        if is_tile(t, TILES, 2):
                            pe.wait_ge(hT_ready, t - 1)
                        pe.wait_ge(h_ready, t + 1)
                        for k in range(TB):
                            last = nc.tensor.transpose(h_ps[u][:, k * P:(k + 1) * P], h[u][:, k, :],
                                                       keep["ident"][:, :])
                        last.then_inc(h_turned, 1)
                    if is_tile(t - 1, TILES):
                        b, u = t - 1, (m - 1) % 2
                        if is_tile(b, TILES, 2):
                            pe.wait_ge(wx_ready, b - 1)
                        pe.wait_ge(hT_ready, b + 1)
                        nc.tensor.matmul(w_ps[u][:, :], wT[:, :], hT[u][:, :], start=True,
                                         stop=True).then_inc(wx_done, 1)

                windows(pe, window)

            @block.scalar
            def _(act):
                act.preload_act_table_set("sqrt_and_others")
                act.wait_ge(w_turned, 1)
                nc.scalar.activation(wT[:, :], w_ps[0][:, 0:C], ACT.Copy).then_inc(wT_ready, 1)

                def window(t, m, q):
                    if is_tile(t - 1, TILES):
                        b, u = t - 1, (m - 1) % 2
                        if is_tile(b, TILES, 2):
                            act.wait_ge(stored[u], 16 * (2 * (q + (m - 1) // 4) + (m - 1) % 4 // 2))
                            act.wait_ge(counted, b - 1)
                        act.wait_ge(wx_done, b + 1)
                        nc.scalar.activation(wx[u][:, :], w_ps[u][:, :], ACT.Copy).then_inc(wx_ready, 1)
                    if is_tile(t, TILES):
                        u = m % 2
                        if is_tile(t, TILES, 2):
                            act.wait_ge(wx_done, t - 1)
                        act.wait_ge(h_turned, t + 1)
                        nc.scalar.activation(hT[u][:, :], h_ps[u][:, :], ACT.Copy).then_inc(hT_ready, 1)
                    if is_tile(t + 2, TILES):
                        act.wait_ge(vv_ready, t + 3)
                        nc.scalar.activation(root[m % 2][:, :], vv[m % 2][:, :], ACT.Sqrt).then_inc(root_ready, 1)

                windows(act, window)
                act.wait_ge(final_vv, 1)
                nc.scalar.activation(all_root[:, :], all_vv[:, :], ACT.Sqrt).then_inc(final_root, 1)
        s.clear()


SECTIONS = 4
CHUNKS = 1024
RUN = TOKENS // SECTIONS // CHUNKS
WARM = 16
GROUPS = 4
LANES = CHUNKS // GROUPS
TOLERANCE = 1e-6


def phase_recurrence(nc, io, keep):
    PART = 2048
    PARTS = TOKENS // SECTIONS // PART
    N = CHUNKS * RUN
    UNROLL = 4
    with ExitStack() as ctx:
        s = Space(nc, ctx, "rnn")
        v, vT = s.sb("v", [P, C]), s.sb("vT", [P, C])
        seqs = [s.sb(f"seq{k}", [P, N]) for k in range(2)]
        y = [[s.sb(f"y{g}{k}", [P, LANES]) for k in range(2)] for g in range(GROUPS)]
        z = [s.sb(f"z{g}", [P, LANES]) for g in range(GROUPS)]
        starts = s.sb("starts", [P, CHUNKS + 1])
        gap, zero = s.sb("gap", [P, CHUNKS]), s.sb("zero", [P, LANES])
        worst, worst_all, z1 = s.sb("worst", [P, 1]), s.sb("worst_all", [P, 1]), s.sb("z_one", [P, 1])
        flag = [s.sb(f"flag{f}", [P, 1], I32) for f in range(SECTIONS)]
        v_ps = [s.bank(f"v{g}") for g in range(GROUPS)]
        one_ps = s.bank("one")

        params, v_turned, vT_ready, first, zeroed, passed = (
            s.sem(n) for n in ("params", "v_turned", "vT_ready", "first", "zeroed", "passed"))
        names = ("loaded", "reloaded", "stored", "multiplied", "added", "squashed", "started", "gapped",
                 "reduced", "all_reduced", "flagged", "one_product", "one_sum",
                 "one_state", "settled")
        hs = [{n: s.sem(f"{n}{f}") for n in names} for f in range(SECTIONS)]

        def lanes(f, g, t):
            return seqs[f % 2][:, :].rearrange("p (g l r) -> p g l r", g=GROUPS, l=LANES)[:, g, :, bass.ds(t, 1)] \
                .rearrange("p l a -> p (l a)")

        with nc.Block() as block:
            @block.sync
            def _(sp):
                def load(f, loaded):
                    for k in range(PARTS):
                        sp.dma_start(seqs[f % 2][:, k * PART:(k + 1) * PART],
                                     io["wx"][:, (f * PARTS + k) * PART:(f * PARTS + k + 1) * PART]
                                     ).then_inc(loaded, 16)

                sp.dma_start(v[:, :], io["L0_ffn_V"]).then_inc(params, 16)
                load(0, hs[0]["loaded"])
                for f in range(SECTIONS):
                    m = hs[f]
                    if f + 1 < SECTIONS:
                        if f:
                            sp.wait_ge(hs[f - 1]["stored"], 16 * PARTS)
                        load(f + 1, hs[f + 1]["loaded"])
                    sp.wait_ge(m["flagged"], 1)
                    with sp.If(sp.value_load(flag[f][0:1, 0:1])):
                        load(f, m["reloaded"])
                    sp.wait_ge(m["settled"], 1)
                    for k in range(PARTS):
                        sp.dma_start(io["yT"][:, (f * PARTS + k) * PART:(f * PARTS + k + 1) * PART],
                                     seqs[f % 2][:, k * PART:(k + 1) * PART]).then_inc(m["stored"], 16)
                for f in range(SECTIONS - 2, SECTIONS):
                    sp.wait_ge(hs[f]["stored"], 16 * PARTS)

            @block.tensor
            def _(pe):
                pe.wait_ge(params, 16)
                nc.tensor.transpose(v_ps[0][:, 0:C], v[:, :], keep["ident"][:, :]).then_inc(v_turned, 1)
                pe.wait_ge(vT_ready, 1)
                for f in range(SECTIONS):
                    m = hs[f]

                    def multiply(step, g, state):
                        pe.wait_ge(m["squashed"], step * GROUPS + g + 1)
                        nc.tensor.matmul(v_ps[g][:, 0:LANES], vT[:, :], state, start=True,
                                         stop=True).then_inc(m["multiplied"], 1)

                    with pe.Fori(0, WARM // 2) as i:
                        for k in range(2):
                            for g in range(GROUPS):
                                multiply(2 * i + k, g, y[g][k][:, :])
                    for k in range(UNROLL):
                        for g in range(GROUPS):
                            multiply(WARM + k, g, lanes(f, g, k - 1) if k else y[g][0][:, :])
                    with pe.Fori(0, RUN // UNROLL - 1) as i:
                        for k in range(UNROLL, 2 * UNROLL):
                            for g in range(GROUPS):
                                multiply(WARM + UNROLL * i + k, g, lanes(f, g, UNROLL * i + k - 1))
                    pe.wait_ge(m["flagged"], 1)
                    with pe.If(pe.value_load(flag[f][0:1, 0:1])):
                        nc.tensor.matmul(one_ps[:, 0:1], vT[:, :], starts[:, 0:1], start=True,
                                         stop=True).then_inc(m["one_product"], 1)
                        with pe.Fori(1, N) as i:
                            pe.wait_ge(m["one_state"], i)
                            nc.tensor.matmul(one_ps[:, 0:1], vT[:, :], seqs[f % 2][:, bass.ds(i - 1, 1)], start=True,
                                             stop=True).then_inc(m["one_product"], 1)

            @block.vector
            def _(dve):
                nc.vector.memset(starts[:, 0:1], 0.0).then_inc(first, 1)
                for f in range(SECTIONS):
                    m = hs[f]

                    def add(count, g, t):
                        dve.wait_ge(m["multiplied"], count + 1)
                        nc.vector.scalar_tensor_tensor(z[g][:, :], lanes(f, g, t), keep["bn_scale"][:, :],
                                                       v_ps[g][:, 0:LANES], ALU.mult, ALU.add
                                                       ).then_inc(m["added"], 1)

                    dve.wait_ge(m["loaded"], 16 * PARTS)
                    with dve.Fori(0, WARM // 2) as i:
                        for k in range(2):
                            for g in range(GROUPS):
                                add((2 * i + k) * GROUPS + g, g, RUN - WARM + 2 * i + k)
                    with dve.Fori(0, RUN // UNROLL) as i:
                        for k in range(UNROLL):
                            for g in range(GROUPS):
                                add((WARM + UNROLL * i + k) * GROUPS + g, g, UNROLL * i + k)
                    dve.wait_ge(m["squashed"], GROUPS * (WARM + RUN + 1))
                    ends = seqs[f % 2][:, :].rearrange("p (c r) -> p c r", r=RUN)[:, :, RUN - 1]
                    nc.vector.tensor_tensor(gap[:, 0:CHUNKS - 1], ends[:, 0:CHUNKS - 1], starts[:, 1:CHUNKS],
                                            ALU.subtract).then_inc(m["gapped"], 1)
                    dve.wait_ge(m["gapped"], 1)
                    nc.vector.tensor_reduce(worst[:, :], gap[:, 0:CHUNKS - 1], AX.X, ALU.max,
                                            apply_absolute_value=True).then_inc(m["reduced"], 1)
                    dve.wait_ge(m["all_reduced"], 1)
                    nc.vector.tensor_scalar(flag[f][:, :], worst_all[:, :], TOLERANCE, None,
                                            ALU.is_gt).then_inc(m["flagged"], 1)
                    dve.wait_ge(m["flagged"], 1)
                    with dve.If(dve.value_load(flag[f][0:1, 0:1])):
                        dve.wait_ge(m["reloaded"], 16 * PARTS)
                        with dve.Fori(0, N) as i:
                            dve.wait_ge(m["one_product"], i + 1)
                            nc.vector.scalar_tensor_tensor(z1[:, :], seqs[f % 2][:, bass.ds(i, 1)],
                                                           keep["bn_scale"][:, :], one_ps[:, 0:1],
                                                           ALU.mult, ALU.add).then_inc(m["one_sum"], 1)
                        dve.wait_ge(m["one_state"], N)
                    nc.vector.tensor_copy(starts[:, 0:1], seqs[f % 2][:, N - 1:N]).then_inc(m["settled"], 1)

            @block.scalar
            def _(act):
                act.preload_act_table_set("sigmoid_and_others")
                act.wait_ge(v_turned, 1)
                nc.scalar.activation(vT[:, :], v_ps[0][:, 0:C], ACT.Copy).then_inc(vT_ready, 1)
                act.wait_ge(first, 1)
                act.wait_ge(zeroed, 1)
                for f in range(SECTIONS):
                    m = hs[f]
                    if f:
                        act.wait_ge(hs[f - 1]["settled"], 1)

                    for g in range(GROUPS):
                        nc.scalar.activation(y[g][0][:, :], zero[:, :], ACT.Copy).then_inc(m["squashed"], 1)

                    def squash(step, g, state):
                        act.wait_ge(m["added"], step * GROUPS + g + 1)
                        nc.scalar.activation(state, z[g][:, :], ACT.Sigmoid, bias=keep["bn_shift"][:, :]
                                             ).then_inc(m["squashed"], 1)

                    with act.Fori(0, WARM // 2 - 1) as i:
                        for k in range(2):
                            for g in range(GROUPS):
                                squash(2 * i + k, g, y[g][1 - k][:, :])
                    for g in range(GROUPS):
                        squash(WARM - 2, g, y[g][1][:, :])
                    for g in range(GROUPS):
                        act.wait_ge(m["added"], (WARM - 1) * GROUPS + g + 1)
                        nc.scalar.activation(starts[:, g * LANES + 1:(g + 1) * LANES + 1], z[g][:, :],
                                             ACT.Sigmoid, bias=keep["bn_shift"][:, :]
                                             ).then_inc(m["started"], 1)
                    act.wait_ge(m["started"], GROUPS)
                    for g in range(GROUPS):
                        nc.scalar.activation(y[g][0][:, :], starts[:, g * LANES:(g + 1) * LANES], ACT.Copy
                                             ).then_inc(m["squashed"], 1)
                    with act.Fori(0, RUN // UNROLL) as i:
                        for k in range(UNROLL):
                            for g in range(GROUPS):
                                squash(WARM + UNROLL * i + k, g, lanes(f, g, UNROLL * i + k))
                    act.wait_ge(m["flagged"], 1)
                    with act.If(act.value_load(flag[f][0:1, 0:1])):
                        with act.Fori(0, N) as i:
                            act.wait_ge(m["one_sum"], i + 1)
                            nc.scalar.activation(seqs[f % 2][:, bass.ds(i, 1)], z1[:, :], ACT.Sigmoid,
                                                 bias=keep["bn_shift"][:, :]
                                                 ).then_inc(m["one_state"], 1)

            @block.gpsimd
            def _(pool):
                pool.memset(zero[:, :], 0.0).then_inc(zeroed, 1)
                for f in range(SECTIONS):
                    m = hs[f]
                    pool.wait_ge(m["reduced"], 1)
                    nc.gpsimd.partition_all_reduce(worst_all[:, :], worst[:, :], P,
                                                   bass.bass_isa.ReduceOp.max).then_inc(m["all_reduced"], 1)
        s.clear()


def phase_join(nc, io, keep):
    x1_v = io["x1"].rearrange("(t b p) c -> t p b c", b=TB, p=P)
    x2_v = io["x2"].rearrange("(t b p) c -> t p b c", b=TB, p=P)
    hT_v = io["hT"].rearrange("p r w -> p (r w)")
    with ExitStack() as ctx:
        s = Space(nc, ctx, "join")

        def ring(n, name, shape):
            return [s.sb(f"{name}{u}", shape) for u in range(n)]

        x1, x2 = (ring(4, n, [P, TB, C]) for n in ("x1", "x2"))
        y, h, hT = ring(4, "y", [P, TILE]), ring(2, "h", [P, TB, C]), ring(2, "hT", [P, TILE])
        stats, mv = ring(2, "stats", [P, TB, 6]), ring(2, "mv", [P, TB, 2])
        vv, root, scale, shift = (ring(2, n, [P, TB]) for n in ("vv", "root", "scale", "shift"))
        zeros = s.sb("zeros", [P, SIDE])
        y_ps = [s.bank(f"y{u}") for u in range(2)]
        h_ps = [s.bank(f"h{u}") for u in range(2)]

        zeros_ready, edges, passed = s.sem("zeros_ready"), s.sem("edges"), s.sem("passed")
        x1_loaded = [s.sem(f"x1_loaded{n}") for n in range(4)]
        y_loaded = [s.sem(f"y_loaded{n}") for n in range(4)]
        x2_stored = [s.sem(f"x2_stored{n}") for n in range(4)]
        hT_stored = [s.sem(f"hT_stored{u}") for u in range(2)]
        y_turned, x2_ready, step, vv_ready, root_ready, scaled, h_ready, h_turned, hT_ready = (
            s.sem(n) for n in ("y_turned", "x2_ready", "step", "vv_ready", "root_ready", "scaled",
                               "h_ready", "h_turned", "hT_ready"))

        def windows(eng, window):
            stages(eng, window, TILES, 4, 1, 2)

        with nc.Block() as block:
            @block.sync
            def _(sp):
                sp.wait_ge(zeros_ready, 1)
                for r in (0, SIDE + 1):
                    sp.dma_start(io["hT"][:, r, :], zeros[:, :]).then_inc(edges, 16)

                def window(t, m, q):
                    if is_tile(t + 4, TILES):
                        if is_tile(t + 4, TILES, 4):
                            sp.wait_ge(x2_ready, t + 1)
                            sp.wait_ge(y_turned, t + 1)
                        sp.dma_start(x1[m][:, :, :], x1_v[t + 4]).then_inc(x1_loaded[m], 16)
                        sp.dma_start(y[m][:, :], io["yT"][:, bass.ds((t + 4) * TILE, TILE)]).then_inc(y_loaded[m], 16)
                    if is_tile(t + 1, TILES):
                        n = (m + 1) % 4
                        sp.wait_ge(x2_ready, t + 2)
                        sp.dma_start(x2_v[t + 1], x2[n][:, :, :]).then_inc(x2_stored[n], 16)
                    if is_tile(t - 1, TILES):
                        u = (m - 1) % 2
                        sp.wait_ge(hT_ready, t)
                        sp.dma_start(hT_v[:, bass.ds((t - 1) * TILE + SIDE, TILE)], hT[u][:, :]
                                     ).then_inc(hT_stored[u], 16)

                windows(sp, window)
                sp.wait_ge(edges, 32)
                for n in range(4):
                    sp.wait_ge(x2_stored[n], 16 * (TILES // 4))
                for u in range(2):
                    sp.wait_ge(hT_stored[u], 16 * (TILES // 2))

            @block.tensor
            def _(pe):
                def window(t, m, q):
                    if is_tile(t + 3, TILES):
                        f, n, u = t + 3, (m + 3) % 4, (m + 3) % 2
                        pe.wait_ge(y_loaded[n], 16 * (q + (m + 3) // 4) + 16)
                        if is_tile(f, TILES, 2):
                            pe.wait_ge(x2_ready, f - 1)
                        for k in range(TB):
                            last = nc.tensor.transpose(y_ps[u][:, k * P:(k + 1) * P],
                                                       y[n][:, k * P:(k + 1) * P], keep["ident"][:, :])
                        last.then_inc(y_turned, 1)
                    if is_tile(t, TILES):
                        u = m % 2
                        pe.wait_ge(h_ready, t + 1)
                        if is_tile(t, TILES, 2):
                            pe.wait_ge(hT_ready, t - 1)
                        for k in range(TB):
                            last = nc.tensor.transpose(h_ps[u][:, k * P:(k + 1) * P], h[u][:, k, :],
                                                       keep["ident"][:, :])
                        last.then_inc(h_turned, 1)

                windows(pe, window)

            @block.vector
            def _(dve):
                nc.vector.memset(zeros[:, :], 0.0).then_inc(zeros_ready, 1)

                def window(t, m, q):
                    if is_tile(t + 2, TILES):
                        f, n, u = t + 2, (m + 2) % 4, m % 2
                        if is_tile(f, TILES, 4):
                            hold(dve, x2_stored[n], 16 * (q + (m + 2) // 4), passed)
                            hold(dve, h_ready, f - 3, passed)
                        hold(dve, x1_loaded[n], 16 * (q + (m + 2) // 4) + 16, passed)
                        dve.wait_ge(y_turned, f + 1)
                        nc.vector.tensor_tensor(x2[n][:, :, :], x1[n][:, :, :],
                                                y_ps[u][:, :].rearrange("p (b c) -> p b c", b=TB),
                                                ALU.add).then_inc(x2_ready, 1)
                    if is_tile(t + 1, TILES):
                        g, w = t + 1, (m + 1) % 2
                        if is_tile(g, TILES, 2):
                            dve.wait_ge(h_ready, g - 1)
                        dve.wait_ge(root_ready, g + 1)
                        nc.vector.reciprocal(scale[w][:, :], root[w][:, :]).then_inc(scaled, 1)
                    if is_tile(t + 2, TILES):
                        dve.wait_ge(x2_ready, f + 1)
                        for k in range(TB):
                            last = nc.vector.bn_stats(stats[u][:, k, :], x2[n][:, k, :])
                        last.then_inc(step, 1)
                    if is_tile(t + 1, TILES):
                        dve.wait_ge(scaled, 2 * g + 1)
                        nc.vector.scalar_tensor_tensor(shift[w][:, :], mv[w][:, :, 0], -1.0, scale[w][:, :],
                                                       ALU.mult, ALU.mult).then_inc(scaled, 1)
                    if is_tile(t + 2, TILES):
                        hold(dve, step, 2 * f + 1, passed)
                        for k in range(TB):
                            last = nc.vector.bn_aggr(mv[u][:, k, :], stats[u][:, k, :])
                        last.then_inc(step, 1)
                        dve.wait_ge(step, 2 * f + 2)
                        nc.vector.tensor_scalar(vv[u][:, :], mv[u][:, :, 1], 1.0, 1e-6,
                                                ALU.mult, ALU.add).then_inc(vv_ready, 1)

                windows(dve, window)

            @block.gpsimd
            def _(pool):
                def window(t, m, q):
                    if is_tile(t + 1, TILES):
                        f, n, u = t + 1, (m + 1) % 4, (m + 1) % 2
                        hold(pool, scaled, 2 * f + 2, passed)
                        if is_tile(f, TILES, 2):
                            hold(pool, h_turned, f - 1, passed)
                        for k in range(TB):
                            last = nc.gpsimd.tensor_scalar(h[u][:, k, :], x2[n][:, k, :],
                                                           scale[u][:, k:k + 1], shift[u][:, k:k + 1],
                                                           ALU.mult, ALU.add)
                        last.then_inc(h_ready, 1)

                windows(pool, window)

            @block.scalar
            def _(act):
                act.preload_act_table_set("sqrt_and_others")

                def window(t, m, q):
                    if is_tile(t, TILES):
                        u = m % 2
                        if is_tile(t, TILES, 2):
                            act.wait_ge(hT_stored[u], 16 * (2 * q + m // 2))
                        act.wait_ge(h_turned, t + 1)
                        nc.scalar.activation(hT[u][:, :], h_ps[u][:, :], ACT.Copy).then_inc(hT_ready, 1)
                    if is_tile(t + 2, TILES):
                        act.wait_ge(vv_ready, t + 3)
                        nc.scalar.activation(root[m % 2][:, :], vv[m % 2][:, :], ACT.Sqrt).then_inc(root_ready, 1)

                windows(act, window)
        s.clear()


STATES = 8
RANK = 8
TAPS = 3
PAD = SIDE + 2
OVERFLOW = 88.72283936
BELOW = 88.72283172607
DEPTH = 4
LAGS = 3
SLOT = 32


def phase_mamba(nc, io, keep):
    ROWS = TILE // SIDE
    x2_v = io["x2"].rearrange("(t b p) c -> t p b c", b=TB, p=P)
    x3_v = io["x3"].rearrange("(t b p) c -> t p b c", b=TB, p=P)
    par = {k[8:]: v for k, v in io.items() if k.startswith("L1_conv_")}
    groups = par["w1"].shape[0]
    G = C // groups
    with ExitStack() as ctx:
        s = Space(nc, ctx, "mamba")

        def two(name, shape, dt=F32):
            return [s.sb(f"{name}{u}", shape, dt) for u in range(2)]

        w1n, w2n, won, inn_u, inn_z, outn = (s.sb(n, [P, C]) for n in ("w1n", "w2n", "won", "inn_u", "inn_z", "outn"))
        tapn, shiftn = s.sb("tapn", [P, TAPS * TAPS, C]), s.sb("shiftn", [P, LAGS, C])
        xpn = s.sb("xpn", [3 * SLOT, C])
        xp_dt, dt_t = s.sb("xp_dt", [RANK, C]), s.sb("dt_t", [RANK, C])
        tap_t, in_u_t = s.sb("tap_t", [P, TAPS * TAPS, C]), s.sb("in_u_t", [P, LAGS, C])
        w2_t, wo_t, in_z_t, out_t, d_t = (s.sb(n, [P, C]) for n in ("w2_t", "wo_t", "in_z_t", "out_t", "d_t"))
        xp_t = s.sb("xp_t", [P, 3 * SLOT])
        dw, cw, a_log, a_neg = s.sb("dw", [P, TAPS * TAPS]), s.sb("cw", [P, 3]), s.sb("a_log", [P, STATES]), s.sb("a_neg", [P, STATES])
        a_exp, a_low, a_gone, a_mil, limit = (
            s.sb(n, [P, STATES]) for n in ("a_exp", "a_low", "a_gone", "a_mil", "limit"))
        cb, dtb, dpar, gamma, beta = (s.sb(n, [P, 1]) for n in ("cb", "dtb", "dpar", "gamma", "beta"))
        select = s.sb("select", [3 * SLOT, 2 * STATES, P], BF16)
        half, one = s.sb("half", [P, TB]), s.sb("one", [P, 1])
        win = two("win", [P, ROWS + 2, PAD])
        centre = two("centre", [P, TILE])
        conv = two("conv", [P, LAGS - 1 + TILE])
        size, ex, logs, rest, over = (s.sb(n, [P, TILE]) for n in ("size", "ex", "logs", "rest", "over"))
        u_act, z_act, delta, du = (two(n, [P, TILE]) for n in ("u_act", "z_act", "delta", "du"))
        parts = two("parts", [3 * SLOT, TILE], BF16)
        remain, middle = s.sb("remain", [3 * SLOT, TILE]), s.sb("middle", [3 * SLOT, TILE], BF16)
        capped, decay, seen = ([s.sb(f"{name}{k}", [P, TILE]) for k in range(DEPTH)]
                               for name in ("capped", "decay", "seen"))
        drive, acc = two("drive", [P, TILE]), s.sb("acc", [P, TILE])
        state = [[s.sb(f"state{u}{n}", [P, TILE]) for n in range(STATES)] for u in range(2)]
        w2_act, y, yz = two("w2_act", [P, TILE]), two("y", [P, TILE]), two("yz", [P, TILE])
        x2, x3 = two("x2", [P, TB, C]), two("x3", [P, TB, C])
        stats, mv, vv, scale, shift = (s.sb("stats", [P, TB, 6]), s.sb("mv", [P, TB, 2]), s.sb("vv", [P, TB]),
                                       s.sb("scale", [P, TB]), s.sb("shift", [P, TB]))
        normed, affine, fused = s.sb("normed", [P, TB, C]), s.sb("affine", [P, TILE]), s.sb("fused", [P, TILE])

        b_ps, conv_ps, w2_ps, u_ps, z_ps, tail_ps = (s.bank(n) for n in ("b", "conv", "w2", "u", "z", "tail"))
        c_ps = [s.bank(f"c{k}") for k in range(2)]
        x_ps, d_ps = w2_ps, u_ps
        mid, lo = slice(SLOT, 2 * SLOT), slice(2 * SLOT, 3 * SLOT)

        names = ("params blank placed scaled_taps w_turned w_kept a_made a_held ready selector passed "
                 "conv_done conv_ready w2_done w2_ready u_done u_ready z_done z_ready "
                 "x_done d_done high_ready remain_ready mid_ready middle_ready parts_ready size_ready ex_ready "
                 "log_ready over_ready back_ready rest_ready sum1 delta_ready du_ready "
                 "b_done c_done driven capped decayed scanned seen_ready summed "
                 "y_ready yz_ready out_done tail_step vv_ready scale_ready shift_ready normed_ready n_turned "
                 "affine_ready fused_ready o_done x3_ready").split()
        S = {n: s.sem(n) for n in names}
        win_loaded = [s.sem(f"win_loaded{u}") for u in range(2)]
        centre_loaded = [s.sem(f"centre_loaded{u}") for u in range(2)]
        x2_loaded = [s.sem(f"x2_loaded{u}") for u in range(2)]
        stored = [s.sem(f"stored{u}") for u in range(2)]

        PARAMS = 3 * groups + 3 + 11 + 2

        def windows(eng, window):
            window(-3, 1, -2, True, False, False, False, False, False)
            window(-2, 0, -1, True, True, False, False, False, False)
            window(-1, 1, -1, True, True, True, False, False, False)
            window(0, 0, 0, True, True, True, True, False, False)
            window(1, 1, 0, True, True, True, True, True, False)
            window(2, 0, 1, True, True, True, True, True, True)
            with eng.Fori(0, TILES // 2 - 3) as i:
                window(2 * i + 3, 1, i + 1, True, True, True, True, True, True)
                window(2 * i + 4, 0, i + 2, True, True, True, True, True, True)
            last = TILES // 2 - 2
            window(TILES - 3, 1, last, False, True, True, True, True, True)
            window(TILES - 2, 0, last + 1, False, False, True, True, True, True)
            window(TILES - 1, 1, last + 1, False, False, False, True, True, True)
            window(TILES, 0, last + 2, False, False, False, False, True, True)
            window(TILES + 1, 1, last + 2, False, False, False, False, False, True)

        with nc.Block() as block:
            @block.sync
            def _(sp):
                n = 0
                sp.wait_ge(S["blank"], 4)
                for w, name in ((w1n, "w1"), (w2n, "w2"), (won, "wout")):
                    for k in range(groups):
                        sp.dma_start(w[k * G:(k + 1) * G, k * G:(k + 1) * G], par[name][k]).then_inc(S["params"], 16)
                        n += 1
                for k in range(3):
                    sp.dma_start(xpn[k * SLOT:k * SLOT + 2 * STATES, :],
                                 par["x_proj_w"][RANK:RANK + 2 * STATES, :]).then_inc(S["params"], 16)
                    n += 1
                for dst, src in ((inn_u, par["in_proj_w"][0:C, :]), (inn_z, par["in_proj_w"][C:2 * C, :]),
                                 (outn, par["out_proj_w"]), (xp_dt, par["x_proj_w"][0:RANK, :]),
                                 (cw, par["conv1d_w"]), (a_log, par["A_log"]),
                                 (cb, column(par["conv1d_b"])), (dtb, column(par["dt_proj_b"])),
                                 (dpar, column(par["D_param"])), (gamma, column(par["gamma"])),
                                 (beta, column(par["beta"]))):
                    sp.dma_start(dst[:, :], src).then_inc(S["params"], 16)
                    n += 1
                with nc.allow_non_contiguous_dma(reason="small weights, once"):
                    sp.dma_start(dt_t[:, :], par["dt_proj_w"].rearrange("d r -> r d")).then_inc(S["params"], 16)
                    sp.dma_start(dw[:, :], par["dw"].rearrange("a b c d -> d (a b c)")).then_inc(S["params"], 16)
                n += 2
                assert n == PARAMS, n

                def window(t, u, half_t, first, second, front, scan, back, late):
                    v = 1 - u
                    if first:
                        g = t + 3
                        sp.wait_ge(S["conv_done"], g + 1)
                        sp.dma_start(win[v][:, :, 1:1 + SIDE],
                                     io["hT"][:, bass.ds(ROWS * g, ROWS + 2), :]).then_inc(win_loaded[v], 16)
                    if front:
                        f = t + 1
                        sp.wait_ge(S["w2_done"], f + 1)
                        sp.dma_start(centre[v][:, :].rearrange("p (r w) -> p r w", r=ROWS),
                                     io["hT"][:, bass.ds(ROWS * f + 1, ROWS), :]).then_inc(centre_loaded[v], 16)
                    if scan:
                        sp.wait_ge(S["o_done"], t + 1)
                        sp.dma_start(x2[u][:, :, :], x2_v[t]).then_inc(x2_loaded[u], 16)
                    if late:
                        sp.wait_ge(S["x3_ready"], t - 1 + AHEAD)
                        sp.dma_start(x3_v[t - 2], x3[u][:, :, :]).then_inc(stored[u], 16)

                windows(sp, window)
                for u in range(2):
                    sp.wait_ge(stored[u], 16 * (TILES // 2))

            @block.tensor
            def _(pe):
                ident = keep["ident"][:, :]
                pe.wait_ge(S["params"], 16 * PARAMS)
                pe.wait_ge(S["scaled_taps"], 1)
                turns = [(w[:, :], P) for w in (w2n, won, inn_z, outn)] \
                    + [(shiftn[:, k, :], P) for k in range(LAGS)] \
                    + [(tapn[:, k, :], P) for k in range(TAPS * TAPS)] + [(xpn[:, :], 3 * SLOT)]
                for k, (src, rows) in enumerate(turns):
                    if k:
                        pe.wait_ge(S["w_kept"], k)
                    nc.tensor.transpose(conv_ps[:, 0:rows], src, ident[0:rows, 0:rows]).then_inc(S["w_turned"], 1)
                pe.wait_ge(S["w_kept"], len(turns))
                nc.tensor.matmul(conv_ps[:, 0:C], xp_dt[:, :], dt_t[:, :], start=True, stop=True
                                 ).then_inc(S["w_turned"], 1)
                pe.wait_ge(S["w_kept"], len(turns) + 1)
                pe.wait_ge(S["selector"], 4)
                pe.sem_inc(S["w2_done"], AHEAD)
                pe.sem_inc(S["conv_done"], AHEAD)
                pe.sem_inc(S["o_done"], AHEAD)

                def window(t, u, half_t, first, second, front, scan, back, late):
                    f, v, b = t + 1, 1 - u, t - 1

                    def taps(v, ks):
                        for k in ks:
                            dy, dx = divmod(k, TAPS)
                            last = nc.tensor.matmul(conv_ps[:, :].rearrange("p (r w) -> p r w", r=ROWS),
                                                    tap_t[:, k, :], win[v][:, dy:dy + ROWS, dx:dx + SIDE],
                                                    start=k == 0, stop=k == TAPS * TAPS - 1)
                        return last

                    def spread_b(t, u, n):
                        if not isinstance(t, int) or t + n > 0:
                            pe.wait_ge(S["driven"], STATES * t + n)
                        nc.tensor.matmul(b_ps[:, :], select[:, n, :], parts[u][:, :], start=True,
                                         stop=True).then_inc(S["b_done"], 1)

                    for n in range(STATES):
                        q = STATES * t + n
                        if scan and n + 1 < STATES:
                            spread_b(t, u, n + 1)
                        if scan:
                            pe.wait_ge(S["seen_ready"], q + 1)
                            nc.tensor.matmul(c_ps[n % 2][:, :], select[:, STATES + n, :], parts[u][:, :],
                                             start=True, stop=True).then_inc(S["c_done"], 1)
                        if n == 0 and front:
                            pe.wait_ge(S["over_ready"], f + 2)
                            pe.wait_ge(S["conv_ready"], f + 1 + AHEAD)
                            for k in range(LAGS):
                                last = nc.tensor.matmul(u_ps[:, :], in_u_t[:, k, :], conv[v][:, k:k + TILE],
                                                        start=k == 0, stop=k == LAGS - 1)
                            last.then_inc(S["u_done"], 1)
                            pe.wait_ge(S["z_ready"], f + 2)
                            nc.tensor.matmul(z_ps[:, :], in_z_t[:, :], conv[v][:, LAGS - 1:], start=True,
                                             stop=True).then_inc(S["z_done"], 1)
                        if n in (1, 2) and second:
                            taps_done = taps(u, (6,) if n == 1 else (7, 8))
                            if n == 2:
                                taps_done.then_inc(S["conv_done"], 1)
                        if n == 5 and first:
                            g = t + 3
                            pe.wait_ge(win_loaded[v], 16 * (half_t + 1 + u) + 16)
                            pe.wait_ge(S["conv_ready"], g + AHEAD)
                        if n >= 5 and first:
                            taps(v, (2 * (n - 5), 2 * (n - 5) + 1))
                        if n == 2 and back:
                            pe.wait_ge(S["yz_ready"], b + 1 + AHEAD)
                            pe.wait_ge(S["x3_ready"], b + 2)
                            for k in range(TB):
                                last = nc.tensor.matmul(tail_ps[:, k * C:(k + 1) * C], yz[1 - u][:, k * P:(k + 1) * P],
                                                        out_t[:, :], start=True, stop=True)
                            last.then_inc(S["out_done"], 1)
                        if n == 1 and scan:
                            pe.wait_ge(S["remain_ready"], t + 1 + AHEAD)
                            pe.wait_ge(centre_loaded[u], 16 * half_t + 16)
                            nc.tensor.matmul(w2_ps[:, :], w2_t[:, :], centre[u][:, :], start=True,
                                             stop=True).then_inc(S["w2_done"], 1)
                        if n == 6 and back:
                            pe.wait_ge(S["normed_ready"], b + 1)
                            for k in range(TB):
                                last = nc.tensor.transpose(tail_ps[:, k * P:(k + 1) * P], normed[:, k, :], ident)
                            last.then_inc(S["n_turned"], 1)
                        if n == 4 and front:
                            if scan:
                                pe.wait_ge(S["w2_ready"], t + 1 + AHEAD)
                            pe.wait_ge(S["u_ready"], f + 1)
                            nc.tensor.matmul(x_ps[0:3 * SLOT, :], xp_t[:, :], u_act[v][:, :], start=True,
                                             stop=True).then_inc(S["x_done"], 1)
                            nc.tensor.matmul(d_ps[:, :], d_t[:, :], u_act[v][:, :], start=True,
                                             stop=True).then_inc(S["d_done"], 1)
                        if n == 7 and front:
                            pe.wait_ge(S["parts_ready"], f + 1)
                            spread_b(f, v, 0)
                        if n == 7 and back:
                            pe.wait_ge(x2_loaded[1 - u], 16 * (half_t if u == 1 else half_t - 1) + 16)
                            pe.wait_ge(S["affine_ready"], b + 1)
                            nc.tensor.matmul(tail_ps[:, :], ident, x2[1 - u][:, :, :].rearrange("p b c -> p (b c)"),
                                             start=True, stop=False)
                            pe.wait_ge(S["fused_ready"], b + 1 + AHEAD)
                            for k in range(TB):
                                last = nc.tensor.matmul(tail_ps[:, k * C:(k + 1) * C], fused[:, k * P:(k + 1) * P],
                                                        wo_t[:, :], start=False, stop=k == TB - 1)
                            last.then_inc(S["o_done"], 1)

                windows(pe, window)

            @block.scalar
            def _(act):
                act.wait_ge(S["params"], 16 * PARAMS)
                keeps = [w2_t[:, :], wo_t[:, :], in_z_t[:, :], out_t[:, :]] \
                    + [in_u_t[:, k, :] for k in range(LAGS)] \
                    + [tap_t[:, k, :] for k in range(TAPS * TAPS)] + [xp_t[:, :], d_t[:, :]]
                for k, dst in enumerate(keeps):
                    act.wait_ge(S["w_turned"], k + 1)
                    nc.scalar.activation(dst, conv_ps[:, 0:dst.shape[-1]], ACT.Copy).then_inc(S["w_kept"], 1)
                act.preload_act_table_set("natural_log_exp_and_others")
                act.wait_ge(S["a_held"], 3)
                nc.scalar.activation(a_exp[:, :], a_low[:, :], ACT.Exp).then_inc(S["a_made"], 1)
                act.wait_ge(S["a_made"], 1)
                nc.scalar.activation(a_neg[:, :], a_exp[:, :], ACT.Copy, scale=-1.0).then_inc(S["a_made"], 1)
                act.wait_ge(S["a_made"], 2)
                act.wait_ge(S["ready"], 4)
                act.sem_inc(S["w2_ready"], AHEAD)
                act.sem_inc(S["decayed"], DEPTH)
                act.sem_inc(S["conv_ready"], AHEAD)
                act.sem_inc(S["over_ready"], AHEAD)
                act.sem_inc(S["z_ready"], AHEAD)
                act.sem_inc(S["x3_ready"], AHEAD)

                def window(t, u, half_t, first, second, front, scan, back, late):
                    f, v, b = t + 1, 1 - u, t - 1
                    def decay_of(n):
                        q = STATES * t + n
                        act.wait_ge(S["capped"], q + 1)
                        act.wait_ge(S["scanned"], q + 1)
                        nc.scalar.activation(decay[n % DEPTH][:, :], capped[n % DEPTH][:, :], ACT.Exp,
                                             bias=a_gone[:, n:n + 1], scale=a_neg[:, n:n + 1]).then_inc(S["decayed"], 1)

                    for n in range(STATES):
                        if scan:
                            for m in ((0, 1) if n == 0 else range(n + 1, min(n + 2, STATES))):
                                decay_of(m)
                        if n == 0 and late:
                            if not isinstance(t, int) or t > 3:
                                act.wait_ge(stored[u], 16 * (half_t - 1))
                            act.wait_ge(S["o_done"], t - 1 + AHEAD)
                            nc.scalar.activation(x3[u][:, :, :].rearrange("p b c -> p (b c)"), tail_ps[:, :],
                                                 ACT.Copy).then_inc(S["x3_ready"], 1)
                        if n == 3 and (second or front or scan):
                            act.preload_act_table_set("silu_and_others")
                            if scan:
                                act.wait_ge(S["fused_ready"], t + 1)
                                act.wait_ge(S["w2_done"], t + 1 + AHEAD)
                                nc.scalar.activation(w2_act[u][:, :], w2_ps[:, :], ACT.Silu).then_inc(S["w2_ready"], 1)
                            if front:
                                act.wait_ge(S["y_ready"], f + 1)
                                act.wait_ge(S["u_done"], f + 1)
                                nc.scalar.activation(u_act[v][:, :], u_ps[:, :], ACT.Silu, bias=cb[:, :]
                                                     ).then_inc(S["u_ready"], 1)
                                act.wait_ge(S["yz_ready"], f + 1)
                                act.wait_ge(S["z_done"], f + 1)
                                nc.scalar.activation(z_act[v][:, :], z_ps[:, :], ACT.Silu).then_inc(S["z_ready"], 1)
                            if second:
                                act.wait_ge(S["conv_done"], t + 2 + 1 + AHEAD)
                                nc.scalar.activation(conv[v][:, 0:LAGS - 1], conv_ps[:, TILE - LAGS + 1:TILE], ACT.Silu)
                                nc.scalar.activation(conv[u][:, LAGS - 1:], conv_ps[:, :], ACT.Silu
                                                     ).then_inc(S["conv_ready"], 1)
                            act.preload_act_table_set("natural_log_exp_and_others")
                        if n == 4 and front:
                            act.wait_ge(S["x_done"], f + 1)
                            nc.scalar.activation(parts[v][:, :], x_ps[0:3 * SLOT, :], ACT.Copy
                                                 ).then_inc(S["high_ready"], 1)
                            act.wait_ge(S["d_done"], f + 1)
                            nc.scalar.activation(size[:, :], d_ps[:, :], ACT.Abs, bias=dtb[:, :]).then_inc(S["size_ready"], 1)
                            nc.scalar.activation(over[:, :], d_ps[:, :], ACT.Relu, bias=dtb[:, :]).then_inc(S["over_ready"], 1)
                            act.wait_ge(S["size_ready"], f + 1)
                            nc.scalar.activation(ex[:, :], size[:, :], ACT.Exp, scale=-1.0).then_inc(S["ex_ready"], 1)
                            act.wait_ge(S["ex_ready"], f + 1)
                            nc.scalar.activation(logs[:, :], ex[:, :], ACT.Ln, bias=one[:, :]).then_inc(S["log_ready"], 1)
                        if n == 5 and front:
                            act.wait_ge(S["remain_ready"], f + 1 + AHEAD)
                            nc.scalar.activation(middle[lo, :], remain[lo, :], ACT.Copy).then_inc(S["middle_ready"], 1)
                            nc.scalar.activation(parts[v][mid, :], remain[mid, :], ACT.Copy).then_inc(S["mid_ready"], 1)
                        if n == 5 and back:
                            act.wait_ge(S["shift_ready"], b + 1)
                            for k in range(TB):
                                last = nc.scalar.activation(normed[:, k, :], tail_ps[:, k * C:(k + 1) * C],
                                                            ACT.Identity, bias=shift[:, k:k + 1],
                                                            scale=scale[:, k:k + 1])
                            last.then_inc(S["normed_ready"], 1)
                        if n == 6 and back:
                            act.wait_ge(S["fused_ready"], b + 2)
                            act.wait_ge(S["n_turned"], b + 1)
                            nc.scalar.activation(affine[:, :], tail_ps[:, :], ACT.Identity, bias=beta[:, :],
                                                 scale=gamma[:, :]).then_inc(S["affine_ready"], 1)

                windows(act, window)

            @block.vector
            def _(dve):
                for w in (w1n, w2n, won):
                    nc.vector.memset(w[:, :], 0.0).then_inc(S["blank"], 1)
                nc.vector.memset(xpn[:, :], 0.0).then_inc(S["blank"], 1)
                for u in range(2):
                    nc.vector.memset(win[u][:, :, 0:1], 0.0)
                    nc.vector.memset(win[u][:, :, PAD - 1:PAD], 0.0)
                nc.vector.memset(conv[0][:, 0:LAGS - 1], 0.0).then_inc(S["ready"], 1)
                nc.vector.memset(one[:, :], 1.0).then_inc(S["ready"], 1)
                for n in range(STATES):
                    nc.vector.memset(state[1][n][:, TILE - 1:TILE], 0.0)
                nc.vector.memset(half[:, :], -0.5).then_inc(S["ready"], 2)
                dve.wait_ge(S["params"], 16 * PARAMS)
                nc.vector.tensor_scalar(a_low[:, :], a_log[:, :], BELOW, None, ALU.min
                                        ).then_inc(S["a_held"], 1)
                nc.vector.tensor_scalar(a_gone[:, :], a_log[:, :], OVERFLOW, -1000.0, ALU.is_ge, ALU.mult
                                        ).then_inc(S["a_held"], 2)
                for k in range(TAPS * TAPS):
                    nc.vector.tensor_scalar(tapn[:, k, :], w1n[:, :], dw[:, k:k + 1], None, ALU.mult)
                for k in range(LAGS):
                    last = nc.vector.tensor_scalar(shiftn[:, k, :], inn_u[:, :], cw[:, k:k + 1], None, ALU.mult)
                last.then_inc(S["scaled_taps"], 1)
                dve.wait_ge(S["a_made"], 1)
                nc.vector.tensor_scalar(a_mil[:, :], a_exp[:, :], 1e-34, 1e-3, ALU.max, ALU.mult
                                        ).then_inc(S["a_held"], 1)
                dve.wait_ge(S["a_held"], 4)
                nc.vector.reciprocal(limit[:, :], a_mil[:, :]).then_inc(S["a_held"], 1)
                dve.wait_ge(S["ready"], 4)
                dve.sem_inc(S["remain_ready"], AHEAD)
                dve.sem_inc(S["y_ready"], AHEAD)
                dve.sem_inc(S["scanned"], DEPTH)
                dve.sem_inc(S["seen_ready"], AHEAD)

                def window(t, u, half_t, first, second, front, scan, back, late):
                    f, v, b = t + 1, 1 - u, t - 1
                    def cap(t, u, n):
                        hold(dve, S["decayed"], STATES * t + n + 1, S["passed"])
                        nc.vector.tensor_scalar(capped[n % DEPTH][:, :], delta[u][:, :], limit[:, n:n + 1], None,
                                                ALU.min).then_inc(S["capped"], 1)

                    def drives(n):
                        dve.wait_ge(S["b_done"], STATES * t + n + 1)
                        nc.vector.tensor_tensor(drive[n % 2][:, :], du[u][:, :], b_ps[:, :],
                                                ALU.mult).then_inc(S["driven"], 1)

                    if scan:
                        dve.wait_ge(S["du_ready"], t + 1)
                        drives(0)
                    for n in range(STATES):
                        q = STATES * t + n
                        if scan:
                            hold(dve, S["decayed"], q + 1 + DEPTH, S["passed"])
                            dve.wait_ge(S["driven"], q + 1)
                            nc.vector.tensor_tensor_scan(state[u][n][:, :], decay[n % DEPTH][:, :], drive[n % 2][:, :],
                                                         initial=state[1 - u][n][:, TILE - 1:TILE],
                                                         op0=ALU.mult, op1=ALU.add).then_inc(S["scanned"], 1)
                            if n + 1 < STATES:
                                drives(n + 1)
                        if n == STATES - 1 and front:
                            hold(dve, S["delta_ready"], f + 1, S["passed"])
                            for m in range(DEPTH - 1):
                                cap(f, v, m)
                        if n == 3 and back:
                            dve.wait_ge(S["out_done"], b + 1)
                            for k in range(TB):
                                last = nc.vector.bn_stats(stats[:, k, :], tail_ps[:, k * C:(k + 1) * C])
                            last.then_inc(S["tail_step"], 1)
                            hold(dve, S["tail_step"], 2 * b + 1, S["passed"])
                            for k in range(TB):
                                last = nc.vector.bn_aggr(mv[:, k, :], stats[:, k, :])
                            last.then_inc(S["tail_step"], 1)
                            dve.wait_ge(S["tail_step"], 2 * b + 2)
                            nc.vector.tensor_scalar(vv[:, :], mv[:, :, 1], 1.0, 1e-5, ALU.mult,
                                                    ALU.add).then_inc(S["vv_ready"], 1)
                        if n == 4 and back:
                            dve.wait_ge(S["scale_ready"], b + 1)
                            nc.vector.scalar_tensor_tensor(shift[:, :], mv[:, :, 0], -1.0, scale[:, :], ALU.mult,
                                                           ALU.mult).then_inc(S["shift_ready"], 1)
                        if scan:
                            hold(dve, S["summed"], q + 1, S["passed"])
                            hold(dve, S["scanned"], q + 1 + DEPTH, S["passed"])
                            dve.wait_ge(S["c_done"], q + 1)
                            nc.vector.tensor_tensor(seen[n % DEPTH][:, :], state[u][n][:, :], c_ps[n % 2][:, :],
                                                    ALU.mult).then_inc(S["seen_ready"], 1)
                            if n + DEPTH - 1 < STATES:
                                cap(t, u, n + DEPTH - 1)
                        if n == 0 and back:
                            dve.wait_ge(S["summed"], STATES * t + DEPTH)
                            nc.vector.scalar_tensor_tensor(y[1 - u][:, :], u_act[1 - u][:, :], dpar[:, :], acc[:, :],
                                                           ALU.mult, ALU.add).then_inc(S["y_ready"], 1)
                        if n == 4 and front:
                            dve.wait_ge(S["high_ready"], f + 1)
                            nc.vector.tensor_tensor(remain[:, :], x_ps[0:3 * SLOT, :], parts[v][:, :],
                                                    ALU.subtract).then_inc(S["remain_ready"], 1)
                            dve.wait_ge(S["ex_ready"], f + 1)
                            nc.vector.tensor_scalar(rest[:, :], ex[:, :], 1.0, -1.0, ALU.add,
                                                    ALU.add).then_inc(S["back_ready"], 1)
                        if n == 5 and front:
                            hold(dve, S["mid_ready"], f + 1, S["passed"])
                            dve.wait_ge(S["middle_ready"], f + 1)
                            nc.vector.tensor_tensor(parts[v][lo, :], remain[lo, :], middle[lo, :],
                                                    ALU.subtract).then_inc(S["parts_ready"], 1)

                windows(dve, window)

            @block.gpsimd
            def _(pool):
                pool.memset(select[:, :, :], 0.0).then_inc(S["selector"], 1)
                for k in range(3):
                    pool.wait_ge(S["selector"], k + 1)
                    pool.affine_select(out=select[:, :, :], in_=select[:, :, :], compare_op=ALU.not_equal,
                                       fill=1.0, base=-k * SLOT, pattern=[[-1, 2 * STATES], [0, P]],
                                       channel_multiplier=1).then_inc(S["selector"], 1)
                pool.wait_ge(S["ready"], 4)
                pool.wait_ge(S["a_held"], 5)
                pool.sem_inc(S["yz_ready"], AHEAD)
                pool.sem_inc(S["fused_ready"], AHEAD)
                pool.sem_inc(S["summed"], DEPTH)

                def window(t, u, half_t, first, second, front, scan, back, late):
                    f, v, b = t + 1, 1 - u, t - 1

                    def add(n):
                        if not scan:
                            return
                        q = STATES * t + n
                        if n == 1:
                            hold(pool, S["y_ready"], t + AHEAD, S["passed"])
                            pool.wait_ge(S["seen_ready"], q + 1 + AHEAD)
                            nc.gpsimd.tensor_tensor(acc[:, :], seen[0][:, :], seen[1][:, :],
                                                    ALU.add).then_inc(S["summed"], 2)
                        else:
                            hold(pool, S["summed"], q + DEPTH, S["passed"])
                            pool.wait_ge(S["seen_ready"], q + 1 + AHEAD)
                            nc.gpsimd.tensor_tensor(acc[:, :], acc[:, :], seen[n % DEPTH][:, :],
                                                    ALU.add).then_inc(S["summed"], 1)

                    if back:
                        pool.wait_ge(S["y_ready"], b + 1 + AHEAD)
                        nc.gpsimd.tensor_tensor(yz[1 - u][:, :], y[1 - u][:, :], z_act[1 - u][:, :],
                                                ALU.mult).then_inc(S["yz_ready"], 1)
                    add(1)
                    add(2)
                    if back:
                        pool.wait_ge(S["vv_ready"], b + 1)
                        nc.gpsimd.tensor_tensor(scale[:, :], vv[:, :], half[:, :], ALU.pow
                                                ).then_inc(S["scale_ready"], 1)
                    add(3)
                    add(4)
                    if front:
                        pool.wait_ge(S["back_ready"], f + 1)
                        nc.gpsimd.tensor_tensor(rest[:, :], ex[:, :], rest[:, :],
                                                ALU.subtract).then_inc(S["rest_ready"], 1)
                        hold(pool, S["log_ready"], f + 1, S["passed"])
                        pool.wait_ge(S["rest_ready"], f + 1)
                        nc.gpsimd.tensor_tensor(rest[:, :], rest[:, :], logs[:, :], ALU.add).then_inc(S["sum1"], 1)
                        hold(pool, S["over_ready"], f + 1 + AHEAD, S["passed"])
                        pool.wait_ge(S["sum1"], f + 1)
                        nc.gpsimd.tensor_tensor(delta[v][:, :], rest[:, :], over[:, :],
                                                ALU.add).then_inc(S["delta_ready"], 1)
                        pool.wait_ge(S["delta_ready"], f + 1)
                        nc.gpsimd.tensor_tensor(du[v][:, :], delta[v][:, :], u_act[v][:, :],
                                                ALU.mult).then_inc(S["du_ready"], 1)
                    if back:
                        hold(pool, S["w2_ready"], b + 1 + AHEAD, S["passed"])
                        pool.wait_ge(S["affine_ready"], b + 1)
                        nc.gpsimd.tensor_tensor(fused[:, :], affine[:, :], w2_act[1 - u][:, :],
                                                ALU.mult).then_inc(S["fused_ready"], 1)
                    add(5)
                    add(6)
                    add(7)

                windows(pool, window)
        s.clear()


def phase_experts(nc, io, keep):
    E = 8
    EB = BANK // C
    x3_v = io["x3"].rearrange("(t b p) c -> t p b c", b=TB, p=P)
    out_v = io["out"].rearrange("a r w c -> (a r w) c").rearrange("(t b p) c -> t p b c", b=TB, p=P)
    with ExitStack() as ctx:
        s = Space(nc, ctx, "moe")

        def two(name, shape, dt=F32):
            return [s.sb(f"{name}{u}", shape, dt) for u in range(2)]

        rw, ew, eb = s.sb("rw", [P, E]), s.sb("ew", [P, E, C]), s.sb("eb", [E, C])
        rb, count, half = s.sb("rb", [P, TB, E]), s.sb("count", [P, TB, E]), s.sb("half", [P, TB])
        x3 = [s.sb(f"x3{m}", [P, TB, C]) for m in range(4)]
        out = two("out", [P, TB, C])
        even, odd = two("even", [P, TB, C]), two("odd", [P, TB, C])
        part = two("part", [P, EB, TB, C])
        stats, mv, vv = s.sb("stats", [P, TB, 6]), s.sb("mv", [P, TB, 2]), s.sb("vv", [P, TB])
        scale, shift = two("scale", [P, TB]), two("shift", [P, TB])
        h, hT, weight = s.sb("h", [P, TB, C]), two("hT", [P, TILE]), two("weight", [P, TB, E])
        logit, best, place = s.sb("logit", [P, TB, E]), s.sb("best", [P, TB, E]), s.sb("place", [P, TB, E], U32)
        placef, lead, ex, total, first, second = (s.sb("placef", [P, TB, 2]), *(s.sb(n, [P, TB]) for n in (
            "lead", "ex", "total", "first", "second")))
        hit0, hit1 = s.sb("hit0", [P, TB, E]), s.sb("hit1", [P, TB, E])
        wT = s.sb("wT", [E, TILE])
        e_ps = [s.bank(f"e{u}", 2) for u in range(2)]
        h_ps, l_ps, wT_ps, bias_ps = (s.bank(n) for n in ("h", "l", "wT", "bias"))

        S = {n: s.sem(n) for n in (
            "params ready passed step vv_ready scale_ready shift_ready h_ready h_turned hT_ready l_done logit_ready "
            "best_ready place_ready lead_ready ex_ready total_ready first_ready second_ready placed hits weight_ready "
            "w_turned wT_ready bias_done e_done mixed parted biased added out_ready").split()}
        x3_loaded = [s.sem(f"x3_loaded{m}") for m in range(4)]
        stored = [s.sem(f"stored{u}") for u in range(2)]
        PARAMS = 3 + TB
        STEPS = TB * EB

        def windows(eng, window):
            window(-2, 2, -1, True, False, False, False)
            window(-1, 3, -1, True, True, False, False)
            window(0, 0, 0, True, True, True, False)
            with eng.Fori(0, TILES // 4 - 1) as i:
                for k in range(1, 5):
                    window(4 * i + k, k % 4, i + k // 4, True, True, True, True)
            window(TILES - 3, 1, TILES // 4 - 1, True, True, True, True)
            window(TILES - 2, 2, TILES // 4 - 1, False, True, True, True)
            window(TILES - 1, 3, TILES // 4 - 1, False, False, True, True)
            window(TILES, 0, TILES // 4, False, False, False, True)

        with nc.Block() as block:
            @block.sync
            def _(sp):
                sp.dma_start(rw[:, :], io["L1_ffn_router_w"]).then_inc(S["params"], 16)
                sp.dma_start(ew[:, :, :], io["L1_ffn_expert_w"].rearrange("e d c -> d e c")).then_inc(S["params"], 16)
                sp.dma_start(eb[:, :], io["L1_ffn_expert_b"]).then_inc(S["params"], 16)
                for k in range(TB):
                    sp.dma_start(rb[:, k, :], io["L1_ffn_router_b"].partition_broadcast(P)).then_inc(S["params"], 16)

                def window(t, m, quarter, early, front, back, total_up):
                    u, half_t = m % 2, 2 * quarter + m // 2
                    if early:
                        if back:
                            sp.wait_ge(S["mixed"], STEPS * t + 2 * EB)
                        sp.dma_start(x3[(m + 2) % 4][:, :, :], x3_v[t + 2]).then_inc(x3_loaded[(m + 2) % 4], 16)
                    if total_up:
                        sp.wait_ge(S["out_ready"], t + AHEAD)
                        sp.dma_start(out_v[t - 1], out[1 - u][:, :, :]).then_inc(stored[1 - u], 16)

                windows(sp, window)
                for u in range(2):
                    sp.wait_ge(stored[u], 16 * (TILES // 2))

            @block.tensor
            def _(pe):
                ident = keep["ident"][:, :]
                pe.wait_ge(S["params"], 16 * PARAMS)

                def window(t, m, quarter, early, front, back, total_up):
                    u, half_t = m % 2, 2 * quarter + m // 2
                    f, v = t + 1, 1 - u

                    def experts(k):
                        pe.wait_ge(S["mixed"], STEPS * t + EB * k + EB)
                        pe.wait_ge(S["parted"], STEPS * t + EB * k + EB)
                        for j in range(E // EB):
                            last = nc.tensor.matmul(
                                e_ps[k % 2][:, j * BANK:(j + 1) * BANK], hT[u][:, k * P:(k + 1) * P],
                                ew[:, j * EB:(j + 1) * EB, :].rearrange("p e c -> p (e c)"), start=True, stop=True)
                        last.then_inc(S["e_done"], 1)

                    if back:
                        experts(0)
                        experts(1)
                        pe.wait_ge(S["weight_ready"], t + 1)
                        for k in range(TB):
                            last = nc.tensor.transpose(wT_ps[0:E, k * P:(k + 1) * P], weight[u][:, k, :], ident)
                        last.then_inc(S["w_turned"], 1)
                        experts(2)
                    if front:
                        pe.wait_ge(S["h_ready"], f + 1)
                        for k in range(TB):
                            last = nc.tensor.transpose(h_ps[:, k * P:(k + 1) * P], h[:, k, :], ident)
                        last.then_inc(S["h_turned"], 1)
                    if back:
                        experts(3)
                    if front:
                        pe.wait_ge(S["hT_ready"], f + 1)
                        for k in range(TB):
                            last = nc.tensor.matmul(l_ps[:, k * E:(k + 1) * E], hT[v][:, k * P:(k + 1) * P], rw[:, :],
                                                    start=True, stop=True)
                        last.then_inc(S["l_done"], 1)
                    if back:
                        pe.wait_ge(S["wT_ready"], t + 1)
                        if total_up:
                            pe.wait_ge(S["biased"], t)
                        for k in range(TB):
                            last = nc.tensor.matmul(bias_ps[:, k * C:(k + 1) * C], wT[:, k * P:(k + 1) * P], eb[:, :],
                                                    start=True, stop=True)
                        last.then_inc(S["bias_done"], 1)

                windows(pe, window)

            @block.scalar
            def _(act):
                act.preload_act_table_set("exp_and_others")
                act.sem_inc(S["parted"], 2 * EB)

                def window(t, m, quarter, early, front, back, total_up):
                    u, half_t = m % 2, 2 * quarter + m // 2
                    f, v = t + 1, 1 - u

                    def weigh(k):
                        act.wait_ge(S["e_done"], TB * t + k + 1)
                        for j in range(EB):
                            nc.scalar.activation(part[u][:, j, k, :], e_ps[k % 2][:, BANK + j * C:BANK + (j + 1) * C],
                                                 ACT.Copy, scale=weight[u][:, k, EB + j:EB + j + 1]
                                                 ).then_inc(S["parted"], 1)

                    if back:
                        act.wait_ge(S["out_ready"], t + 1)
                        act.wait_ge(S["weight_ready"], t + 1)
                        weigh(0)
                        weigh(1)
                    if back:
                        act.wait_ge(S["w_turned"], t + 1)
                        nc.scalar.activation(wT[:, :], wT_ps[0:E, :], ACT.Copy).then_inc(S["wT_ready"], 1)
                    if front:
                        act.wait_ge(S["h_turned"], f + 1)
                        nc.scalar.activation(hT[v][:, :], h_ps[:, :], ACT.Copy).then_inc(S["hT_ready"], 1)
                    if back:
                        weigh(2)
                        weigh(3)
                    if front:
                        act.wait_ge(S["lead_ready"], f + 1)
                        nc.scalar.activation(ex[:, :], lead[:, :], ACT.Exp).then_inc(S["ex_ready"], 1)

                windows(act, window)

            @block.vector
            def _(dve):
                for e in range(E):
                    nc.vector.memset(count[:, :, e:e + 1], float(e)).then_inc(S["ready"], 1)
                nc.vector.memset(half[:, :], -0.5).then_inc(S["ready"], 1)
                dve.wait_ge(S["ready"], E + 1)
                dve.wait_ge(S["params"], 16 * PARAMS)
                dve.sem_inc(S["mixed"], 2 * EB)

                def window(t, m, quarter, early, front, back, total_up):
                    u, half_t = m % 2, 2 * quarter + m // 2
                    f, v = t + 1, 1 - u

                    def mix(k):
                        hold(dve, S["e_done"], TB * t + k + 1, S["passed"])
                        for e in range(EB):
                            p = e_ps[k % 2][:, e * C:(e + 1) * C]
                            w = weight[u][:, k, e:e + 1]
                            if e >= 2:
                                dve.wait_ge(S["mixed"], STEPS * t + EB * k + e - 1 + 2 * EB)
                            if e == 1:
                                last = nc.vector.tensor_scalar(odd[u][:, k, :], p, w, None, ALU.mult)
                            else:
                                side = (even, odd)[e % 2][u][:, k, :]
                                last = nc.vector.scalar_tensor_tensor(side, p, w, x3[m][:, k, :] if e == 0 else side,
                                                                      ALU.mult, ALU.add)
                            last.then_inc(S["mixed"], 1)

                    if front:
                        dve.wait_ge(S["scale_ready"], f + 1)
                        nc.vector.scalar_tensor_tensor(shift[v][:, :], mv[:, :, 0], -1.0, scale[v][:, :], ALU.mult,
                                                       ALU.mult).then_inc(S["shift_ready"], 1)
                    if back:
                        hold(dve, S["out_ready"], t + 1, S["passed"])
                        mix(0)
                        mix(1)
                    if early:
                        a, x3_a = t + 2, x3[(m + 2) % 4]
                        dve.wait_ge(x3_loaded[(m + 2) % 4], 16 * (quarter + (m + 2) // 4) + 16)
                        for k in range(TB):
                            last = nc.vector.bn_stats(stats[:, k, :], x3_a[:, k, :])
                        last.then_inc(S["step"], 1)
                        hold(dve, S["step"], 2 * a + 1, S["passed"])
                        for k in range(TB):
                            last = nc.vector.bn_aggr(mv[:, k, :], stats[:, k, :])
                        last.then_inc(S["step"], 1)
                        dve.wait_ge(S["step"], 2 * a + 2)
                        nc.vector.tensor_scalar(vv[:, :], mv[:, :, 1], 1.0, 1e-5, ALU.mult,
                                                ALU.add).then_inc(S["vv_ready"], 1)
                    if back:
                        mix(2)
                        mix(3)
                    if front:
                        dve.wait_ge(S["l_done"], f + 1)
                        nc.vector.tensor_tensor(logit[:, :, :], l_ps[:, 0:TB * E].rearrange("p (b e) -> p b e", b=TB),
                                                rb[:, :, :], ALU.add).then_inc(S["logit_ready"], 1)
                        hold(dve, S["logit_ready"], f + 1, S["passed"])
                        for k in range(TB):
                            last = nc.vector.max(best[:, k, :], logit[:, k, :])
                        last.then_inc(S["best_ready"], 1)
                        dve.wait_ge(S["best_ready"], f + 1)
                        nc.vector.tensor_tensor(lead[:, :], best[:, :, 1], best[:, :, 0],
                                                ALU.subtract).then_inc(S["lead_ready"], 1)
                        for k in range(TB):
                            last = nc.vector.max_index(place[:, k, :], best[:, k, :], logit[:, k, :])
                        last.then_inc(S["place_ready"], 1)
                        dve.wait_ge(S["place_ready"], f + 1)
                        nc.vector.tensor_copy(placef[:, :, :], place[:, :, 0:2]).then_inc(S["placed"], 1)
                        dve.wait_ge(S["ex_ready"], f + 1)
                        nc.vector.tensor_scalar(total[:, :], ex[:, :], 1.0, None, ALU.add).then_inc(S["total_ready"], 1)
                        dve.wait_ge(S["total_ready"], f + 1)
                        nc.vector.reciprocal(first[:, :], total[:, :]).then_inc(S["first_ready"], 1)
                        dve.wait_ge(S["first_ready"], f + 1)
                        nc.vector.tensor_tensor(second[:, :], ex[:, :], first[:, :], ALU.mult
                                                ).then_inc(S["second_ready"], 1)
                        dve.wait_ge(S["placed"], f + 1)
                        for j, hit in enumerate((hit0, hit1)):
                            nc.vector.tensor_tensor(hit[:, :, :], count[:, :, :],
                                                    placef[:, :, j].unsqueeze(2).broadcast_to([P, TB, E]),
                                                    ALU.is_equal).then_inc(S["hits"], 1)
                        dve.wait_ge(S["second_ready"], f + 1)
                        for j, (hit, w) in enumerate(((hit0, first), (hit1, second))):
                            dve.wait_ge(S["hits"], 4 * f + 1 + j)
                            nc.vector.tensor_tensor(hit[:, :, :], hit[:, :, :],
                                                    w[:, :].unsqueeze(2).broadcast_to([P, TB, E]),
                                                    ALU.mult).then_inc(S["hits"], 1)
                        if back:
                            dve.wait_ge(S["parted"], STEPS * t + 2 * EB)
                        dve.wait_ge(S["hits"], 4 * f + 4)
                        nc.vector.tensor_tensor(weight[v][:, :, :], hit0[:, :, :], hit1[:, :, :],
                                                ALU.add).then_inc(S["weight_ready"], 1)
                        dve.wait_ge(S["weight_ready"], f + 1)
                    if back:
                        hold(dve, S["bias_done"], t + 1, S["passed"])
                        dve.wait_ge(S["mixed"], STEPS * (t + 1) + 2 * EB)
                        nc.vector.tensor_tensor(even[u][:, :, :], even[u][:, :, :],
                                                bias_ps[:, :].rearrange("p (b c) -> p b c", b=TB),
                                                ALU.add).then_inc(S["biased"], 1)

                windows(dve, window)

            @block.gpsimd
            def _(pool):
                pool.wait_ge(S["ready"], E + 1)
                pool.sem_inc(S["out_ready"], AHEAD)

                def window(t, m, quarter, early, front, back, total_up):
                    u, half_t = m % 2, 2 * quarter + m // 2
                    f, v = t + 1, 1 - u
                    if front:
                        hold(pool, S["shift_ready"], f + 1, S["passed"])
                        if back:
                            hold(pool, S["h_turned"], f, S["passed"])
                        for k in range(TB):
                            last = nc.gpsimd.tensor_scalar(h[:, k, :], x3[(m + 1) % 4][:, k, :], scale[v][:, k:k + 1],
                                                           shift[v][:, k:k + 1], ALU.mult, ALU.add)
                        last.then_inc(S["h_ready"], 1)
                    if total_up:
                        b, w = t - 1, 1 - u
                        pool.wait_ge(S["parted"], STEPS * t + 2 * EB)
                        nc.gpsimd.tensor_tensor(part[w][:, 0:2, :, :], part[w][:, 0:2, :, :], part[w][:, 2:4, :, :],
                                                ALU.add).then_inc(S["added"], 1)
                        pool.wait_ge(S["added"], 3 * b + 1)
                        nc.gpsimd.tensor_tensor(part[w][:, 0, :, :], part[w][:, 0, :, :], part[w][:, 1, :, :],
                                                ALU.add).then_inc(S["added"], 1)
                        hold(pool, S["added"], 3 * b + 2, S["passed"])
                        pool.wait_ge(S["biased"], b + 1)
                        nc.gpsimd.tensor_tensor(even[w][:, :, :], even[w][:, :, :], odd[w][:, :, :],
                                                ALU.add).then_inc(S["added"], 1)
                        hold(pool, stored[w], 16 * (half_t if u == 1 else half_t - 1), S["passed"])
                        pool.wait_ge(S["added"], 3 * b + 3)
                        nc.gpsimd.tensor_tensor(out[w][:, :, :], even[w][:, :, :], part[w][:, 0, :, :],
                                                ALU.add).then_inc(S["out_ready"], 1)
                    if early:
                        pool.wait_ge(S["vv_ready"], t + 2 + 1)
                        nc.gpsimd.tensor_tensor(scale[u][:, :], vv[:, :], half[:, :], ALU.pow
                                                ).then_inc(S["scale_ready"], 1)

                windows(pool, window)
        s.clear()


def metaformer(nc, io):
    io["x1"] = nc.dram_tensor("x1_map", (TOKENS, C), F32).ap()
    io["wx"] = nc.dram_tensor("wx_map", (C, TOKENS), F32).ap()
    io["yT"] = nc.dram_tensor("y_map", (C, TOKENS), F32).ap()
    io["x2"] = nc.dram_tensor("x2_map", (TOKENS, C), F32).ap()
    io["hT"] = nc.dram_tensor("h_map", (C, SIDE + 2, SIDE), F32).ap()
    io["x3"] = nc.dram_tensor("x3_map", (TOKENS, C), F32).ap()
    with ExitStack() as ctx:
        s = Space(nc, ctx, "keep")
        keep = {"ident": s.sb("ident", [P, P]), "bn_scale": s.sb("bn_scale", [P, 1]),
                "bn_shift": s.sb("bn_shift", [P, 1])}
        with ExitStack() as attention:
            a = Space(nc, attention, "keep")
            keep["bias"] = a.sb("bias", [P, HEADS, RB, SIDE])
            keep["scale"] = a.sb("scale", [P, TOKENS // P])
            keep["shift"] = a.sb("shift", [P, TOKENS // P])
            phase_bias(nc, io, keep)
            phase_attention(nc, io, keep)
        phase_batchnorm(nc, io, keep)
        phase_recurrence(nc, io, keep)
        phase_join(nc, io, keep)
        phase_mamba(nc, io, keep)
        phase_experts(nc, io, keep)


def kernel(**inputs):
    import numpy as _np
    import concourse.bacc as _bacc
    from concourse import mybir as _mybir
    from concourse.bass_utils import run_bass_kernel_spmd as _run

    nc = _bacc.Bacc("TRN2", target_bir_lowering=False, num_devices=1)
    arrays, io = {}, {}
    for name, value in inputs.items():
        a = _np.ascontiguousarray(value)
        arrays[f"in_{name}_dram"] = a
        io[name] = nc.dram_tensor(f"in_{name}_dram", a.shape, _mybir.dt.from_np(a.dtype), kind="ExternalInput").ap()
    io["out"] = nc.dram_tensor("out_dram", (1, SIDE, SIDE, C), _mybir.dt.float32, kind="ExternalOutput").ap()
    metaformer(nc, io)
    r = _run(nc, [arrays], core_ids=[0])
    return r.results[0]["out_dram"]
```
